# Optimizing a Trainium2 kernel written in Bass

```python
import numpy as np
import jax
import jax.numpy as jnp

def _softmax(x, axis=-1):
    return jax.nn.softmax(x, axis=axis)

def _gelu(x):
    return jax.nn.gelu(x, approximate=True)

def _silu(x):
    return jax.nn.silu(x)

def _sigmoid(x):
    return jax.nn.sigmoid(x)

def _layernorm(x, axis=-1, eps=1e-05):
    m = jnp.mean(x, axis=axis, keepdims=True)
    v = jnp.var(x, axis=axis, keepdims=True)
    return (x - m) / jnp.sqrt(v + eps)

def _scatter_add(tgt, idx, src, axis=0):
    return tgt.at[idx].add(src)

def _segment_sum(src, seg, n):
    return jax.ops.segment_sum(src, seg, n)
kernel_name = 'mk_gps_d1_gnn_r8_913955'

def setup_inputs(seed: int=0):
    np.random.seed(seed)
    _w = jnp.asarray

    def _rec_inputs():
        import jax
        import jax.numpy as jnp
        _gk = jax.random.key(seed)
        x = -0.0003713 + 1 * jax.random.normal(jax.random.fold_in(_gk, 1), (6250, 256), jnp.float32)
        src = jax.random.randint(jax.random.fold_in(_gk, 2), (100000,), 0, 6250, jnp.int32)
        dst = jax.random.randint(jax.random.fold_in(_gk, 3), (100000,), 0, 6250, jnp.int32)
        _o = jnp.argsort(dst, stable=True)
        src = src[_o]
        dst = dst[_o]
        return (x, src, dst)
    x, src, dst = _rec_inputs()

    def _L0_gnn_setup():
        import jax, jax.numpy as jnp
        import numpy as np
        N = 6250
        E = 100000
        DIN = 256
        DOUT = 64
        H = 4
        NEG_SLOPE = 0.01
        key = jax.random.key(seed)
        k0, k1, k2, k3, k4 = jax.random.split(key, 5)
        h = jax.random.normal(k0, (N, DIN), dtype=jnp.float32)
        src = jax.random.randint(k1, (E,), 0, N)
        dst = jax.random.randint(k2, (E,), 0, N)
        W = jax.random.normal(k3, (H, DOUT, DIN), dtype=jnp.float32) * np.float32(np.sqrt(2.0) * np.sqrt(2.0 / (DIN + DOUT)))
        att = jax.random.normal(k4, (H, 2 * DOUT), dtype=jnp.float32) * np.float32(np.sqrt(2.0) * np.sqrt(2.0 / (2 * DOUT + 1)))
        return {'h': h, 'src': src, 'dst': dst, 'W': W, 'att': att}
    _L0_gnn_all = _L0_gnn_setup()
    _L0_gnn_in = {k: v for k, v in _L0_gnn_all.items() if k in ('W', 'att')}
    del _L0_gnn_all

    def _L0_mix_setup():
        import jax, jax.numpy as jnp
        import numpy as np
        HEADS = 8
        DIM_HEAD = 32
        SCALE = DIM_HEAD ** (-0.5)
        EPS = 1e-05

        def _layernorm_gamma(x, gamma):
            mu = jnp.mean(x, axis=-1, keepdims=True)
            var = jnp.var(x, axis=-1, keepdims=True)
            return (x - mu) * jax.lax.rsqrt(var + EPS) * gamma
        key = jax.random.key(seed)
        k1, k2, k3 = jax.random.split(key, 3)
        B, N, D = (8, 2048, 256)
        hidden = HEADS * DIM_HEAD
        x = jax.random.normal(k1, (B, N, D), dtype=jnp.float32)
        Wqkv = jax.random.normal(k2, (D, 3 * hidden), dtype=jnp.float32) * D ** (-0.5)
        Wout = jax.random.normal(k3, (hidden, D), dtype=jnp.float32) * hidden ** (-0.5)
        gamma = jnp.ones((D,), dtype=jnp.float32)
        return {'x': x, 'Wqkv': Wqkv, 'Wout': Wout, 'gamma': gamma}
    _L0_mix_all = _L0_mix_setup()
    _L0_mix_in = {k: v for k, v in _L0_mix_all.items() if k in ('Wqkv', 'Wout', 'gamma')}
    del _L0_mix_all

    def _L0_ffn_setup():
        import jax, jax.numpy as jnp
        import numpy as np
        B, N, D = (16, 512, 256)
        NUM_EXPERTS, TOP_K, HEADS = (4, 2, 4)
        N_EDGES = 131072
        LN_EPS = 1e-05

        def _layernorm(x, g, b):
            mu = x.mean(-1, keepdims=True)
            var = ((x - mu) ** 2).mean(-1, keepdims=True)
            return (x - mu) * jax.lax.rsqrt(var + LN_EPS) * g + b

        def _forward(x, edge_index, W_gat, att_src, att_dst, b_gat, ln_gamma, ln_beta, W1, b1, W2, b2):
            Bc, Nc, Dc = x.shape
            M = Bc * Nc
            x_flat = x.reshape(M, Dc)
            h = (x_flat @ W_gat).reshape(M, HEADS, NUM_EXPERTS)
            loops = jnp.arange(M, dtype=edge_index.dtype)
            src = jnp.concatenate([edge_index[0], loops])
            dst = jnp.concatenate([edge_index[1], loops])
            a_src = (h * att_src).sum(-1)
            a_dst = (h * att_dst).sum(-1)
            e = jax.nn.leaky_relu(a_src[src] + a_dst[dst], negative_slope=0.2)
            e_max = jax.ops.segment_max(e, dst, num_segments=M)
            ee = jnp.exp(e - e_max[dst])
            denom = jax.ops.segment_sum(ee, dst, num_segments=M)
            alpha = ee / (denom[dst] + 1e-16)
            msg = h[src] * alpha[:, :, None]
            agg = jax.ops.segment_sum(msg, dst, num_segments=M).reshape(M, HEADS * NUM_EXPERTS) + b_gat
            scores = _layernorm(agg, ln_gamma, ln_beta).reshape(M, HEADS, NUM_EXPERTS).mean(1)
            scores = scores.reshape(Bc, Nc, NUM_EXPERTS)
            topk_s, topk_i = jax.lax.top_k(scores, TOP_K)
            w = jax.nn.softmax(topk_s, axis=-1)
            out = jnp.zeros_like(x)
            for ei in range(NUM_EXPERTS):
                g = jnp.where(topk_i == ei, w, 0.0).sum(-1)
                hh = jax.nn.gelu(x @ W1[ei] + b1[ei], approximate=False)
                out = out + g[..., None] * (hh @ W2[ei] + b2[ei])
            return out
        key = jax.random.key(seed)
        ks = jax.random.split(key, 8)
        s = 0.05
        return {'x': jax.random.normal(ks[0], (B, N, D), jnp.float32), 'W_gat': jax.random.normal(ks[1], (D, HEADS * NUM_EXPERTS), jnp.float32) * s, 'att_src': jax.random.normal(ks[2], (HEADS, NUM_EXPERTS), jnp.float32) * s, 'att_dst': jax.random.normal(ks[3], (HEADS, NUM_EXPERTS), jnp.float32) * s, 'b_gat': jnp.zeros((HEADS * NUM_EXPERTS,), jnp.float32), 'ln_gamma': jnp.ones((HEADS * NUM_EXPERTS,), jnp.float32), 'ln_beta': jnp.zeros((HEADS * NUM_EXPERTS,), jnp.float32), 'W1': jax.random.normal(ks[4], (NUM_EXPERTS, D, 2 * D), jnp.float32) * s, 'b1': jnp.zeros((NUM_EXPERTS, 2 * D), jnp.float32), 'W2': jax.random.normal(ks[5], (NUM_EXPERTS, 2 * D, D), jnp.float32) * s, 'b2': jnp.zeros((NUM_EXPERTS, D), jnp.float32), 'edge_index': jax.random.randint(ks[6], (2, N_EDGES), 0, B * N, jnp.int32)}
    _L0_ffn_all = _L0_ffn_setup()
    _L0_ffn_in = {k: v for k, v in _L0_ffn_all.items() if k in ('W_gat', 'att_src', 'att_dst', 'b_gat', 'ln_gamma', 'ln_beta', 'W1', 'b1', 'W2', 'b2', 'edge_index')}
    del _L0_ffn_all
    return {'x': x, 'src': src, 'dst': dst, 'L0_gnn_W': _L0_gnn_in['W'], 'L0_gnn_att': _L0_gnn_in['att'], 'L0_mix_Wqkv': _L0_mix_in['Wqkv'], 'L0_mix_Wout': _L0_mix_in['Wout'], 'L0_mix_gamma': _L0_mix_in['gamma'], 'L0_ffn_W_gat': _L0_ffn_in['W_gat'], 'L0_ffn_att_src': _L0_ffn_in['att_src'], 'L0_ffn_att_dst': _L0_ffn_in['att_dst'], 'L0_ffn_b_gat': _L0_ffn_in['b_gat'], 'L0_ffn_ln_gamma': _L0_ffn_in['ln_gamma'], 'L0_ffn_ln_beta': _L0_ffn_in['ln_beta'], 'L0_ffn_W1': _L0_ffn_in['W1'], 'L0_ffn_b1': _L0_ffn_in['b1'], 'L0_ffn_W2': _L0_ffn_in['W2'], 'L0_ffn_b2': _L0_ffn_in['b2'], 'L0_ffn_edge_index': _L0_ffn_in['edge_index']}

def reference(x, src, dst, L0_gnn_W, L0_gnn_att, L0_mix_Wqkv, L0_mix_Wout, L0_mix_gamma, L0_ffn_W_gat, L0_ffn_att_src, L0_ffn_att_dst, L0_ffn_b_gat, L0_ffn_ln_gamma, L0_ffn_ln_beta, L0_ffn_W1, L0_ffn_b1, L0_ffn_W2, L0_ffn_b2, L0_ffn_edge_index):
    import jax
    import jax.numpy as jnp

    def _L0_gnn_ref(h, src, dst, W, att):
        import jax, jax.numpy as jnp
        import numpy as np
        N = 6250
        E = 100000
        DIN = 256
        DOUT = 64
        H = 4
        NEG_SLOPE = 0.01
        z = jnp.einsum('ni,hoi->hno', h, W)
        a_src, a_dst = (att[:, :DOUT], att[:, DOUT:])
        e_src = jnp.einsum('hno,ho->hn', z, a_src)
        e_dst = jnp.einsum('hno,ho->hn', z, a_dst)
        e = e_src[:, src] + e_dst[:, dst]
        e = jnp.where(e > 0, e, NEG_SLOPE * e)

        def per_head(e_h, z_h):
            m = jax.ops.segment_max(e_h, dst, num_segments=N)
            m = jnp.where(jnp.isfinite(m), m, 0.0)
            ex = jnp.exp(e_h - m[dst])
            den = jax.ops.segment_sum(ex, dst, num_segments=N)
            alpha = ex / jnp.maximum(den[dst], jnp.float32(1e-16))
            return jax.ops.segment_sum(alpha[:, None] * z_h[src], dst, num_segments=N)
        out = jax.vmap(per_head)(e, z)
        return jnp.transpose(out, (1, 0, 2)).reshape(N, H * DOUT)

    def _L0_mix_ref(x, Wqkv, Wout, gamma):
        import jax, jax.numpy as jnp
        import numpy as np
        HEADS = 8
        DIM_HEAD = 32
        SCALE = DIM_HEAD ** (-0.5)
        EPS = 1e-05

        def _layernorm_gamma(x, gamma):
            mu = jnp.mean(x, axis=-1, keepdims=True)
            var = jnp.var(x, axis=-1, keepdims=True)
            return (x - mu) * jax.lax.rsqrt(var + EPS) * gamma
        B, N, D = x.shape
        qkv = x @ Wqkv
        q, k, v = jnp.split(qkv, 3, axis=-1)

        def to_heads(t):
            return t.reshape(B, N, HEADS, DIM_HEAD).transpose(0, 2, 1, 3)
        q, k, v = map(to_heads, (q, k, v))
        q = jax.nn.softmax(q, axis=-1) * SCALE
        k = jax.nn.softmax(k, axis=2)
        context = jnp.einsum('bhnd,bhne->bhde', k, v)
        out = jnp.einsum('bhde,bhnd->bhne', context, q)
        out = out.transpose(0, 2, 1, 3).reshape(B, N, HEADS * DIM_HEAD)
        out = out @ Wout
        return _layernorm_gamma(out, gamma)

    def _L0_ffn_ref(x, W_gat, att_src, att_dst, b_gat, ln_gamma, ln_beta, W1, b1, W2, b2, edge_index):
        import jax, jax.numpy as jnp
        import numpy as np
        B, N, D = (16, 512, 256)
        NUM_EXPERTS, TOP_K, HEADS = (4, 2, 4)
        N_EDGES = 131072
        LN_EPS = 1e-05

        def _layernorm(x, g, b):
            mu = x.mean(-1, keepdims=True)
            var = ((x - mu) ** 2).mean(-1, keepdims=True)
            return (x - mu) * jax.lax.rsqrt(var + LN_EPS) * g + b

        def _forward(x, edge_index, W_gat, att_src, att_dst, b_gat, ln_gamma, ln_beta, W1, b1, W2, b2):
            Bc, Nc, Dc = x.shape
            M = Bc * Nc
            x_flat = x.reshape(M, Dc)
            h = (x_flat @ W_gat).reshape(M, HEADS, NUM_EXPERTS)
            loops = jnp.arange(M, dtype=edge_index.dtype)
            src = jnp.concatenate([edge_index[0], loops])
            dst = jnp.concatenate([edge_index[1], loops])
            a_src = (h * att_src).sum(-1)
            a_dst = (h * att_dst).sum(-1)
            e = jax.nn.leaky_relu(a_src[src] + a_dst[dst], negative_slope=0.2)
            e_max = jax.ops.segment_max(e, dst, num_segments=M)
            ee = jnp.exp(e - e_max[dst])
            denom = jax.ops.segment_sum(ee, dst, num_segments=M)
            alpha = ee / (denom[dst] + 1e-16)
            msg = h[src] * alpha[:, :, None]
            agg = jax.ops.segment_sum(msg, dst, num_segments=M).reshape(M, HEADS * NUM_EXPERTS) + b_gat
            scores = _layernorm(agg, ln_gamma, ln_beta).reshape(M, HEADS, NUM_EXPERTS).mean(1)
            scores = scores.reshape(Bc, Nc, NUM_EXPERTS)
            topk_s, topk_i = jax.lax.top_k(scores, TOP_K)
            w = jax.nn.softmax(topk_s, axis=-1)
            out = jnp.zeros_like(x)
            for ei in range(NUM_EXPERTS):
                g = jnp.where(topk_i == ei, w, 0.0).sum(-1)
                hh = jax.nn.gelu(x @ W1[ei] + b1[ei], approximate=False)
                out = out + g[..., None] * (hh @ W2[ei] + b2[ei])
            return out
        return _forward(x, edge_index, W_gat, att_src, att_dst, b_gat, ln_gamma, ln_beta, W1, b1, W2, b2)
    xn = _layernorm(x, axis=-1)
    x = x + _L0_gnn_ref(xn, src, dst, L0_gnn_W, L0_gnn_att) + _L0_mix_ref(xn[None], L0_mix_Wqkv, L0_mix_Wout, L0_mix_gamma)[0]
    x = x + _L0_ffn_ref(_layernorm(x, axis=-1)[None], L0_ffn_W_gat, L0_ffn_att_src, L0_ffn_att_dst, L0_ffn_b_gat, L0_ffn_ln_gamma, L0_ffn_ln_beta, L0_ffn_W1, L0_ffn_b1, L0_ffn_W2, L0_ffn_b2, L0_ffn_edge_index)[0]
    return x

_drawn_inputs = setup_inputs


def setup_inputs(seed=0):
    import zlib

    import numpy as np

    out = dict(_drawn_inputs(seed))
    spreads = {'L0_mix_gamma': (1.0, 0.2),
     'L0_ffn_b_gat': (0.0, 0.1),
     'L0_ffn_ln_gamma': (1.0, 0.2),
     'L0_ffn_ln_beta': (0.0, 0.1),
     'L0_ffn_b1': (0.0, 0.1),
     'L0_ffn_b2': (0.0, 0.1)}
    factors = {}
    for name, (base, spread) in spreads.items():
        noise = np.random.default_rng([zlib.crc32(name.encode()), seed]).standard_normal(out[name].shape)
        drawn = base * np.exp(spread * noise) if base else spread * noise
        out[name] = jnp.asarray(drawn.astype(out[name].dtype))
    for name, factor in factors.items():
        out[name] = (out[name] * factor).astype(out[name].dtype)
    return out
```

```python
from contextlib import ExitStack

import concourse.bass as bass
from concourse import mybir

P = 128
N = 6250
NT = (N + P - 1) // P
NPAD = NT * P
LAST = N - (NT - 1) * P
D = 256
H = 4
EPS = 1e-5
NEG = -1.0e30
NOWHERE = 1 << 20
HIS = 64

MIX_HEADS, MIX_DIM = 8, 32
EXPERTS, HIDDEN = 4, 512
FFN_BLOCK = 7
F32 = mybir.dt.float32
BF16 = mybir.dt.bfloat16
FP16 = mybir.dt.float16
I32 = mybir.dt.int32
ALU = mybir.AluOpType
ACT = mybir.ActivationFunctionType
AX = mybir.AxisListType.X


class Graph:

    def __init__(self, name, edges, width, chunk, cols, slope):
        self.name, self.edges, self.width, self.chunk, self.cols, self.slope = name, edges, width, chunk, cols, slope
        self.per_head = cols // H
        self.chunks = width // chunk
        self.row = cols + H
        self.state = cols + 2 * H
        assert width % chunk == 0 and self.chunks % 2 == 0 and P * width >= edges


GNN = Graph("gnn", 100000, 782, 17, 256, 0.01)
FFN = Graph("ffn", 131072, 1024, 16, 16, 0.2)
SORT_BLOCKS = P
SORT_TILES = FFN.width // P


def first(i):
    return isinstance(i, int) and i == 0


def in_pairs(eng, count, step):
    for s in range(2):
        step(s, 0, s)
    with eng.Fori(1, count // 2) as i:
        for s in range(2):
            step(i * 2 + s, i, s)
    if count % 2:
        step(count - 1, count // 2, 0)


def tile_rows(t):
    return LAST if isinstance(t, int) and t == NT - 1 else P


def heads(ap, per_head):
    return ap.unsqueeze(2).to_broadcast([P, H, per_head])


class Kernel:
    def __init__(self, nc, io):
        self.nc, self.io = nc, io
        self.keep = ExitStack()
        self.scratch, self.sems = {}, {}
        self.part = "all"

    def sb(self, stack, name, shape, dt=F32):
        return stack.enter_context(self.nc.sbuf_tensor(f"{self.part}_{name}", list(shape), dt))

    def several(self, stack, name, *shapes):
        sizes = [1] * len(shapes)
        for n, shape in enumerate(shapes):
            for d in shape[1:]:
                sizes[n] *= d
        whole, at, views = self.sb(stack, name, [P, sum(sizes)]), 0, []
        for shape, size in zip(shapes, sizes):
            view = whole[0:shape[0], at:at + size]
            if len(shape) == 3:
                view = view.rearrange("p (a b) -> p a b", b=shape[2])
            elif len(shape) == 4:
                view = view.rearrange("p (a b c) -> p a b c", b=shape[2], c=shape[3])
            views.append(view)
            at += size
        return views

    def ps(self, stack, name, shape, dt=F32):
        return stack.enter_context(self.nc.psum_tensor(f"{self.part}_{name}", list(shape), dt))

    def sem(self, stack, name):
        sem = self.nc.alloc_semaphore(f"{self.part}_{name}")
        if stack not in self.sems:
            self.sems[stack] = []
            stack.callback(self.clear_sems, stack)
        self.sems[stack].append(sem)
        return sem

    def clear_sems(self, stack):
        self.nc.clear_and_free_semaphores(self.sems.pop(stack))
        self.nc.all_engine_barrier()

    def dram(self, name, shape, dt=F32):
        t = self.nc.dram_tensor(name, list(shape), dt, kind="Internal").ap()
        self.scratch[name] = t
        return t

    def setup(self):
        nc, io, keep = self.nc, self.io, self.keep
        self.X = self.sb(keep, "X", [P, NT, D])
        self.ident = self.sb(keep, "ident", [P, P])
        self.ones = self.sb(keep, "ones", [P, P])
        self.below = self.sb(keep, "below", [P, P])
        self.ed = {g.name: self.sb(keep, f"ed_{g.name}", [P, NT, H]) for g in (GNN, FFN)}
        self.seg_at = {g.name: self.sb(keep, f"seg_at_{g.name}", [P, NT + 1], I32) for g in (GNN, FFN)}
        self.end_at = {g.name: self.sb(keep, f"end_at_{g.name}", [P, NT + 1], I32) for g in (GNN, FFN)}
        self.carry_at = {g.name: self.sb(keep, f"carry_at_{g.name}", [P, NT + 1], I32) for g in (GNN, FFN)}
        self.base_ffn = self.sb(keep, "base_ffn", [P, HIS])
        self.edge_src = {g.name: self.sb(keep, f"src_{g.name}", [P, g.width + 2 * g.chunk], I32)
                         for g in (GNN, FFN)}
        self.row_dram = {"gnn": self.dram("gnn_rows", [NPAD, GNN.row]), "ffn": self.dram("ffn_rows", [NPAD, FFN.row])}
        self.qkv_dram = self.dram("qkv", [NPAD, 3 * D])
        self.seg_dram = {g.name: self.dram(f"seg_{g.name}", [P * g.width, 1 + H]) for g in (GNN, FFN)}
        self.state_dram = {g.name: self.dram(f"state_{g.name}", [P * g.width, g.state]) for g in (GNN, FFN)}
        self.carry_dram = {g.name: self.dram(f"carry_{g.name}", [P, g.state]) for g in (GNN, FFN)}
        self.lo_dram = self.dram("dst_lo", [P, FFN.width], I32)
        X, ident, ones, below = self.X, self.ident, self.ones, self.below

        with ExitStack() as here:
            cleared, loaded = self.sem(here, "cleared"), self.sem(here, "x_loaded")
            block = here.enter_context(nc.Block())

            @block.gpsimd
            def _(pool):
                pool.memset(X[:, NT - 1, :], 0.0).then_inc(cleared, 1)
                pool.memset(ident[:, :], 0.0)
                pool.memset(ones[:, :], 1.0)
                pool.drain()
                pool.affine_select(out=ident[:, :], in_=ident[:, :], compare_op=ALU.not_equal, fill=1.0,
                                   base=0, pattern=[[-1, P]], channel_multiplier=1)
                pool.affine_select(out=below[:, :], in_=ones[:, :], compare_op=ALU.is_gt, fill=0.0,
                                   base=0, pattern=[[1, P]], channel_multiplier=-1)

            @block.vector
            def _(dve):
                for g in (GNN, FFN):
                    dve.memset(self.edge_src[g.name][:, :], 0)
                    dve.memset(self.end_at[g.name][:, NT:NT + 1], NOWHERE)
                    dve.memset(self.carry_at[g.name][:, NT:NT + 1], NOWHERE)

            @block.sync
            def _(sp):
                sp.dma_start(X[:, 0:NT - 1, :], io["x"][0:(NT - 1) * P, :].rearrange("(t p) d -> p t d", p=P)) \
                  .then_inc(loaded, 16)
                sp.wait_ge(cleared, 1)
                sp.dma_start(X[0:LAST, NT - 1, :], io["x"][(NT - 1) * P:N, :]).then_inc(loaded, 16)
                sp.wait_ge(loaded, 32)

    def segments(self, g, dst):
        nc = self.nc
        U = 17 if g is GNN else 16
        W = g.width
        with ExitStack() as here:
            dst_i = self.sb(here, "dst_i", [P, W], I32)
            part_i = self.sb(here, "part_i", [P, W], I32)
            lo, hi = self.sb(here, "lo", [P, W]), self.sb(here, "hi", [P, W])
            iota_i = self.sb(here, "iota_i", [P, P], I32)
            iota = self.sb(here, "iota", [P, P], BF16)
            oh_lo, oh_hi = self.sb(here, "oh_lo", [P, U, P], BF16), self.sb(here, "oh_hi", [P, U, HIS], BF16)
            (cnt, tot, run, base, nz, end, t1, t2, q1, q2) = self.several(
                here, "nodes_small",
                [P, HIS],
                [P, HIS],
                [P, HIS],
                [P, NT],
                [P, NT],
                [P, NT],
                [P, NT],
                [P, NT],
                [P, NT],
                [P, NT])
            qi = self.sb(here, "qi", [P, NT], I32)
            hist = self.ps(here, "hist", [P, HIS])
            pre, total = self.ps(here, "pre", [P, HIS]), self.ps(here, "total", [P, HIS])
            padded, loaded, iota_made = self.sem(here, "padded"), self.sem(here, "dst_loaded"), self.sem(here, "iota_made")
            hot, counted = self.sem(here, "hot"), self.sem(here, "counted")
            cnt_ready, prefixed = self.sem(here, "cnt_ready"), self.sem(here, "prefixed")
            lo_ready, lo_stored = self.sem(here, "lo_ready"), self.sem(here, "lo_stored")
            block = here.enter_context(nc.Block())

            @block.sync
            def _(sp):
                full = g.edges // W
                if g.edges == P * W:
                    sp.dma_start(dst_i[:, :], dst.rearrange("(p w) -> p w", w=W)).then_inc(loaded, 16)
                    sp.wait_ge(loaded, 16)
                else:
                    sp.dma_start(self.edge_src[g.name][0:full, 0:W],
                                 self.io["src"][0:full * W].rearrange("(p w) -> p w", w=W)).then_inc(loaded, 16)
                    sp.dma_start(self.edge_src[g.name][full:full + 1, 0:g.edges - full * W],
                                 self.io["src"][full * W:g.edges].rearrange("(p w) -> p w", p=1)).then_inc(loaded, 16)
                    sp.wait_ge(padded, 1)
                    sp.dma_start(dst_i[0:full, :], dst[0:full * W].rearrange("(p w) -> p w", w=W)).then_inc(loaded, 16)
                    sp.dma_start(dst_i[full:full + 1, 0:g.edges - full * W],
                                 dst[full * W:g.edges].rearrange("(p w) -> p w", p=1)).then_inc(loaded, 16)
                    sp.wait_ge(loaded, 64)
                if g is FFN:
                    sp.wait_ge(lo_ready, 1)
                    sp.dma_start(self.lo_dram[:, :], part_i[:, :]).then_inc(lo_stored, 16)
                    sp.wait_ge(lo_stored, 16)

            @block.gpsimd
            def _(pool):
                pool.iota(iota_i[:, :], pattern=[[1, P]], base=0, channel_multiplier=0)
                pool.drain()
                pool.tensor_copy(iota[:, :], iota_i[:, :]).then_inc(iota_made, 1)

            @block.tensor
            def _(pe):
                def step(i, u, start, stop):
                    pe.wait_ge(hot, i * U + (u + 1))
                    pe.matmul(hist[:, :], oh_lo[:, u, :], oh_hi[:, u, :], start=start, stop=stop,
                              skip_group_check=True).then_inc(counted, 1)
                for u in range(U):
                    step(0, u, u == 0, False)
                with pe.Fori(1, W // U) as i:
                    for u in range(U):
                        step(i, u, False, False)
                pe.wait_ge(cnt_ready, 1)
                pe.matmul(pre[:, :], self.below[:, :], cnt[:, :], start=True, stop=True)
                pe.matmul(total[:, :], self.ones[:, :], cnt[:, :], start=True, stop=True).then_inc(prefixed, 1)

            @block.vector
            def _(dve):
                if g.edges != P * W:
                    dve.memset(dst_i[:, :], HIS * P - 1).then_inc(padded, 1)
                dve.wait_ge(loaded, 16 if g.edges == P * W else 64)
                dve.tensor_scalar(part_i[:, :], dst_i[:, :], 7, None, ALU.logical_shift_right)
                dve.drain()
                dve.tensor_copy(hi[:, :], part_i[:, :])
                dve.drain()
                dve.tensor_scalar(part_i[:, :], dst_i[:, :], P - 1, None, ALU.bitwise_and).then_inc(lo_ready, 1)
                dve.drain()
                dve.tensor_copy(lo[:, :], part_i[:, :])
                dve.drain()
                dve.wait_ge(iota_made, 1)

                def step(i, u):
                    if not first(i):
                        dve.wait_ge(counted, i * U + (u + 1 - U))
                    dve.tensor_scalar(oh_lo[:, u, :], iota[:, :], lo[:, bass.ds(i * U + u, 1)], None, ALU.is_equal)
                    dve.tensor_scalar(oh_hi[:, u, :], iota[:, 0:HIS], hi[:, bass.ds(i * U + u, 1)], None,
                                      ALU.is_equal).then_inc(hot, 1)
                for u in range(U):
                    step(0, u)
                with dve.Fori(1, W // U) as i:
                    for u in range(U):
                        step(i, u)
                dve.wait_ge(counted, W)
                dve.tensor_copy(cnt[:, :], hist[:, :]).then_inc(cnt_ready, 1)
                dve.wait_ge(prefixed, 1)
                dve.tensor_copy(tot[:, :], total[:, :])
                dve.drain()
                dve.tensor_tensor_scan(run[:, :], self.ones[:, 0:HIS], tot[:, :], 0.0, ALU.mult, ALU.add)
                dve.drain()
                dve.tensor_tensor(run[:, :], run[:, :], tot[:, :], ALU.subtract)
                dve.drain()
                dve.tensor_tensor(run[:, :], run[:, :], pre[:, :], ALU.add)
                dve.drain()
                if g is FFN:
                    dve.tensor_copy(self.base_ffn[:, :], run[:, :])
                dve.tensor_copy(base[:, :], run[:, 0:NT])
                dve.tensor_scalar(nz[:, :], cnt[:, 0:NT], 1.0, None, ALU.min)
                dve.tensor_tensor(end[:, :], run[:, 0:NT], cnt[:, 0:NT], ALU.add)
                dve.drain()
                dve.tensor_scalar(end[:, :], end[:, :], -1.0, 0.0, ALU.add, ALU.max)
                dve.drain()

                def row_of(q, x):
                    dve.tensor_scalar(t1[:, :], x[:, :], 1.0 / W, None, ALU.mult)
                    dve.drain()
                    dve.tensor_copy(qi[:, :], t1[:, :])
                    dve.drain()
                    dve.tensor_copy(q[:, :], qi[:, :])
                    dve.drain()
                    dve.scalar_tensor_tensor(t1[:, :], q[:, :], -float(W), x[:, :], ALU.mult, ALU.add)
                    dve.drain()
                    dve.tensor_scalar(t2[:, :], t1[:, :], 0.0, None, ALU.is_lt)
                    dve.tensor_scalar(t1[:, :], t1[:, :], float(W), None, ALU.is_ge)
                    dve.drain()
                    dve.tensor_tensor(t1[:, :], t1[:, :], t2[:, :], ALU.subtract)
                    dve.drain()
                    dve.tensor_tensor(q[:, :], q[:, :], t1[:, :], ALU.add)
                    dve.drain()

                def index(out, value, valid):
                    dve.tensor_tensor(t1[:, :], value[:, :], valid[:, :], ALU.mult)
                    dve.tensor_scalar(t2[:, :], valid[:, :], -float(NOWHERE), float(NOWHERE), ALU.mult, ALU.add)
                    dve.drain()
                    dve.tensor_tensor(t1[:, :], t1[:, :], t2[:, :], ALU.add)
                    dve.drain()
                    dve.tensor_copy(out[:, 0:NT], t1[:, :])
                    dve.drain()

                row_of(q1, base)
                row_of(q2, end)
                index(self.seg_at[g.name], base, nz)
                index(self.end_at[g.name], end, nz)
                dve.tensor_tensor(q1[:, :], q2[:, :], q1[:, :], ALU.is_gt)
                dve.drain()
                dve.tensor_tensor(nz[:, :], nz[:, :], q1[:, :], ALU.mult)
                dve.drain()
                index(self.carry_at[g.name], q2, nz)

    def norm_stats(self, stack):
        nc = self.nc
        mean = self.sb(stack, "mean", [P, NT])
        rstd = self.sb(stack, "rstd", [P, NT])
        with ExitStack() as here:
            (mv, st, mv7, eps, std) = self.several(
                here, "stat_parts",
                [P, NT, 2],
                [P, 7, 6],
                [P, 7, 2],
                [P, 1],
                [P, NT])
            stats_done, root_done = self.sem(here, "stats_done"), self.sem(here, "root_done")
            block = here.enter_context(nc.Block())

            @block.vector
            def _(dve):
                dve.memset(eps[:, :], EPS)
                with dve.Fori(0, NT // 7) as i:
                    for u in range(7):
                        dve.bn_stats(st[:, u, :], self.X[:, bass.ds(i * 7 + u, 1), :].rearrange("p a d -> p (a d)"))
                    dve.drain()
                    for u in range(7):
                        dve.bn_aggr(mv7[:, u, :], st[:, u, :])
                    dve.drain()
                    dve.tensor_copy(mv[:, bass.ds(i * 7, 7), :], mv7[:, :, :])
                    dve.drain()
                dve.tensor_copy(mean[:, :], mv[:, :, 0]).then_inc(stats_done, 1)
                dve.wait_ge(root_done, 1)
                dve.reciprocal(rstd[:, :], std[:, :])

            @block.scalar
            def _(act):
                act.wait_ge(stats_done, 1)
                act.activation(std[:, :], mv[:, :, 1], ACT.Sqrt, bias=eps[:, 0:1]).then_inc(root_done, 1)
        return mean, rstd

    def project(self, stack):
        nc, io = self.nc, self.io
        ident, ones = self.ident, self.ones
        kmax = self.sb(stack, "kmax", [P, D])
        with ExitStack() as here:
            mean, rstd = self.norm_stats(here)
            w_rows = self.sb(here, "w_rows", [P, 2, D])
            att = self.sb(here, "att", [P, 2, 2 * H])
            wz = self.sb(here, "wz", [P, 2, D + 2 * H])
            wqkv = self.sb(here, "wqkv", [P, 2, 3 * D])
            (xn, xt) = self.several(
                here, "turned_rows",
                [P, 2, D],
                [P, 2, 2, P])
            (z_row, qkv, km) = self.several(
                here, "kmax_parts",
                [P, 2, D + 2 * H],
                [P, 2, 3 * D],
                [P, D])
            kcol = self.sb(here, "kcol", [P, 2])
            kdiag = self.sb(here, "kdiag", [P, 2, P])
            tp = self.ps(here, "tp", [P, 2, 512])
            pz, pqk = self.ps(here, "pz", [P, 2, 512]), self.ps(here, "pqk", [P, 2, 512])
            pv = self.ps(here, "pv", [P, 2, 512])
            names = ("att_clear", "w_loaded", "w_turned", "w_ready", "xn_ready", "turned", "xt_ready", "projected",
                     "z_evac", "qk_evac", "km_ready", "k_turned", "k_diag", "k_spread")
            (att_clear, w_loaded, w_turned, w_ready, xn_ready, turned, xt_ready, projected,
             z_evac, qk_evac, km_ready, k_turned, k_diag, k_spread) = (self.sem(here, n) for n in names)
            z_out = [self.sem(here, f"z_out{s}") for s in range(2)]
            qkv_out = [self.sem(here, f"qkv_out{s}") for s in range(2)]
            block = here.enter_context(nc.Block())

            @block.sync
            def _(sp):
                sp.dma_start(w_rows[:, :, :], io["L0_gnn_W"].rearrange("h o i -> (h o) i").rearrange("(k p) i -> p k i", p=P)) \
                  .then_inc(w_loaded, 16)
                sp.dma_start(wqkv[:, :, :], io["L0_mix_Wqkv"].rearrange("(k p) c -> p k c", p=P)).then_inc(w_loaded, 16)
                sp.wait_ge(att_clear, 1)
                for h in range(H):
                    rows = slice(64 * (h % 2), 64 * (h % 2) + 64)
                    for side in range(2):
                        sp.dma_start(att[rows, h // 2, side * H + h:side * H + h + 1],
                                     io["L0_gnn_att"][h, 64 * side:64 * side + 64].rearrange("(o a) -> o a", a=1)) \
                          .then_inc(w_loaded, 16)
                sp.wait_ge(w_loaded, 160)

                def store(t, i, s):
                    sp.wait_ge(z_evac, t + 1)
                    sp.dma_start(self.row_dram["gnn"][bass.ds(t * P, P), :], z_row[:, s, 0:GNN.row]).then_inc(z_out[s], 16)
                    sp.wait_ge(qk_evac, t + 1)
                    sp.dma_start(self.qkv_dram[bass.ds(t * P, P), :], qkv[:, s, :]).then_inc(qkv_out[s], 16)
                in_pairs(sp, NT, store)
                for s in range(2):
                    sp.wait_ge(z_out[s], 16 * ((NT + 1 - s) // 2))
                    sp.wait_ge(qkv_out[s], 16 * ((NT + 1 - s) // 2))

            @block.tensor
            def _(pe):
                pe.wait_ge(w_loaded, 160)
                for k in range(2):
                    for r in range(2):
                        pe.transpose(pz[:, k, r * P:(r + 1) * P], w_rows[:, r, k * P:(k + 1) * P], ident[:, :])
                for k in range(2):
                    for r in range(2):
                        mm = pe.matmul(pqk[:, k, 0:2 * H], w_rows[:, r, k * P:(k + 1) * P], att[:, r, :],
                                       start=(r == 0), stop=(r == 1))
                mm.then_inc(w_turned, 1)
                pe.wait_ge(w_ready, 1)

                def step(t, i, s):
                    pe.wait_ge(xn_ready, t + 1)
                    if not first(i):
                        pe.wait_ge(xt_ready, t - 1)
                    for k in range(2):
                        mm = pe.transpose(tp[:, s, k * P:(k + 1) * P], xn[:, s, k * P:(k + 1) * P], ident[:, :])
                    mm.then_inc(turned, 1)
                    pe.wait_ge(xt_ready, t + 1)
                    if not first(i):
                        pe.wait_ge(z_evac, t - 1)
                        pe.wait_ge(qk_evac, t - 1)
                    for k in range(2):
                        pe.matmul(pz[:, s, 0:D + 2 * H], xt[:, s, k, :], wz[:, k, :], start=(k == 0), stop=(k == 1))
                    for k in range(2):
                        pe.matmul(pqk[:, s, :], xt[:, s, k, :], wqkv[:, k, 0:2 * D], start=(k == 0), stop=(k == 1))
                    for k in range(2):
                        mm = pe.matmul(pv[:, s, 0:D], xt[:, s, k, :], wqkv[:, k, 2 * D:3 * D], start=(k == 0), stop=(k == 1))
                    mm.then_inc(projected, 1)
                in_pairs(pe, NT, step)
                pe.wait_ge(km_ready, 1)
                for k in range(2):
                    mm = pe.transpose(tp[:, k, 0:P], km[:, k * P:(k + 1) * P], ident[:, :])
                mm.then_inc(k_turned, 1)
                pe.wait_ge(k_diag, 1)
                pe.wait_ge(z_evac, NT)
                for k in range(2):
                    mm = pe.matmul(pz[:, 0, k * P:(k + 1) * P], ones[:, :], kdiag[:, k, :], start=True, stop=True)
                mm.then_inc(k_spread, 1)

            @block.scalar
            def _(act):
                act.wait_ge(w_turned, 1)
                for k in range(2):
                    act.activation(wz[:, k, 0:D], pz[:, k, 0:D], ACT.Copy)
                    ins = act.activation(wz[:, k, D:D + 2 * H], pqk[:, k, 0:2 * H], ACT.Copy)
                ins.then_inc(w_ready, 1)

                def step(t, i, s):
                    act.wait_ge(turned, t + 1)
                    if not first(i):
                        act.wait_ge(projected, t - 1)
                    act.activation(xt[:, s, :, :].rearrange("p k n -> p (k n)"), tp[:, s, 0:D], ACT.Copy).then_inc(xt_ready, 1)
                    act.wait_ge(projected, t + 1)
                    if not first(i):
                        act.wait_ge(z_out[s], i * 16)
                        act.wait_ge(qkv_out[s], i * 16)
                    act.activation(z_row[:, s, :], pz[:, s, 0:D + 2 * H], ACT.Copy)
                    act.activation(self.ed["gnn"][:, bass.ds(t, 1), :].rearrange("p a h -> p (a h)"),
                                   pz[:, s, D + H:D + 2 * H], ACT.Copy)
                    act.activation(qkv[:, s, 2 * D:3 * D], pv[:, s, 0:D], ACT.Copy).then_inc(z_evac, 1)
                in_pairs(act, NT, step)

            @block.vector
            def _(dve):
                dve.memset(att[:, :, :], 0.0).then_inc(att_clear, 1)
                dve.memset(km[:, :], NEG)

                def step(t, i, s):
                    if not first(i):
                        dve.wait_ge(turned, t - 1)
                    dve.tensor_scalar(xn[:, s, :], self.X[:, bass.ds(t, 1), :].rearrange("p a d -> p (a d)"),
                                      mean[:, bass.ds(t, 1)], rstd[:, bass.ds(t, 1)], ALU.subtract, ALU.mult) \
                       .then_inc(xn_ready, 1)
                    dve.drain()
                    dve.wait_ge(projected, t + 1)
                    if not first(i):
                        dve.wait_ge(qkv_out[s], i * 16)
                    rows = tile_rows(t)
                    dve.tensor_tensor(km[0:rows, :], km[0:rows, :], pqk[0:rows, s, D:2 * D], ALU.max)
                    dve.tensor_copy(qkv[:, s, 0:2 * D], pqk[:, s, :]).then_inc(qk_evac, 1)
                in_pairs(dve, NT, step)
                dve.drain()
                dve.sem_inc(km_ready, 1)
                dve.wait_ge(k_turned, 1)
                dve.tensor_reduce(kcol[:, :], tp[:, :, 0:P], AX, ALU.max)
                dve.drain()
                for k in range(2):
                    ins = dve.tensor_scalar(kdiag[:, k, :], ident[:, :], kcol[:, k:k + 1], None, ALU.mult)
                ins.then_inc(k_diag, 1)
                dve.wait_ge(k_spread, 1)
                dve.tensor_copy(kmax[:, :], pz[:, 0, 0:D])
        return kmax

    def mix(self, kmax):
        nc, io = self.nc, self.io
        ident, ones = self.ident, self.ones
        SCALE = MIX_DIM ** -0.5
        with ExitStack() as here:
            (kv, ke, wout, gamma, bmask, ctx, rden, cw, q, qe, qt, mx, sm, st, mv, mv1, std, eps) = self.several(
                here, "mix_parts",
                [P, 2, 2 * D],
                [P, 2, D],
                [P, 2, D],
                [P, D],
                [P, P],
                [P, 2, P],
                [P, 2],
                [P, 2, D],
                [P, 2, D],
                [P, 2, D],
                [P, 2, D],
                [P, 2, MIX_HEADS],
                [P, 2, MIX_HEADS],
                [P, 6],
                [P, NT, 2],
                [P, 2],
                [P, NT],
                [P, 1])
            out = self.sb(here, "mix_out", [P, NT, D])
            pc = [self.ps(here, f"pc{j}", [P, 512]) for j in range(2)]
            pd = [self.ps(here, f"pd{j}", [P, 512]) for j in range(2)]
            pt, pm = self.ps(here, "pt", [P, 2, 512]), self.ps(here, "pm", [P, 2, 512])
            names = ("w_loaded", "shifted", "k_exp", "summed", "ctx_ready", "cw_made", "cw_ready", "q_shifted", "q_exp",
                     "q_ready", "q_turned", "qt_ready", "mixed", "mix_evac", "var_ready", "std_ready")
            (w_loaded, shifted, k_exp, summed, ctx_ready, cw_made, cw_ready, q_shifted, q_exp,
             q_ready, q_turned, qt_ready, mixed, mix_evac, var_ready, std_ready) = (self.sem(here, n) for n in names)
            kv_in = [self.sem(here, f"kv_in{s}") for s in range(2)]
            q_in = [self.sem(here, f"q_in{s}") for s in range(2)]
            block = here.enter_context(nc.Block())

            @block.sync
            def _(sp):
                sp.dma_start(wout[:, :, :], io["L0_mix_Wout"].rearrange("(k p) c -> p k c", p=P)).then_inc(w_loaded, 16)
                sp.dma_start(gamma[:, :], io["L0_mix_gamma"].partition_broadcast(P)).then_inc(w_loaded, 16)

                def load_kv(t, i, s):
                    if not first(i):
                        sp.wait_ge(summed, t - 1)
                    sp.dma_start(kv[:, s, :], self.qkv_dram[bass.ds(t * P, P), D:3 * D]).then_inc(kv_in[s], 16)
                in_pairs(sp, NT, load_kv)

                def load_q(t, i, s):
                    if not first(i):
                        sp.wait_ge(q_shifted, t - 1)
                    sp.dma_start(q[:, s, :], self.qkv_dram[bass.ds(t * P, P), 0:D]).then_inc(q_in[s], 16)
                in_pairs(sp, NT, load_q)

            @block.tensor
            def _(pe):
                def context(t, i, s):
                    rows = tile_rows(t)
                    pe.wait_ge(k_exp, t + 1)
                    head, tail = first(i) and s == 0, isinstance(t, int) and t == NT - 1
                    for j in range(2):
                        cols = slice(j * P, (j + 1) * P)
                        pe.matmul(pc[j][:, 0:P], kv[0:rows, s, D + j * P:D + (j + 1) * P], ke[0:rows, s, cols],
                                  start=head, stop=tail, skip_group_check=True)
                        mm = pe.matmul(pd[j][:, 0:1], ke[0:rows, s, cols], ones[0:rows, 0:1], start=head, stop=tail,
                                       skip_group_check=True)
                    mm.then_inc(summed, 1)
                in_pairs(pe, NT, context)
                pe.wait_ge(w_loaded, 32)
                pe.wait_ge(ctx_ready, 1)
                for j in range(2):
                    mm = pe.matmul(pm[:, j, 0:D], ctx[:, j, :], wout[:, j, :], start=True, stop=True)
                mm.then_inc(cw_made, 1)
                pe.wait_ge(cw_ready, 1)

                def rows_out(t, i, s):
                    pe.wait_ge(q_ready, t + 1)
                    if not first(i):
                        pe.wait_ge(qt_ready, t - 1)
                    for j in range(2):
                        mm = pe.transpose(pt[:, s, j * P:(j + 1) * P], qe[:, s, j * P:(j + 1) * P], ident[:, :])
                    mm.then_inc(q_turned, 1)
                    pe.wait_ge(qt_ready, t + 1)
                    if not first(i):
                        pe.wait_ge(mix_evac, t - 1)
                    for j in range(2):
                        mm = pe.matmul(pm[:, s, 0:D], qt[:, s, j * P:(j + 1) * P], cw[:, j, :], start=(j == 0), stop=(j == 1))
                    mm.then_inc(mixed, 1)
                in_pairs(pe, NT, rows_out)

            @block.scalar
            def _(act):
                def exp_k(t, i, s):
                    act.wait_ge(shifted, t + 1)
                    act.activation(ke[:, s, :], ke[:, s, :], ACT.Exp).then_inc(k_exp, 1)
                in_pairs(act, NT, exp_k)

                def step(t, i, s):
                    act.wait_ge(q_shifted, t + 1)
                    act.activation(qe[:, s, :], qe[:, s, :], ACT.Exp).then_inc(q_exp, 1)
                    act.wait_ge(q_turned, t + 1)
                    if not first(i):
                        act.wait_ge(mixed, t - 1)
                    act.activation(qt[:, s, :], pt[:, s, 0:D], ACT.Copy).then_inc(qt_ready, 1)
                in_pairs(act, NT, step)
                act.wait_ge(var_ready, 1)
                act.activation(std[:, :], mv[:, :, 1], ACT.Sqrt, bias=eps[:, 0:1]).then_inc(std_ready, 1)

            @block.vector
            def _(dve):
                dve.memset(eps[:, :], EPS)
                dve.memset(bmask[:, :], 0.0)
                dve.drain()
                for a in range(P // MIX_DIM):
                    b = slice(a * MIX_DIM, (a + 1) * MIX_DIM)
                    dve.memset(bmask[b, b], 1.0)

                def shift_k(t, i, s):
                    dve.wait_ge(kv_in[s], i * 16 + 16)
                    if not first(i):
                        dve.wait_ge(summed, t - 1)
                    dve.tensor_tensor(ke[:, s, :], kv[:, s, 0:D], kmax[:, :], ALU.subtract).then_inc(shifted, 1)
                in_pairs(dve, NT, shift_k)
                dve.wait_ge(summed, NT)
                for j in range(2):
                    dve.tensor_tensor(ctx[:, j, :], pc[j][:, 0:P], bmask[:, :], ALU.mult)
                    ins = dve.reciprocal(rden[:, j:j + 1], pd[j][:, 0:1])
                ins.then_inc(ctx_ready, 1)
                dve.drain()
                dve.wait_ge(cw_made, 1)
                for j in range(2):
                    ins = dve.tensor_scalar(cw[:, j, :], pm[:, j, 0:D], rden[:, j:j + 1], SCALE, ALU.mult, ALU.mult)
                ins.then_inc(cw_ready, 1)
                dve.wait_ge(w_loaded, 32)

                def by_head(ap):
                    return ap.rearrange("p (h d) -> p h d", d=MIX_DIM)

                def each(ap):
                    return ap.unsqueeze(2).to_broadcast([P, MIX_HEADS, MIX_DIM])

                def step(t, i, s):
                    dve.wait_ge(q_in[s], i * 16 + 16)
                    if not first(i):
                        dve.wait_ge(q_turned, t - 1)
                    dve.tensor_reduce(mx[:, s, :], by_head(q[:, s, :]), AX, ALU.max)
                    dve.drain()
                    dve.tensor_tensor(by_head(qe[:, s, :]), by_head(q[:, s, :]), each(mx[:, s, :]), ALU.subtract) \
                       .then_inc(q_shifted, 1)
                    dve.wait_ge(q_exp, t + 1)
                    dve.tensor_reduce(sm[:, s, :], by_head(qe[:, s, :]), AX, ALU.add)
                    dve.drain()
                    dve.reciprocal(sm[:, s, :], sm[:, s, :])
                    dve.drain()
                    dve.tensor_tensor(by_head(qe[:, s, :]), by_head(qe[:, s, :]), each(sm[:, s, :]), ALU.mult) \
                       .then_inc(q_ready, 1)
                    dve.wait_ge(mixed, t + 1)
                    dve.bn_stats(st[:, :], pm[:, s, 0:D])
                    dve.tensor_copy(row(out, t), pm[:, s, 0:D]).then_inc(mix_evac, 1)
                    dve.drain()
                    dve.bn_aggr(mv1[:, :], st[:, :])
                    dve.drain()
                    dve.tensor_copy(row(mv, t), mv1[:, :])
                    dve.drain()

                def row(tensor, t):
                    return tensor[:, bass.ds(t, 1), :].rearrange("p a d -> p (a d)")
                in_pairs(dve, NT, step)
                dve.sem_inc(var_ready, 1)
                dve.wait_ge(std_ready, 1)
                dve.reciprocal(std[:, :], std[:, :])
                dve.drain()
                with dve.Fori(0, NT // 7) as i:
                    for u in range(7):
                        t = i * 7 + u
                        dve.tensor_scalar(row(out, t), row(out, t), mv[:, bass.ds(t, 1), 0], std[:, bass.ds(t, 1)],
                                          ALU.subtract, ALU.mult)
                    dve.drain()
                    block7 = out[:, bass.ds(i * 7, 7), :]
                    dve.tensor_tensor(block7, block7, gamma[:, :].unsqueeze(1).to_broadcast([P, 7, D]), ALU.mult)
                    dve.drain()
                    x7 = self.X[:, bass.ds(i * 7, 7), :]
                    dve.tensor_tensor(x7, x7, block7, ALU.add)

    def sort_edges(self):
        nc, io = self.nc, self.io
        W, T = FFN.width, SORT_TILES
        ident = self.ident
        dst, src = io["L0_ffn_edge_index"][1, :], io["L0_ffn_edge_index"][0, :]
        with ExitStack() as here:
            raw, rawf = self.sb(here, "raw", [P, W], I32), self.sb(here, "rawf", [P, W])
            di = self.sb(here, "di", [P, W], I32)
            (dcol, lo, hi, src_lo, src_hi) = self.several(
                here, "columns",
                [P, T, P],
                [P, T, P],
                [P, T, P],
                [P, T, P],
                [P, T, P])
            iota_i = self.sb(here, "iota_i", [P, W], I32)
            iota_w, iota_b = self.sb(here, "iota_w", [P, W], FP16), self.sb(here, "iota_b", [P, P], BF16)
            iota_p, iota_pi = self.sb(here, "iota_p", [P, 1]), self.sb(here, "iota_pi", [P, 1], I32)
            earlier = self.sb(here, "earlier", [P, P])
            row_d, row_lo = self.sb(here, "row_d", [P, 2, W], I32), self.sb(here, "row_lo", [P, 2, W], I32)
            oht = self.sb(here, "oht", [P, 2, W])
            oh_lo, oh_hi = self.sb(here, "oh_lo", [P, 2, T, P], BF16), self.sb(here, "oh_hi", [P, 2, T, HIS], BF16)
            equal, looked = self.sb(here, "equal", [P, T, P], BF16), self.sb(here, "looked", [P, T, HIS])
            (intra, slot, to_p, to_w, free_sb) = self.several(
                here, "sort_small",
                [P, 2, T],
                [P, 2, T],
                [P, T],
                [P, T],
                [P, 2, HIS])
            pos_i, part_i = self.sb(here, "pos_i", [P, T], I32), self.sb(here, "part_i", [P, T], I32)
            oh_w = self.sb(here, "oh_w", [P, 4, W], FP16)
            put_lo, put_hi = self.sb(here, "put_lo", [P, 4, P], FP16), self.sb(here, "put_hi", [P, 4, P], FP16)
            free = self.ps(here, "free", [P, 512])
            at = self.ps(here, "at", [P, 2, T, HIS])
            placed = self.ps(here, "placed", [P, W])
            tp = self.ps(here, "tp", [P, 2, 512])
            names = ("made", "raw_loaded", "raw_ready", "raw_turned", "cols_ready", "hot", "table_ready", "looked_up",
                     "table_next", "ranked", "put_ready", "put_done")
            (made, raw_loaded, raw_ready, raw_turned, cols_ready, hot, table_ready, looked_up,
             table_next, ranked, put_ready, put_done) = (self.sem(here, n) for n in names)
            rows_in = [self.sem(here, f"rows_in{s}") for s in range(2)]
            block = here.enter_context(nc.Block())

            @block.gpsimd
            def _(pool):
                pool.iota(iota_i[:, :], pattern=[[1, W]], base=0, channel_multiplier=0)
                pool.iota(iota_pi[:, :], pattern=[[0, 1]], base=0, channel_multiplier=1)
                pool.affine_select(out=earlier[:, :], in_=self.ones[:, :], compare_op=ALU.is_gt, fill=0.0,
                                   base=0, pattern=[[-1, P]], channel_multiplier=1)
                pool.drain()
                pool.tensor_copy(iota_w[:, :], iota_i[:, :])
                pool.tensor_copy(iota_b[:, :], iota_i[:, 0:P])
                pool.tensor_copy(iota_p[:, :], iota_pi[:, :]).then_inc(made, 1)

            @block.sync
            def _(sp):
                sp.dma_start(raw[:, :], dst.rearrange("(p w) -> p w", w=W)).then_inc(raw_loaded, 16)
                sp.wait_ge(raw_ready, 1)
                sp.dma_start(raw[:, :], src.rearrange("(p w) -> p w", w=W)).then_inc(raw_loaded, 16)

                def load_rows(b, i, s):
                    if not first(i):
                        sp.wait_ge(hot, b * T - T)
                    sp.dma_start(row_d[:, s, :], dst[bass.ds(b * W, W)].partition_broadcast(P)).then_inc(rows_in[s], 16)
                    sp.dma_start(row_lo[:, s, :], self.lo_dram[bass.ds(b, 1), :].rearrange("a w -> (a w)")
                                 .partition_broadcast(P)).then_inc(rows_in[s], 16)
                in_pairs(sp, SORT_BLOCKS, load_rows)

            @block.tensor
            def _(pe):
                for n in range(2):
                    pe.wait_ge(raw_ready, n + 1)
                    for j in range(T):
                        mm = pe.transpose(tp[:, j // 4, (j % 4) * P:(j % 4 + 1) * P], rawf[:, j * P:(j + 1) * P], ident[:, :])
                    mm.then_inc(raw_turned, 1)
                    pe.wait_ge(cols_ready, n + 1)
                pe.matmul(free[:, 0:HIS], ident[:, :], self.base_ffn[:, :], start=True, stop=False,
                          skip_group_check=True).then_inc(table_next, 1)

                def rank(b, i, s):
                    for j in range(T):
                        n = b * T + j
                        pe.wait_ge(table_ready, n + 1)
                        pe.wait_ge(hot, n + 1)
                        pe.matmul(at[:, s, j, :], oht[:, s, j * P:(j + 1) * P], free_sb[:, j % 2, :],
                                  start=True, stop=True, skip_group_check=True).then_inc(looked_up, 1)
                        pe.matmul(free[:, 0:HIS], oh_lo[:, s, j, :], oh_hi[:, s, j, :], start=False, stop=False,
                                  skip_group_check=True).then_inc(table_next, 1)

                def put(b, head, tail):
                    for j in range(T):
                        pe.wait_ge(put_ready, b * T + (j + 1))
                        for half in range(2):
                            cols = slice(half * 512, (half + 1) * 512)
                            pe.matmul(placed[:, cols], put_hi[:, j % 4, :], oh_w[:, j % 4, cols],
                                      start=(head and j == 0), stop=False, skip_group_check=True)
                            mm = pe.matmul(placed[:, cols], put_lo[:, j % 4, :], oh_w[:, j % 4, cols],
                                           start=False, stop=(tail and j == T - 1), skip_group_check=True)
                        mm.then_inc(put_done, 1)
                rank(0, 0, 0)
                rank(1, 0, 1)
                put(0, True, False)
                with pe.Fori(1, SORT_BLOCKS // 2) as i:
                    rank(i * 2, i, 0)
                    put(i * 2 - 1, False, False)
                    rank(i * 2 + 1, i, 1)
                    put(i * 2, False, False)
                put(SORT_BLOCKS - 1, False, True)

            @block.scalar
            def _(act):
                def copy_table(b, i, s):
                    for j in range(T):
                        n = b * T + j
                        act.wait_ge(table_next, n + 1)
                        act.activation(free_sb[:, j % 2, :], free[:, 0:HIS], ACT.Copy).then_inc(table_ready, 1)
                in_pairs(act, SORT_BLOCKS, copy_table)

            @block.vector
            def _(dve):
                dve.wait_ge(raw_loaded, 16)
                dve.tensor_copy(rawf[:, :], raw[:, :]).then_inc(raw_ready, 1)
                flat = "p a b -> p (a b)"
                dve.wait_ge(raw_turned, 1)
                turned = tp[:, :, :].rearrange(flat)
                dve.tensor_copy(dcol[:, :, :].rearrange(flat), turned)
                dve.tensor_copy(di[:, :], turned)
                dve.drain()
                dve.tensor_scalar(di[:, :], di[:, :], 7, None, ALU.logical_shift_right)
                dve.drain()
                dve.tensor_copy(hi[:, :, :].rearrange(flat), di[:, :])
                dve.drain()
                dve.scalar_tensor_tensor(lo[:, :, :].rearrange(flat), hi[:, :, :].rearrange(flat), -float(P),
                                         dcol[:, :, :].rearrange(flat), ALU.mult, ALU.add)
                dve.wait_ge(raw_loaded, 32)
                dve.tensor_scalar(rawf[:, :], raw[:, :], float(N - 1), None, ALU.min)
                dve.drain()
                dve.sem_inc(cols_ready, 1)
                dve.sem_inc(raw_ready, 1)
                dve.wait_ge(raw_turned, 2)
                dve.tensor_copy(di[:, :], turned)
                dve.tensor_copy(src_lo[:, :, :].rearrange(flat), turned)
                dve.drain()
                dve.tensor_scalar(di[:, :], di[:, :], (HIS - 1) * P, None, ALU.bitwise_and)
                dve.drain()
                dve.tensor_copy(src_hi[:, :, :].rearrange(flat), di[:, :])
                dve.drain()
                dve.tensor_tensor(src_lo[:, :, :].rearrange(flat), src_lo[:, :, :].rearrange(flat),
                                  src_hi[:, :, :].rearrange(flat), ALU.subtract)
                dve.drain()
                dve.sem_inc(cols_ready, 1)
                dve.wait_ge(made, 1)

                def prepare(b, i, s):
                    dve.drain()
                    dve.wait_ge(rows_in[s], i * 32 + 32)
                    if not first(i):
                        dve.wait_ge(looked_up, b * T - T)
                        dve.wait_ge(table_next, b * T - T + 1)
                    dve.tensor_scalar(oht[:, s, :], row_lo[:, s, :], iota_p[:, 0:1], None, ALU.is_equal)
                    for j in range(T):
                        dve.tensor_scalar(oh_lo[:, s, j, :], iota_b[:, :], lo[:, j, bass.ds(b, 1)], None, ALU.is_equal)
                        dve.tensor_scalar(oh_hi[:, s, j, :], iota_b[:, 0:HIS], hi[:, j, bass.ds(b, 1)], None, ALU.is_equal)
                        dve.scalar_tensor_tensor(equal[:, j, :], row_d[:, s, j * P:(j + 1) * P], dcol[:, j, bass.ds(b, 1)],
                                                 earlier[:, :], ALU.is_equal, ALU.mult,
                                                 accum_out=intra[:, s, j:j + 1]).then_inc(hot, 1)

                def finish(b, s):
                    dve.wait_ge(looked_up, b * T + T)
                    for j in range(T):
                        dve.tensor_tensor_reduce(looked[:, j, :], at[:, s, j, :], oh_hi[:, s, j, :], 1.0, 0.0,
                                                 ALU.mult, ALU.add, slot[:, s, j:j + 1])
                    dve.drain()
                    dve.tensor_tensor(pos_i[:, :], slot[:, s, :], intra[:, s, :], ALU.add)
                    dve.drain()
                    dve.tensor_scalar(part_i[:, :], pos_i[:, :], 10, None, ALU.logical_shift_right)
                    dve.tensor_scalar(pos_i[:, :], pos_i[:, :], W - 1, None, ALU.bitwise_and)
                    dve.drain()
                    dve.tensor_copy(to_p[:, :], part_i[:, :])
                    dve.tensor_copy(to_w[:, :], pos_i[:, :])
                    dve.drain()
                    for j in range(T):
                        if not (isinstance(b, int) and b == 0 and j < 4):
                            dve.wait_ge(put_done, b * T + (j - 3))
                        dve.tensor_scalar(oh_w[:, j % 4, :], iota_w[:, :], to_w[:, j:j + 1], None, ALU.is_equal)
                        dve.tensor_scalar(put_hi[:, j % 4, :], iota_w[:, 0:P], to_p[:, j:j + 1],
                                          src_hi[:, j, bass.ds(b, 1)], ALU.is_equal, ALU.mult)
                        dve.tensor_scalar(put_lo[:, j % 4, :], iota_w[:, 0:P], to_p[:, j:j + 1],
                                          src_lo[:, j, bass.ds(b, 1)], ALU.is_equal, ALU.mult).then_inc(put_ready, 1)
                assert W == 1 << 10
                prepare(0, 0, 0)
                prepare(1, 0, 1)
                finish(0, 0)
                with dve.Fori(1, SORT_BLOCKS // 2) as i:
                    prepare(i * 2, i, 0)
                    finish(i * 2 - 1, 1)
                    prepare(i * 2 + 1, i, 1)
                    finish(i * 2, 0)
                finish(SORT_BLOCKS - 1, 1)
                dve.wait_ge(put_done, SORT_BLOCKS * T)
                dve.tensor_copy(self.edge_src["ffn"][:, 0:W], placed[:, :])

    def edges(self, g):
        nc = self.nc
        W, T, C, R, S, K = g.width, g.chunk, g.cols, g.row, g.state, g.per_head
        ident, ones = self.ident, self.ones
        seg_dram, state_dram, carry_dram = self.seg_dram[g.name], self.state_dram[g.name], self.carry_dram[g.name]
        src = self.edge_src[g.name]
        with ExitStack() as here:
            neg = self.sb(here, "neg", [P, W])
            ed = self.sb(here, "ed_edge", [P, H, W])
            whole, whole_neg = self.sb(here, "whole", [P, 1]), self.sb(here, "whole_neg", [P, 1])
            diag = self.sb(here, "diag", [P, P])
            whole_row = self.sb(here, "whole_row", [H, P])
            self.part = f"starts_{g.name}"
            with ExitStack() as mine:
                (seg_rows, seg, same, last, chain, carry_in, lastt) = self.several(
                    mine, "start_parts",
                    [P, NT, 1 + H],
                    [P, W, 1 + H],
                    [P, W],
                    [P, H],
                    [H, P + 1],
                    [P, H],
                    [H, P])
                pa, pb = self.ps(mine, "pa", [P, P]), self.ps(mine, "pb", [P, P])
                names = ("zeroed", "cleared", "rows_ready", "scattered", "seg_loaded", "last_ready", "spread", "chained", "turned")
                zeroed, cleared, rows_ready, scattered, seg_loaded, last_ready, spread, chained, turned = \
                    (self.sem(mine, n) for n in names)
                block = mine.enter_context(nc.Block())

                @block.sync
                def _(sp):
                    sp.wait_ge(zeroed, 1)
                    sp.dma_start(seg_dram.rearrange("(p w) c -> p (w c)", w=W), seg[:, :, :].rearrange("p w c -> p (w c)")) \
                      .then_inc(cleared, 16)
                    sp.wait_ge(scattered, 16 * NT)
                    sp.dma_start(seg[:, :, :].rearrange("p w c -> p (w c)"), seg_dram.rearrange("(p w) c -> p (w c)", w=W)) \
                      .then_inc(seg_loaded, 16)
                    sp.wait_ge(seg_loaded, 16)

                @block.gpsimd
                def _(pool):
                    bound = pool.to_reg(P * W - 1)
                    pool.wait_ge(rows_ready, 1)
                    pool.wait_ge(cleared, 16)
                    for t in range(NT):
                        pool.indirect_dma_start(
                            out=seg_dram[:, :], out_offset=bass.IndirectOffsetOnAxis(ap=self.seg_at[g.name][:, t:t + 1], axis=0),
                            in_=seg_rows[:, t, :], in_offset=None, bounds_check=bound, oob_is_err=False).then_inc(scattered, 16)
                    pool.wait_ge(scattered, 16 * NT)

                @block.vector
                def _(dve):
                    dve.memset(seg[:, :, :], 0.0).then_inc(zeroed, 1)
                    dve.memset(seg_rows[:, :, 0:1], 1.0)
                    dve.tensor_copy(seg_rows[:, :, 1:1 + H], self.ed[g.name][:, :, :]).then_inc(rows_ready, 1)
                    dve.wait_ge(seg_loaded, 16)
                    dve.tensor_scalar(neg[:, :], seg[:, :, 0], NEG, None, ALU.mult)
                    dve.tensor_scalar(same[:, :], seg[:, :, 0], -1.0, 1.0, ALU.mult, ALU.add)
                    dve.tensor_reduce(whole[:, :], seg[:, :, 0], AX, ALU.max)
                    dve.drain()
                    dve.tensor_scalar(whole[:, :], whole[:, :], -1.0, 1.0, ALU.mult, ALU.add)
                    for h in range(H):
                        dve.tensor_tensor_scan(ed[:, h, :], same[:, :], seg[:, :, 1 + h], 0.0, ALU.mult, ALU.add)
                    dve.drain()
                    dve.tensor_copy(last[:, :], ed[:, :, W - 1])
                    dve.tensor_scalar(whole_neg[:, :], whole[:, :], -NEG, NEG, ALU.mult, ALU.add)
                    dve.tensor_scalar(diag[:, :], ident[:, :], whole[:, 0:1], None, ALU.mult)
                    dve.drain()
                    dve.sem_inc(last_ready, 1)
                    dve.wait_ge(spread, 1)
                    dve.tensor_copy(whole_row[:, :], pb[0:H, :])
                    dve.tensor_copy(lastt[:, :], pa[0:H, :])
                    dve.memset(chain[:, 0:1], 0.0)
                    dve.drain()
                    dve.tensor_tensor_scan(chain[:, 1:P + 1], whole_row[:, :], lastt[:, :], 0.0, ALU.mult, ALU.add).then_inc(chained, 1)
                    dve.wait_ge(turned, 1)
                    dve.tensor_copy(carry_in[:, :], pa[:, 0:H])
                    dve.drain()
                    for h in range(H):
                        dve.tensor_tensor_scan(ed[:, h, :], same[:, :], seg[:, :, 1 + h], carry_in[:, h:h + 1], ALU.mult, ALU.add)

                @block.tensor
                def _(pe):
                    pe.wait_ge(last_ready, 1)
                    pe.transpose(pa[0:H, :], last[:, :], ident[:, :])
                    pe.matmul(pb[0:H, :], ones[:, 0:H], diag[:, :], start=True, stop=True).then_inc(spread, 1)
                    pe.wait_ge(chained, 1)
                    pe.transpose(pa[:, 0:H], chain[:, 0:P], ident[0:H, 0:H]).then_inc(turned, 1)

            self.part = f"edges_{g.name}"
            fin, finm = self.sb(here, "fin", [P, C + H]), self.sb(here, "finm", [P, H])
            with ExitStack() as mine:
                idx = self.sb(mine, "idx", [P, 2, T], I32)
                got = self.sb(mine, "got", [P, 2, T, R])
                (e, m, dl, pm, w, r) = self.several(
                    mine, "chunk_parts",
                    [P, H, T],
                    [P, 2, H, T + 1],
                    [P, H, T + 1],
                    [P, H, T],
                    [P, H, T],
                    [P, C + H, T + 1])
                y = self.sb(mine, "y", [P, 2, C + H, T + 1])
                rows = self.sb(mine, "rows", [P, 2, T, S])
                names = ("idx_ready", "gather_begun", "logits_ready", "w_ready", "r_ready", "scanned", "rows_ready")
                idx_ready, gather_begun, logits_ready, w_ready, r_ready, scanned, rows_ready = \
                    (self.sem(mine, n) for n in names)
                gathered = [self.sem(mine, f"gathered{s}") for s in range(2)]
                stored = [self.sem(mine, f"stored{s}") for s in range(2)]
                block = mine.enter_context(nc.Block())

                @block.gpsimd
                def _(pool):
                    bound = pool.to_reg(NPAD - 1)

                    def gather(c, i, s):
                        pool.wait_ge(idx_ready, c + 1)
                        pool.sem_inc(gather_begun, 1)
                        for t in range(T):
                            pool.indirect_dma_start(
                                out=got[:, s, t, :], out_offset=None, in_=self.row_dram[g.name][:, :],
                                in_offset=bass.IndirectOffsetOnAxis(ap=idx[:, s, t:t + 1], axis=0),
                                bounds_check=bound, oob_is_err=False).then_inc(gathered[s], 16)
                    in_pairs(pool, g.chunks, gather)

                @block.vector
                def _(dve):
                    for s in range(2):
                        dve.tensor_copy(idx[:, s, :], src[:, s * T:(s + 1) * T]).then_inc(idx_ready, 1)
                    dve.memset(m[:, 1, :, T:T + 1], NEG)
                    dve.memset(dl[:, :, 0:1], NEG)
                    dve.memset(y[:, 1, :, T:T + 1], 0.0)
                    dve.drain()

                    def step(c, i, s):
                        at = bass.ds(c * T, T)
                        neg_h = neg[:, at].unsqueeze(1).to_broadcast([P, H, T])
                        dve.wait_ge(gathered[s], i * (16 * T) + 16 * T)
                        dve.tensor_tensor(e[:, :, :], got[:, s, :, C:C + H].rearrange("p t h -> p h t"), ed[:, :, at], ALU.add)
                        if not first(i):
                            dve.wait_ge(rows_ready, c - 1)
                        dve.tensor_copy(m[:, s, :, 0:1], m[:, 1 - s, :, T:T + 1])
                        dve.drain()
                        dve.scalar_tensor_tensor(e[:, :, :], e[:, :, :], g.slope, e[:, :, :], ALU.mult, ALU.max)
                        dve.drain()
                        for h in range(H):
                            dve.tensor_tensor_scan(m[:, s, h, 1:T + 1], neg[:, at], e[:, h, :], m[:, s, h, 0:1], ALU.add, ALU.max)
                        dve.drain()
                        dve.tensor_tensor(pm[:, :, :], e[:, :, :], m[:, s, :, 1:T + 1], ALU.subtract)
                        dve.tensor_tensor(dl[:, :, 1:T + 1], m[:, s, :, 0:T], neg_h, ALU.add)
                        dve.drain()
                        dve.tensor_tensor(dl[:, :, 1:T + 1], dl[:, :, 1:T + 1], m[:, s, :, 1:T + 1], ALU.subtract) \
                           .then_inc(logits_ready, 1)
                        dve.tensor_copy(y[:, s, :, 0:1], y[:, 1 - s, :, T:T + 1])
                        dve.wait_ge(w_ready, c + 1)
                        for h in range(H):
                            dve.tensor_tensor(y[:, s, h * K:(h + 1) * K, 1:T + 1],
                                              got[:, s, :, h * K:(h + 1) * K].rearrange("p t k -> p k t"),
                                              w[:, h, :].unsqueeze(1).to_broadcast([P, K, T]), ALU.mult)
                        dve.tensor_copy(y[:, s, C:C + H, 1:T + 1], w[:, :, :])
                        dve.drain()
                        dve.tensor_copy(idx[:, s, :], src[:, bass.ds((c + 2) * T, T)]).then_inc(idx_ready, 1)
                        dve.wait_ge(r_ready, c + 1)
                        flat = y[:, s, :, :].rearrange("p c t -> p (c t)")
                        dve.tensor_tensor_scan(flat, r[:, :, :].rearrange("p c t -> p (c t)"), flat, 0.0, ALU.mult, ALU.add) \
                           .then_inc(scanned, 1)
                        dve.drain()
                    in_pairs(dve, g.chunks, step)
                    dve.tensor_copy(fin[:, :], y[:, 1, :, T])
                    dve.tensor_copy(finm[:, :], m[:, 1, :, T])

                @block.scalar
                def _(act):
                    def step(c, i, s):
                        act.wait_ge(logits_ready, c + 1)
                        act.activation(w[:, :, :], pm[:, :, :], ACT.Exp).then_inc(w_ready, 1)
                        if not first(i):
                            act.wait_ge(scanned, c)
                        elif s == 1:
                            act.wait_ge(scanned, 1)
                        for h in range(H):
                            act.activation(r[:, h * K:(h + 1) * K, :], dl[:, h, :].unsqueeze(1).to_broadcast([P, K, T + 1]), ACT.Exp)
                        act.activation(r[:, C:C + H, :], dl[:, :, :], ACT.Exp).then_inc(r_ready, 1)
                        act.wait_ge(scanned, c + 1)
                        if not first(i):
                            act.wait_ge(stored[s], i * 16)
                        act.activation(rows[:, s, :, 0:C + H].rearrange("p t c -> p c t"), y[:, s, :, 1:T + 1], ACT.Copy)
                        act.activation(rows[:, s, :, C + H:S].rearrange("p t h -> p h t"), m[:, s, :, 1:T + 1], ACT.Copy) \
                           .then_inc(rows_ready, 1)
                    in_pairs(act, g.chunks, step)

                @block.sync
                def _(sp):
                    by_part = state_dram.rearrange("(p w) s -> p w s", w=W)

                    def store(c, i, s):
                        sp.wait_ge(rows_ready, c + 1)
                        sp.dma_start(by_part[:, bass.ds(c * T, T), :], rows[:, s, :, :]).then_inc(stored[s], 16)
                    in_pairs(sp, g.chunks, store)
                    for s in range(2):
                        sp.wait_ge(stored[s], 16 * (g.chunks // 2))

            self.part = f"carry_{g.name}"
            with ExitStack() as mine:
                groups = [(a, min(a + P, C)) for a in range(0, C, P)] + [(C, C + H)]
                (mt, ms, wn_row, f0, f1, f1c, diag2, spread_w, acc, keep_row, run, table) = self.several(
                    mine, "carry_parts",
                    [H, P],
                    [H, P + 1],
                    [H, P],
                    [H, P],
                    [H, P],
                    [P, H],
                    [P, P],
                    [H, C + H],
                    [P, P],
                    [P, P],
                    [P, len(groups), P + 1],
                    [P, S])
                pa, pb, pc = (self.ps(mine, n, [P, 512]) for n in ("pa", "pb", "pc"))
                names = ("sel_made", "diag_ready", "spread", "max_ready", "f_ready", "f_turned", "fin_ready", "fin_turned", "run_ready",
                         "run_turned", "table_ready", "table_out")
                sel_made, diag_ready, spread, max_ready, f_ready, f_turned, fin_ready, fin_turned, run_ready, run_turned, table_ready, table_out = \
                    (self.sem(mine, n) for n in names)
                block = mine.enter_context(nc.Block())

                @block.gpsimd
                def _(pool):
                    pool.memset(spread_w[:, :], 1.0)
                    pool.drain()
                    pool.affine_select(out=spread_w[:, 0:C], in_=spread_w[:, 0:C], compare_op=ALU.is_ge, fill=0.0,
                                       base=0, pattern=[[1, C]], channel_multiplier=-K)
                    pool.drain()
                    pool.affine_select(out=spread_w[:, 0:C], in_=spread_w[:, 0:C], compare_op=ALU.is_gt, fill=0.0,
                                       base=K, pattern=[[-1, C]], channel_multiplier=K)
                    pool.affine_select(out=spread_w[:, C:C + H], in_=spread_w[:, C:C + H], compare_op=ALU.is_equal, fill=0.0,
                                       base=0, pattern=[[1, H]], channel_multiplier=-1).then_inc(sel_made, 1)

                @block.tensor
                def _(pe):
                    pe.wait_ge(diag_ready, 1)
                    pe.transpose(pa[0:H, 0:P], finm[:, :], ident[:, :])
                    pe.matmul(pb[0:H, 0:P], ones[:, 0:H], diag2[:, :], start=True, stop=True).then_inc(spread, 1)
                    pe.wait_ge(max_ready, 1)
                    pe.transpose(pc[:, 0:H], ms[:, 0:P], ident[0:H, 0:H])
                    pe.wait_ge(f_ready, 1)
                    pe.transpose(pc[:, H:2 * H], f1[:, :], ident[0:H, 0:H]).then_inc(f_turned, 1)
                    pe.wait_ge(sel_made, 1)
                    pe.wait_ge(fin_ready, 1)
                    for n, (a, b) in enumerate(groups):
                        if n:
                            pe.wait_ge(run_ready, n)
                        pe.transpose(pa[0:b - a, 0:P], fin[:, a:b], ident[:, :])
                        pe.matmul(pb[0:b - a, 0:P], spread_w[:, a:b], f0[:, :], start=True, stop=True).then_inc(fin_turned, 1)
                    pe.wait_ge(run_ready, len(groups))
                    for n, (a, b) in enumerate(groups):
                        mm = pe.transpose(pc[:, a:b], run[0:b - a, n, 0:P], ident[0:b - a, 0:b - a])
                    mm.then_inc(run_turned, 1)

                @block.vector
                def _(dve):
                    dve.tensor_scalar(diag2[:, :], ident[:, :], whole_neg[:, 0:1], None, ALU.mult).then_inc(diag_ready, 1)
                    dve.memset(ms[:, 0:1], NEG)
                    dve.memset(run[:, :, 0:1], 0.0)
                    dve.wait_ge(spread, 1)
                    dve.tensor_copy(wn_row[:, :], pb[0:H, 0:P])
                    dve.tensor_copy(mt[:, :], pa[0:H, 0:P])
                    dve.drain()
                    dve.tensor_tensor_scan(ms[:, 1:P + 1], wn_row[:, :], mt[:, :], NEG, ALU.add, ALU.max)
                    dve.drain()
                    dve.tensor_tensor(f1[:, :], mt[:, :], ms[:, 1:P + 1], ALU.subtract)
                    dve.tensor_tensor(f0[:, :], ms[:, 0:P], wn_row[:, :], ALU.add)
                    dve.drain()
                    dve.tensor_tensor(f0[:, :], f0[:, :], ms[:, 1:P + 1], ALU.subtract).then_inc(max_ready, 1)
                    dve.wait_ge(f_turned, 1)
                    dve.tensor_copy(f1c[:, :], pc[:, H:2 * H])
                    dve.tensor_copy(table[:, C + H:S], pc[:, 0:H])
                    dve.drain()
                    by_head = fin[:, 0:C].rearrange("p (h k) -> p h k", k=K)
                    dve.tensor_tensor(by_head, by_head, heads(f1c[:, :], K), ALU.mult)
                    dve.tensor_tensor(fin[:, C:C + H], fin[:, C:C + H], f1c[:, :], ALU.mult).then_inc(fin_ready, 1)
                    for n, (a, b) in enumerate(groups):
                        dve.wait_ge(fin_turned, n + 1)
                        dve.tensor_copy(acc[0:b - a, :], pa[0:b - a, 0:P])
                        dve.tensor_copy(keep_row[0:b - a, :], pb[0:b - a, 0:P])
                        dve.drain()
                        dve.tensor_tensor_scan(run[0:b - a, n, 1:P + 1], keep_row[0:b - a, :], acc[0:b - a, :], 0.0,
                                               ALU.mult, ALU.add).then_inc(run_ready, 1)
                        dve.drain()
                    dve.wait_ge(run_turned, 1)
                    dve.tensor_copy(table[:, 0:C + H], pc[:, 0:C + H]).then_inc(table_ready, 1)

                @block.scalar
                def _(act):
                    act.wait_ge(max_ready, 1)
                    act.activation(f0[:, :], f0[:, :], ACT.Exp)
                    act.activation(f1[:, :], f1[:, :], ACT.Exp).then_inc(f_ready, 1)

                @block.sync
                def _(sp):
                    sp.wait_ge(table_ready, 1)
                    sp.dma_start(carry_dram[:, :], table[:, :]).then_inc(table_out, 16)
                    sp.wait_ge(table_out, 16)

    def gather_nodes(self, g, own=None, agg=None):
        nc = self.nc
        C, S, K = g.cols, g.state, g.per_head
        parts = 2 if own is None else 3
        with ExitStack() as here:
            idx = self.sb(here, "idx", [P, 2, 2], I32)
            st = self.sb(here, "st", [P, 2, 2, S])
            (mstar, d, ya, yb, den, den2) = self.several(
                here, "node_parts",
                [P, H],
                [P, 2, 3, H],
                [P, C],
                [P, C],
                [P, H],
                [P, 3, H])
            names = ("ready", "begun", "shift_ready", "exp_ready")
            ready, begun, shift_ready, exp_ready = (self.sem(here, n) for n in names)
            got = [self.sem(here, f"got{s}") for s in range(2)]
            block = here.enter_context(nc.Block())

            @block.gpsimd
            def _(pool):
                bound, bound_c = pool.to_reg(P * g.width - 1), pool.to_reg(P - 1)

                def gather(t, i, s):
                    pool.wait_ge(ready, t + 1)
                    pool.sem_inc(begun, 1)
                    for n, (table, last) in enumerate(((self.state_dram[g.name], bound), (self.carry_dram[g.name], bound_c))):
                        pool.indirect_dma_start(out=st[:, s, n, :], out_offset=None, in_=table[:, :],
                                                in_offset=bass.IndirectOffsetOnAxis(ap=idx[:, s, n:n + 1], axis=0),
                                                bounds_check=last, oob_is_err=False).then_inc(got[s], 16)
                in_pairs(pool, NT, gather)

            @block.scalar
            def _(act):
                def step(t, i, s):
                    act.wait_ge(shift_ready, t + 1)
                    act.activation(d[:, s, 0:parts, :], d[:, s, 0:parts, :], ACT.Exp).then_inc(exp_ready, 1)
                in_pairs(act, NT, step)

            @block.vector
            def _(dve):
                def prefill(t, s):
                    dve.memset(st[:, s, :, 0:C + H], 0.0)
                    dve.memset(st[:, s, :, C + H:S], NEG)
                    dve.tensor_copy(idx[:, s, 0:1], self.end_at[g.name][:, bass.ds(t, 1)])
                    dve.tensor_copy(idx[:, s, 1:2], self.carry_at[g.name][:, bass.ds(t, 1)]).then_inc(ready, 1)
                prefill(0, 0)
                prefill(1, 1)

                def head_view(ap):
                    return ap.rearrange("p (h k) -> p h k", k=K)

                def step(t, i, s):
                    at = bass.ds(t, 1)
                    dve.drain()
                    dve.wait_ge(got[s], i * 32 + 32)
                    m0, m1 = st[:, s, 0, C + H:S], st[:, s, 1, C + H:S]
                    dve.tensor_tensor(mstar[:, :], m0, m1, ALU.max)
                    dve.drain()
                    if own is not None:
                        own_m = own[1][:, at, :].rearrange("p a h -> p (a h)")
                        dve.tensor_tensor(mstar[:, :], mstar[:, :], own_m, ALU.max)
                        dve.drain()
                        dve.tensor_tensor(d[:, s, 2, :], own_m, mstar[:, :], ALU.subtract)
                    dve.tensor_tensor(d[:, s, 0, :], m0, mstar[:, :], ALU.subtract)
                    dve.tensor_tensor(d[:, s, 1, :], m1, mstar[:, :], ALU.subtract)
                    dve.drain()
                    dve.sem_inc(shift_ready, 1)
                    dve.wait_ge(exp_ready, t + 1)
                    dve.tensor_tensor(head_view(ya[:, :]), head_view(st[:, s, 0, 0:C]), heads(d[:, s, 0, :], K), ALU.mult)
                    dve.tensor_tensor(head_view(yb[:, :]), head_view(st[:, s, 1, 0:C]), heads(d[:, s, 1, :], K), ALU.mult)
                    dve.tensor_tensor(den2[:, 0, :], st[:, s, 0, C:C + H], d[:, s, 0, :], ALU.mult)
                    dve.tensor_tensor(den2[:, 1, :], st[:, s, 1, C:C + H], d[:, s, 1, :], ALU.mult)
                    dve.drain()
                    dve.tensor_tensor(ya[:, :], ya[:, :], yb[:, :], ALU.add)
                    dve.tensor_tensor(den[:, :], den2[:, 0, :], den2[:, 1, :], ALU.add)
                    dve.drain()
                    if own is not None:
                        own_h = own[0][:, at, :].rearrange("p a c -> p (a c)")
                        dve.tensor_tensor(head_view(yb[:, :]), head_view(own_h), heads(d[:, s, 2, :], K), ALU.mult)
                        dve.tensor_tensor(den[:, :], den[:, :], d[:, s, 2, :], ALU.add)
                        dve.drain()
                        dve.tensor_tensor(ya[:, :], ya[:, :], yb[:, :], ALU.add)
                        dve.tensor_scalar(den[:, :], den[:, :], 1e-16, None, ALU.add)
                    else:
                        dve.tensor_scalar(den[:, :], den[:, :], 1e-16, None, ALU.max)
                    dve.drain()
                    dve.reciprocal(den[:, :], den[:, :])
                    dve.drain()
                    if own is None:
                        dve.tensor_tensor(head_view(ya[:, :]), head_view(ya[:, :]), heads(den[:, :], K), ALU.mult)
                        dve.drain()
                        x = self.X[:, at, :].rearrange("p a d -> p (a d)")
                        dve.tensor_tensor(x, x, ya[:, :], ALU.add)
                    else:
                        dve.tensor_tensor(head_view(agg[:, at, :].rearrange("p a c -> p (a c)")), head_view(ya[:, :]),
                                          heads(den[:, :], K), ALU.mult)
                    if not (isinstance(t, int) and t == NT - 1):
                        prefill(t + 2, s)
                in_pairs(dve, NT, step)

    def project_ffn(self, own_h, own_m, xt_all):
        nc, io = self.nc, self.io
        C = FFN.cols
        ident = self.ident
        with ExitStack() as here:
            mean, rstd = self.norm_stats(here)
            att = self.sb(here, "att", [C, 2 * H])
            w = self.sb(here, "w_ffn", [P, 2, C + 2 * H])
            wt = self.sb(here, "w_turned_sb", [C, 2, P])
            (xn, xt, rows, own) = self.several(
                here, "row_parts",
                [P, 2, D],
                [P, 2, 2, P],
                [P, 2, C + 2 * H],
                [P, NT, H])
            tp, pz, pw = self.ps(here, "tp", [P, 2, 512]), self.ps(here, "pz", [P, 2, 512]), self.ps(here, "pw", [P, 512])
            names = ("att_clear", "w_loaded", "w_turned", "wt_ready", "w_made", "w_ready", "xn_ready", "turned", "xt_ready",
                     "projected", "evac")
            (att_clear, w_loaded, w_turned, wt_ready, w_made, w_ready, xn_ready, turned, xt_ready, projected, evac) = \
                (self.sem(here, n) for n in names)
            stored = [self.sem(here, f"stored{s}") for s in range(2)]
            block = here.enter_context(nc.Block())

            @block.sync
            def _(sp):
                sp.dma_start(w[:, :, 0:C], io["L0_ffn_W_gat"].rearrange("(k p) c -> p k c", p=P)).then_inc(w_loaded, 16)
                sp.wait_ge(att_clear, 1)
                for side, name in enumerate(("L0_ffn_att_src", "L0_ffn_att_dst")):
                    for h in range(H):
                        sp.dma_start(att[h * EXPERTS:(h + 1) * EXPERTS, side * H + h:side * H + h + 1],
                                     io[name][h, :].rearrange("(e a) -> e a", a=1)).then_inc(w_loaded, 16)
                sp.wait_ge(w_loaded, 144)

                def store(t, i, s):
                    sp.wait_ge(evac, t + 1)
                    sp.dma_start(self.row_dram["ffn"][bass.ds(t * P, P), :], rows[:, s, 0:FFN.row]).then_inc(stored[s], 16)
                in_pairs(sp, NT, store)
                for s in range(2):
                    sp.wait_ge(stored[s], 16 * ((NT + 1 - s) // 2))

            @block.tensor
            def _(pe):
                pe.wait_ge(w_loaded, 144)
                for k in range(2):
                    mm = pe.transpose(tp[0:C, k, 0:P], w[:, k, 0:C], ident[:, :])
                mm.then_inc(w_turned, 1)
                pe.wait_ge(wt_ready, 1)
                for k in range(2):
                    mm = pe.matmul(pw[:, k * 2 * H:(k + 1) * 2 * H], wt[:, k, :], att[:, :], start=True, stop=True)
                mm.then_inc(w_made, 1)
                pe.wait_ge(w_ready, 1)

                def step(t, i, s):
                    pe.wait_ge(xn_ready, t + 1)
                    if not first(i):
                        pe.wait_ge(xt_ready, t - 1)
                    for k in range(2):
                        mm = pe.transpose(tp[:, s, k * P:(k + 1) * P], xn[:, s, k * P:(k + 1) * P], ident[:, :])
                    mm.then_inc(turned, 1)
                    pe.wait_ge(xt_ready, t + 1)
                    if not first(i):
                        pe.wait_ge(evac, t - 1)
                    for k in range(2):
                        mm = pe.matmul(pz[:, s, 0:C + 2 * H], xt[:, s, k, :], w[:, k, :], start=(k == 0), stop=(k == 1))
                    mm.then_inc(projected, 1)
                in_pairs(pe, NT, step)

            @block.scalar
            def _(act):
                act.wait_ge(w_turned, 1)
                for k in range(2):
                    ins = act.activation(wt[:, k, :], tp[0:C, k, 0:P], ACT.Copy)
                ins.then_inc(wt_ready, 1)
                act.wait_ge(w_made, 1)
                for k in range(2):
                    ins = act.activation(w[:, k, C:C + 2 * H], pw[:, k * 2 * H:(k + 1) * 2 * H], ACT.Copy)
                ins.then_inc(w_ready, 1)

                def step(t, i, s):
                    act.wait_ge(turned, t + 1)
                    if not first(i):
                        act.wait_ge(projected, t - 1)
                    act.activation(xt[:, s, :, :].rearrange("p k n -> p (k n)"), tp[:, s, 0:D], ACT.Copy).then_inc(xt_ready, 1)
                    act.activation(xt_all[:, :, bass.ds(t * P, P)], tp[:, s, 0:D].rearrange("p (k n) -> p k n", k=2), ACT.Copy)
                    act.wait_ge(projected, t + 1)
                    if not first(i):
                        act.wait_ge(stored[s], i * 16)
                    act.activation(rows[:, s, :], pz[:, s, 0:C + 2 * H], ACT.Copy)
                    flat = "p a h -> p (a h)"
                    act.activation(own_h[:, bass.ds(t, 1), :].rearrange(flat), pz[:, s, 0:C], ACT.Copy)
                    act.activation(own[:, bass.ds(t, 1), :].rearrange(flat), pz[:, s, C:C + H], ACT.Copy)
                    act.activation(self.ed["ffn"][:, bass.ds(t, 1), :].rearrange(flat), pz[:, s, C + H:C + 2 * H], ACT.Copy) \
                       .then_inc(evac, 1)
                in_pairs(act, NT, step)

            @block.vector
            def _(dve):
                dve.memset(att[:, :], 0.0).then_inc(att_clear, 1)

                def step(t, i, s):
                    if not first(i):
                        dve.wait_ge(turned, t - 1)
                    dve.tensor_scalar(xn[:, s, :], self.X[:, bass.ds(t, 1), :].rearrange("p a d -> p (a d)"),
                                      mean[:, bass.ds(t, 1)], rstd[:, bass.ds(t, 1)], ALU.subtract, ALU.mult) \
                       .then_inc(xn_ready, 1)
                in_pairs(dve, NT, step)
                dve.wait_ge(evac, NT)
                dve.tensor_tensor(own[:, :, :], own[:, :, :], self.ed["ffn"][:, :, :], ALU.add)
                dve.drain()
                dve.scalar_tensor_tensor(own_m[:, :, :], own[:, :, :], FFN.slope, own[:, :, :], ALU.mult, ALU.max)

    def route(self, agg, gate):
        nc, io = self.nc, self.io
        C = FFN.cols
        with ExitStack() as here:
            (par, y, sq, mean, var, std, eps, sc, rank, cmp, tops, is_top, ex, ws) = self.several(
                here, "route_parts",
                [P, 3, C],
                [P, NT, C],
                [P, NT, C],
                [P, NT],
                [P, NT],
                [P, NT],
                [P, 1],
                [P, NT, EXPERTS],
                [P, NT, EXPERTS],
                [P, NT, EXPERTS],
                [P, 2, NT],
                [P, 2, NT, EXPERTS],
                [P, NT],
                [P, 2, NT])
            par_in, var_ready, std_ready, diff_ready, ex_ready = \
                (self.sem(here, n) for n in ("par_in", "var_ready", "std_ready", "diff_ready", "ex_ready"))
            block = here.enter_context(nc.Block())

            @block.sync
            def _(sp):
                for n, name in enumerate(("L0_ffn_b_gat", "L0_ffn_ln_gamma", "L0_ffn_ln_beta")):
                    sp.dma_start(par[:, n, :], io[name].partition_broadcast(P)).then_inc(par_in, 16)

            @block.scalar
            def _(act):
                act.wait_ge(var_ready, 1)
                act.activation(std[:, :], var[:, :], ACT.Sqrt, bias=eps[:, 0:1], scale=1.0 / C).then_inc(std_ready, 1)
                act.wait_ge(diff_ready, 1)
                act.activation(ex[:, :], ex[:, :], ACT.Exp).then_inc(ex_ready, 1)

            @block.vector
            def _(dve):
                def op(call, *args):
                    call(*args)
                    dve.drain()

                def over_nodes(ap):
                    return ap.unsqueeze(1).to_broadcast([P, NT, C])

                def over(ap, n):
                    return ap.unsqueeze(2).to_broadcast([P, NT, n])
                dve.memset(eps[:, :], EPS)
                dve.wait_ge(par_in, 48)
                op(dve.tensor_tensor, y[:, :, :], agg[:, 0:NT, :], over_nodes(par[:, 0, :]), ALU.add)
                op(dve.tensor_reduce, mean[:, :], y[:, :, :], AX, ALU.add)
                op(dve.tensor_scalar, mean[:, :], mean[:, :], 1.0 / C, None, ALU.mult)
                op(dve.tensor_tensor, y[:, :, :], y[:, :, :], over(mean[:, :], C), ALU.subtract)
                op(dve.tensor_tensor, sq[:, :, :], y[:, :, :], y[:, :, :], ALU.mult)
                dve.tensor_reduce(var[:, :], sq[:, :, :], AX, ALU.add).then_inc(var_ready, 1)
                dve.wait_ge(std_ready, 1)
                op(dve.reciprocal, std[:, :], std[:, :])
                op(dve.tensor_tensor, y[:, :, :], y[:, :, :], over(std[:, :], C), ALU.mult)
                op(dve.tensor_tensor, y[:, :, :], y[:, :, :], over_nodes(par[:, 1, :]), ALU.mult)
                op(dve.tensor_tensor, y[:, :, :], y[:, :, :], over_nodes(par[:, 2, :]), ALU.add)
                op(dve.tensor_tensor, sc[:, :, :], y[:, :, 0:EXPERTS], y[:, :, EXPERTS:2 * EXPERTS], ALU.add)
                for h in range(2, H):
                    op(dve.tensor_tensor, sc[:, :, :], sc[:, :, :], y[:, :, h * EXPERTS:(h + 1) * EXPERTS], ALU.add)
                op(dve.tensor_scalar, sc[:, :, :], sc[:, :, :], 1.0 / H, None, ALU.mult)
                op(dve.memset, rank[:, :, :], 0.0)
                for a in range(EXPERTS):
                    for lo, hi, rel in ((0, a, ALU.is_gt), (a + 1, EXPERTS, ALU.is_ge)):
                        if lo < hi:
                            op(dve.tensor_tensor, cmp[:, :, lo:hi], over(sc[:, :, a], hi - lo), sc[:, :, lo:hi], rel)
                            op(dve.tensor_tensor, rank[:, :, lo:hi], rank[:, :, lo:hi], cmp[:, :, lo:hi], ALU.add)
                for k in range(2):
                    op(dve.tensor_scalar, is_top[:, k, :, :], rank[:, :, :], float(k), None, ALU.is_equal)
                    op(dve.tensor_tensor, cmp[:, :, :], is_top[:, k, :, :], sc[:, :, :], ALU.mult)
                    op(dve.tensor_reduce, tops[:, k, :], cmp[:, :, :], AX, ALU.add)
                dve.tensor_tensor(ex[:, :], tops[:, 1, :], tops[:, 0, :], ALU.subtract).then_inc(diff_ready, 1)
                dve.wait_ge(ex_ready, 1)
                op(dve.tensor_scalar, ws[:, 0, :], ex[:, :], 1.0, None, ALU.add)
                op(dve.reciprocal, ws[:, 0, :], ws[:, 0, :])
                op(dve.tensor_tensor, ws[:, 1, :], ws[:, 0, :], ex[:, :], ALU.mult)
                op(dve.tensor_tensor, gate[:, :, :], is_top[:, 0, :, :], over(ws[:, 0, :], EXPERTS), ALU.mult)
                op(dve.tensor_tensor, cmp[:, :, :], is_top[:, 1, :, :], over(ws[:, 1, :], EXPERTS), ALU.mult)
                op(dve.tensor_tensor, gate[:, :, :], gate[:, :, :], cmp[:, :, :], ALU.add)

    def experts(self, gate, xt_all, out):
        nc, io = self.nc, self.io
        FT = HIDDEN // P
        B = FFN_BLOCK
        HALF = B * P // 2
        blocks = NT // B
        with ExitStack() as here:
            w1 = self.sb(here, "w1", [P, EXPERTS, 2, HIDDEN])
            w2 = self.sb(here, "w2", [P, EXPERTS, FT, D])
            b1, b2 = self.sb(here, "b1", [P, EXPERTS, FT]), self.sb(here, "b2", [1, EXPERTS, D])
            hid = self.sb(here, "hid", [P, 2, FT, B * P])
            ph, po = self.ps(here, "ph", [P, 4, 512]), self.ps(here, "po", [P, 4, 512])
            names = ("w_loaded", "hid_made", "hid_ready", "out_made", "out_used", "x_stored")
            w_loaded, hid_made, hid_ready, out_made, out_used, x_stored = (self.sem(here, n) for n in names)
            block = here.enter_context(nc.Block())
            EH = FT * 2

            @block.sync
            def _(sp):
                for e in range(EXPERTS):
                    sp.dma_start(w1[:, e, :, :], io["L0_ffn_W1"][e, :, :].rearrange("(k p) f -> p k f", p=P)).then_inc(w_loaded, 16)
                    sp.dma_start(w2[:, e, :, :], io["L0_ffn_W2"][e, :, :].rearrange("(f p) d -> p f d", p=P)).then_inc(w_loaded, 16)
                    sp.dma_start(b2[:, e, :], io["L0_ffn_b2"][e, :].rearrange("(a d) -> a d", a=1)).then_inc(w_loaded, 16)
                    for f in range(FT):
                        sp.dma_start(b1[:, e, f:f + 1], io["L0_ffn_b1"][e, f * P:(f + 1) * P].rearrange("(p a) -> p a", a=1)) \
                          .then_inc(w_loaded, 16)
                for i in range(blocks):
                    sp.wait_ge(out_used, (i + 1) * B * EXPERTS)
                    full = B if i < blocks - 1 else B - 1
                    a = i * B
                    sp.dma_start(out[a * P:(a + full) * P, :].rearrange("(t p) d -> p t d", p=P), self.X[:, a:a + full, :]) \
                      .then_inc(x_stored, 16)
                sp.dma_start(out[(NT - 1) * P:N, :], self.X[0:LAST, NT - 1, :]).then_inc(x_stored, 16)
                sp.wait_ge(x_stored, 16 * (blocks + 1))

            @block.tensor
            def _(pe):
                pe.wait_ge(w_loaded, 16 * EXPERTS * (3 + FT))

                def hidden(i, e, start):
                    for f in range(FT):
                        for half in range(2):
                            n = f * 2 + half
                            if not (start and e == 0 and n < 4):
                                pe.wait_ge(hid_ready, i * (EH * EXPERTS) + (e * EH + n - 3))
                            for k in range(2):
                                mm = pe.matmul(ph[:, n % 4, 0:HALF], w1[:, e, k, f * P:(f + 1) * P],
                                               xt_all[:, k, bass.ds(i * (B * P) + half * HALF, HALF)],
                                               start=(k == 0), stop=(k == 1))
                            mm.then_inc(hid_made, 1)

                def output(i, e, start):
                    pe.wait_ge(hid_ready, i * (EH * EXPERTS) + (e + 1) * EH)
                    for t in range(B):
                        n = e * B + t
                        if not (start and n < 4):
                            pe.wait_ge(out_used, i * (B * EXPERTS) + (n - 3))
                        pe.matmul(po[:, n % 4, 0:D], self.ones[0:1, :], b2[:, e, :], start=True, stop=False)
                        for f in range(FT):
                            mm = pe.matmul(po[:, n % 4, 0:D], hid[:, e % 2, f, t * P:(t + 1) * P], w2[:, e, f, :],
                                           start=False, stop=(f == FT - 1))
                        mm.then_inc(out_made, 1)

                def block_of(i, start):
                    hidden(i, 0, start)
                    for e in range(EXPERTS):
                        if e + 1 < EXPERTS:
                            hidden(i, e + 1, start)
                        output(i, e, start)
                block_of(0, True)
                with pe.Fori(1, blocks) as i:
                    block_of(i, False)

            @block.scalar
            def _(act):
                act.wait_ge(w_loaded, 16 * EXPERTS * (3 + FT))

                def block_of(i, start):
                    for e in range(EXPERTS):
                        if not (start and e < 2):
                            act.wait_ge(out_made, i * (B * EXPERTS) + (e - 1) * B)
                        for f in range(FT):
                            for half in range(2):
                                n = f * 2 + half
                                act.wait_ge(hid_made, i * (EH * EXPERTS) + (e * EH + n + 1))
                                act.activation(hid[:, e % 2, f, half * HALF:(half + 1) * HALF], ph[:, n % 4, 0:HALF],
                                               ACT.Gelu, bias=b1[:, e, f:f + 1]).then_inc(hid_ready, 1)
                block_of(0, True)
                with act.Fori(1, blocks) as i:
                    block_of(i, False)

            @block.vector
            def _(dve):
                def block_of(i):
                    for e in range(EXPERTS):
                        for t in range(B):
                            n = e * B + t
                            dve.wait_ge(out_made, i * (B * EXPERTS) + (n + 1))
                            x = self.X[:, bass.ds(i * B + t, 1), :].rearrange("p a d -> p (a d)")
                            dve.scalar_tensor_tensor(x, po[:, n % 4, 0:D], gate[:, bass.ds(i * B + t, 1), e], x,
                                                     ALU.mult, ALU.add).then_inc(out_used, 1)
                        dve.drain()
                block_of(0)
                with dve.Fori(1, blocks) as i:
                    block_of(i)

    def run(self, out):
        with self.keep, ExitStack() as later:
            self.setup()
            self.part = "segments_gnn"
            self.segments(GNN, self.io["dst"])
            self.part = "segments_ffn"
            self.segments(FFN, self.io["L0_ffn_edge_index"][1, :])
            self.part = "sort"
            self.sort_edges()
            with ExitStack() as mine:
                self.part = "project"
                kmax = self.project(mine)
                self.part = "mix"
                self.mix(kmax)
            self.part = "edges_gnn"
            self.edges(GNN)
            self.part = "nodes_gnn"
            self.gather_nodes(GNN)
            self.part = "ffn"
            xt_all = self.sb(later, "xt_all", [P, 2, NPAD])
            own_h, own_m = self.sb(later, "own_h", [P, NT, FFN.cols]), self.sb(later, "own_m", [P, NT, H])
            agg, gate = self.sb(later, "agg", [P, NT, FFN.cols]), self.sb(later, "gate", [P, NT, EXPERTS])
            self.part = "project_ffn"
            self.project_ffn(own_h, own_m, xt_all)
            self.part = "edges_ffn"
            self.edges(FFN)
            self.part = "nodes_ffn"
            self.gather_nodes(FFN, (own_h, own_m), agg)
            self.part = "route"
            self.route(agg, gate)
            self.part = "experts"
            self.experts(gate, xt_all, out)


_INS = ['x', 'src', 'dst', 'L0_gnn_W', 'L0_gnn_att', 'L0_mix_Wqkv', 'L0_mix_Wout', 'L0_mix_gamma', 'L0_ffn_W_gat',
        'L0_ffn_att_src', 'L0_ffn_att_dst', 'L0_ffn_b_gat', 'L0_ffn_ln_gamma', 'L0_ffn_ln_beta', 'L0_ffn_W1',
        'L0_ffn_b1', 'L0_ffn_W2', 'L0_ffn_b2', 'L0_ffn_edge_index']


def kernel(**inputs):
    import numpy as _np
    import concourse.bacc as _bacc
    from concourse import mybir as _mybir
    from concourse.bass_utils import run_bass_kernel_spmd as _run

    nc = _bacc.Bacc("TRN2", target_bir_lowering=False, num_devices=1)
    arrays, io = {}, {}
    for name in _INS:
        a = _np.ascontiguousarray(inputs[name])
        arrays[f"in_{name}_dram"] = a
        io[name] = nc.dram_tensor(f"in_{name}_dram", a.shape, _mybir.dt.from_np(a.dtype), kind="ExternalInput").ap()
    out = nc.dram_tensor("out_0_dram", (N, D), _mybir.dt.float32, kind="ExternalOutput").ap()
    Kernel(nc, io).run(out)
    r = _run(nc, [arrays], core_ids=[0])
    return r.results[0]["out_0_dram"]
```

```python
from contextlib import ExitStack

import concourse.bass as bass
from concourse import mybir

P = 128
N = 6250
NT = (N + P - 1) // P
NPAD = NT * P
LAST = N - (NT - 1) * P
D = 256
H = 4
EPS = 1e-5
NEG = -1.0e30
NOWHERE = 1 << 20
HIS = 64

MIX_HEADS, MIX_DIM = 8, 32
EXPERTS, HIDDEN = 4, 512
FFN_BLOCK = 7
F32 = mybir.dt.float32
BF16 = mybir.dt.bfloat16
FP16 = mybir.dt.float16
I32 = mybir.dt.int32
ALU = mybir.AluOpType
ACT = mybir.ActivationFunctionType
AX = mybir.AxisListType.X


class Graph:

    def __init__(self, name, edges, width, chunk, cols, slope):
        self.name, self.edges, self.width, self.chunk, self.cols, self.slope = name, edges, width, chunk, cols, slope
        self.per_head = cols // H
        self.chunks = width // chunk
        self.row = cols + H
        self.state = cols + 2 * H
        assert width % chunk == 0 and self.chunks % 2 == 0 and P * width >= edges


GNN = Graph("gnn", 100000, 784, 14, 256, 0.01)
FFN = Graph("ffn", 131072, 1024, 16, 16, 0.2)
SORT_BLOCKS = P
SORT_TILES = FFN.width // P
PUT_TILES = 2


def first(i):
    return isinstance(i, int) and i == 0


def in_pairs(eng, count, step):
    for s in range(2):
        step(s, 0, s)
    with eng.Fori(1, count // 2) as i:
        for s in range(2):
            step(i * 2 + s, i, s)
    if count % 2:
        step(count - 1, count // 2, 0)


def tile_rows(t):
    return LAST if isinstance(t, int) and t == NT - 1 else P


def heads(ap, per_head):
    return ap.unsqueeze(2).to_broadcast([P, H, per_head])


class Kernel:
    def __init__(self, nc, io):
        self.nc, self.io = nc, io
        self.keep = ExitStack()
        self.scratch, self.sems = {}, {}
        self.part = "all"

    def sb(self, stack, name, shape, dt=F32):
        return stack.enter_context(self.nc.sbuf_tensor(f"{self.part}_{name}", list(shape), dt))

    def several(self, stack, name, *shapes):
        sizes = [1] * len(shapes)
        for n, shape in enumerate(shapes):
            for d in shape[1:]:
                sizes[n] *= d
        whole, at, views = self.sb(stack, name, [P, sum(sizes)]), 0, []
        for shape, size in zip(shapes, sizes):
            view = whole[0:shape[0], at:at + size]
            if len(shape) == 3:
                view = view.rearrange("p (a b) -> p a b", b=shape[2])
            elif len(shape) == 4:
                view = view.rearrange("p (a b c) -> p a b c", b=shape[2], c=shape[3])
            views.append(view)
            at += size
        return views

    def ps(self, stack, name, shape, dt=F32):
        return stack.enter_context(self.nc.psum_tensor(f"{self.part}_{name}", list(shape), dt))

    def sem(self, stack, name):
        sem = self.nc.alloc_semaphore(f"{self.part}_{name}")
        if stack not in self.sems:
            self.sems[stack] = []
            stack.callback(self.clear_sems, stack)
        self.sems[stack].append(sem)
        return sem

    def clear_sems(self, stack):
        self.nc.clear_and_free_semaphores(self.sems.pop(stack))
        self.nc.all_engine_barrier()

    def dram(self, name, shape, dt=F32):
        t = self.nc.dram_tensor(name, list(shape), dt, kind="Internal").ap()
        self.scratch[name] = t
        return t

    def setup(self):
        nc, io, keep = self.nc, self.io, self.keep
        self.ident = self.sb(keep, "ident", [P, P])
        self.ones = self.sb(keep, "ones", [P, P])
        self.below = self.sb(keep, "below", [P, P])
        self.ed = {g.name: self.sb(keep, f"ed_{g.name}", [P, NT, H]) for g in (GNN, FFN)}
        self.seg_at = {g.name: self.sb(keep, f"seg_at_{g.name}", [P, NT + 1], I32) for g in (GNN, FFN)}
        self.end_at = {g.name: self.sb(keep, f"end_at_{g.name}", [P, NT + 1], I32) for g in (GNN, FFN)}
        self.carry_at = {g.name: self.sb(keep, f"carry_at_{g.name}", [P, NT + 1], I32) for g in (GNN, FFN)}
        self.base_ffn = self.sb(keep, "base_ffn", [P, HIS])
        self.edge_src = {g.name: self.sb(keep, f"src_{g.name}", [P, g.width + 2 * g.chunk], I32)
                         for g in (GNN, FFN)}
        self.row_dram = {"gnn": self.dram("gnn_rows", [NPAD, GNN.row]), "ffn": self.dram("ffn_rows", [NPAD, FFN.row])}
        self.qkv_dram = self.dram("qkv", [NPAD, 3 * D])
        self.seg_dram = {g.name: self.dram(f"seg_{g.name}", [P * g.width, 1 + H]) for g in (GNN, FFN)}
        self.state_dram = {g.name: self.dram(f"state_{g.name}", [P * g.width, g.state]) for g in (GNN, FFN)}
        self.carry_dram = {g.name: self.dram(f"carry_{g.name}", [P, g.state]) for g in (GNN, FFN)}
        self.lo_dram = self.dram("dst_lo", [P, FFN.width], I32)
        self.sorted_dram = self.dram("sorted_src", [P * FFN.width, 1], I32)
        self.kmax = self.sb(keep, "kmax", [P, D])
        ident, ones, below = self.ident, self.ones, self.below

        with ExitStack() as here:
            block = here.enter_context(nc.Block())

            @block.gpsimd
            def _(pool):
                pool.memset(ident[:, :], 0.0)
                pool.memset(ones[:, :], 1.0)
                pool.drain()
                pool.affine_select(out=ident[:, :], in_=ident[:, :], compare_op=ALU.not_equal, fill=1.0,
                                   base=0, pattern=[[-1, P]], channel_multiplier=1)
                pool.affine_select(out=below[:, :], in_=ones[:, :], compare_op=ALU.is_gt, fill=0.0,
                                   base=0, pattern=[[1, P]], channel_multiplier=-1)

            @block.vector
            def _(dve):
                for g in (GNN, FFN):
                    dve.memset(self.edge_src[g.name][:, :], 0)
                    dve.memset(self.end_at[g.name][:, NT:NT + 1], NOWHERE)
                    dve.memset(self.carry_at[g.name][:, NT:NT + 1], NOWHERE)

    def load_x(self, stack):
        nc, x = self.nc, self.io["x"]
        self.X = self.sb(stack, "X", [P, NT, D])
        X = self.X
        with ExitStack() as here:
            cleared, loaded = self.sem(here, "cleared"), self.sem(here, "loaded")
            block = here.enter_context(nc.Block())

            @block.vector
            def _(dve):
                dve.memset(X[:, NT - 1, :], 0.0).then_inc(cleared, 1)

            @block.sync
            def _(sp):
                sp.dma_start(X[:, 0:NT - 1, :], x[0:(NT - 1) * P, :].rearrange("(t p) d -> p t d", p=P)).then_inc(loaded, 16)
                sp.wait_ge(cleared, 1)
                sp.dma_start(X[0:LAST, NT - 1, :], x[(NT - 1) * P:N, :]).then_inc(loaded, 16)
                sp.wait_ge(loaded, 32)

    def segments(self, g, dst):
        nc = self.nc
        W = g.width
        U = 16
        groups = W // U
        with ExitStack() as here:
            dst_i = self.sb(here, "dst_i", [P, W], I32)
            part_i = self.sb(here, "part_i", [P, W], I32)
            lo, hi = self.sb(here, "lo", [P, W], BF16), self.sb(here, "hi", [P, W], BF16)
            iota_i = self.sb(here, "iota_i", [P, P], I32)
            iota = self.sb(here, "iota", [P, P], BF16)
            oh_lo, oh_hi = self.sb(here, "oh_lo", [P, 2, U, P], BF16), self.sb(here, "oh_hi", [P, 2, U, HIS], BF16)
            (cnt, tot, run, base, nz, end, t1, t2, q1, q2) = self.several(
                here, "nodes_small",
                [P, HIS],
                [P, HIS],
                [P, HIS],
                [P, NT],
                [P, NT],
                [P, NT],
                [P, NT],
                [P, NT],
                [P, NT],
                [P, NT])
            qi = self.sb(here, "qi", [P, NT], I32)
            hist = self.ps(here, "hist", [P, HIS])
            pre, total = self.ps(here, "pre", [P, HIS]), self.ps(here, "total", [P, HIS])
            padded, loaded, iota_made = self.sem(here, "padded"), self.sem(here, "dst_loaded"), self.sem(here, "iota_made")
            hot, counted = self.sem(here, "hot"), self.sem(here, "counted")
            cnt_ready, prefixed = self.sem(here, "cnt_ready"), self.sem(here, "prefixed")
            lo_ready, lo_stored = self.sem(here, "lo_ready"), self.sem(here, "lo_stored")
            block = here.enter_context(nc.Block())

            @block.sync
            def _(sp):
                full = g.edges // W
                if g.edges == P * W:
                    sp.dma_start(dst_i[:, :], dst.rearrange("(p w) -> p w", w=W)).then_inc(loaded, 16)
                    sp.wait_ge(loaded, 16)
                else:
                    sp.dma_start(self.edge_src[g.name][0:full, 0:W],
                                 self.io["src"][0:full * W].rearrange("(p w) -> p w", w=W)).then_inc(loaded, 16)
                    sp.dma_start(self.edge_src[g.name][full:full + 1, 0:g.edges - full * W],
                                 self.io["src"][full * W:g.edges].rearrange("(p w) -> p w", p=1)).then_inc(loaded, 16)
                    sp.wait_ge(padded, 1)
                    sp.dma_start(dst_i[0:full, :], dst[0:full * W].rearrange("(p w) -> p w", w=W)).then_inc(loaded, 16)
                    sp.dma_start(dst_i[full:full + 1, 0:g.edges - full * W],
                                 dst[full * W:g.edges].rearrange("(p w) -> p w", p=1)).then_inc(loaded, 16)
                    sp.wait_ge(loaded, 64)
                if g is FFN:
                    sp.wait_ge(lo_ready, 1)
                    sp.dma_start(self.lo_dram[:, :], part_i[:, :]).then_inc(lo_stored, 16)
                    sp.wait_ge(lo_stored, 16)

            @block.gpsimd
            def _(pool):
                pool.iota(iota_i[:, :], pattern=[[1, P]], base=0, channel_multiplier=0)
                pool.drain()
                pool.tensor_copy(iota[:, :], iota_i[:, :]).then_inc(iota_made, 1)

            @block.tensor
            def _(pe):
                def step(n, i, s):
                    pe.wait_ge(hot, n + 1)
                    for u in range(U):
                        mm = pe.matmul(hist[:, :], oh_lo[:, s, u, :], oh_hi[:, s, u, :],
                                       start=(first(n) and u == 0), stop=False, skip_group_check=True)
                    mm.then_inc(counted, 1)
                in_pairs(pe, groups, step)
                pe.wait_ge(cnt_ready, 1)
                pe.matmul(pre[:, :], self.below[:, :], cnt[:, :], start=True, stop=True)
                pe.matmul(total[:, :], self.ones[:, :], cnt[:, :], start=True, stop=True).then_inc(prefixed, 1)

            @block.vector
            def _(dve):
                if g.edges != P * W:
                    dve.memset(dst_i[:, :], HIS * P - 1).then_inc(padded, 1)
                dve.wait_ge(loaded, 16 if g.edges == P * W else 64)
                dve.tensor_scalar(part_i[:, :], dst_i[:, :], 7, None, ALU.logical_shift_right)
                dve.drain()
                dve.tensor_copy(hi[:, :], part_i[:, :])
                dve.drain()
                dve.tensor_scalar(part_i[:, :], dst_i[:, :], P - 1, None, ALU.bitwise_and).then_inc(lo_ready, 1)
                dve.drain()
                dve.tensor_copy(lo[:, :], part_i[:, :])
                dve.drain()
                dve.wait_ge(iota_made, 1)

                def step(n, i, s):
                    if not first(i):
                        dve.wait_ge(counted, n - 1)
                    for out, part, size in ((oh_lo, lo, P), (oh_hi, hi, HIS)):
                        ins = dve.tensor_tensor(out[:, s, :, :], iota[:, 0:size].unsqueeze(1).to_broadcast([P, U, size]),
                                                part[:, bass.ds(n * U, U)].unsqueeze(2).to_broadcast([P, U, size]),
                                                ALU.is_equal)
                    ins.then_inc(hot, 1)
                in_pairs(dve, groups, step)
                dve.wait_ge(counted, groups)
                dve.tensor_copy(cnt[:, :], hist[:, :]).then_inc(cnt_ready, 1)
                dve.wait_ge(prefixed, 1)
                dve.tensor_copy(tot[:, :], total[:, :])
                dve.drain()
                dve.tensor_tensor_scan(run[:, :], self.ones[:, 0:HIS], tot[:, :], 0.0, ALU.mult, ALU.add)
                dve.drain()
                dve.tensor_tensor(run[:, :], run[:, :], tot[:, :], ALU.subtract)
                dve.drain()
                dve.tensor_tensor(run[:, :], run[:, :], pre[:, :], ALU.add)
                dve.drain()
                if g is FFN:
                    dve.tensor_copy(self.base_ffn[:, :], run[:, :])
                dve.tensor_copy(base[:, :], run[:, 0:NT])
                dve.tensor_scalar(nz[:, :], cnt[:, 0:NT], 1.0, None, ALU.min)
                dve.tensor_tensor(end[:, :], run[:, 0:NT], cnt[:, 0:NT], ALU.add)
                dve.drain()
                dve.tensor_scalar(end[:, :], end[:, :], -1.0, 0.0, ALU.add, ALU.max)
                dve.drain()

                def row_of(q, x):
                    dve.tensor_scalar(t1[:, :], x[:, :], 1.0 / W, None, ALU.mult)
                    dve.drain()
                    dve.tensor_copy(qi[:, :], t1[:, :])
                    dve.drain()
                    dve.tensor_copy(q[:, :], qi[:, :])
                    dve.drain()
                    dve.scalar_tensor_tensor(t1[:, :], q[:, :], -float(W), x[:, :], ALU.mult, ALU.add)
                    dve.drain()
                    dve.tensor_scalar(t2[:, :], t1[:, :], 0.0, None, ALU.is_lt)
                    dve.tensor_scalar(t1[:, :], t1[:, :], float(W), None, ALU.is_ge)
                    dve.drain()
                    dve.tensor_tensor(t1[:, :], t1[:, :], t2[:, :], ALU.subtract)
                    dve.drain()
                    dve.tensor_tensor(q[:, :], q[:, :], t1[:, :], ALU.add)
                    dve.drain()

                def index(out, value, valid):
                    dve.tensor_tensor(t1[:, :], value[:, :], valid[:, :], ALU.mult)
                    dve.tensor_scalar(t2[:, :], valid[:, :], -float(NOWHERE), float(NOWHERE), ALU.mult, ALU.add)
                    dve.drain()
                    dve.tensor_tensor(t1[:, :], t1[:, :], t2[:, :], ALU.add)
                    dve.drain()
                    dve.tensor_copy(out[:, 0:NT], t1[:, :])
                    dve.drain()

                row_of(q1, base)
                row_of(q2, end)
                index(self.seg_at[g.name], base, nz)
                index(self.end_at[g.name], end, nz)
                dve.tensor_tensor(q1[:, :], q2[:, :], q1[:, :], ALU.is_gt)
                dve.drain()
                dve.tensor_tensor(nz[:, :], nz[:, :], q1[:, :], ALU.mult)
                dve.drain()
                index(self.carry_at[g.name], q2, nz)

    def norm_stats(self, stack):
        nc = self.nc
        mean = self.sb(stack, "mean", [P, NT])
        rstd = self.sb(stack, "rstd", [P, NT])
        with ExitStack() as here:
            (mv, st, mv7, eps, std) = self.several(
                here, "stat_parts",
                [P, NT, 2],
                [P, 7, 6],
                [P, 7, 2],
                [P, 1],
                [P, NT])
            stats_done, root_done = self.sem(here, "stats_done"), self.sem(here, "root_done")
            block = here.enter_context(nc.Block())

            @block.vector
            def _(dve):
                dve.memset(eps[:, :], EPS)
                with dve.Fori(0, NT // 7) as i:
                    for u in range(7):
                        dve.bn_stats(st[:, u, :], self.X[:, bass.ds(i * 7 + u, 1), :].rearrange("p a d -> p (a d)"))
                    dve.drain()
                    for u in range(7):
                        dve.bn_aggr(mv7[:, u, :], st[:, u, :])
                    dve.drain()
                    dve.tensor_copy(mv[:, bass.ds(i * 7, 7), :], mv7[:, :, :])
                    dve.drain()
                dve.tensor_copy(mean[:, :], mv[:, :, 0]).then_inc(stats_done, 1)
                dve.wait_ge(root_done, 1)
                dve.reciprocal(rstd[:, :], std[:, :])

            @block.scalar
            def _(act):
                act.wait_ge(stats_done, 1)
                act.activation(std[:, :], mv[:, :, 1], ACT.Sqrt, bias=eps[:, 0:1]).then_inc(root_done, 1)
        return mean, rstd

    def project(self):
        nc, io = self.nc, self.io
        ident, ones = self.ident, self.ones
        kmax = self.kmax
        with ExitStack() as here:
            mean, rstd = self.norm_stats(here)
            w_rows = self.sb(here, "w_rows", [P, 2, D])
            att = self.sb(here, "att", [P, 2, 2 * H])
            wz = self.sb(here, "wz", [P, 2, D + 2 * H])
            wqkv = self.sb(here, "wqkv", [P, 2, 3 * D])
            (xn, xt) = self.several(
                here, "turned_rows",
                [P, 2, D],
                [P, 2, 2, P])
            (z_row, qkv, km) = self.several(
                here, "kmax_parts",
                [P, 2, D + 2 * H],
                [P, 2, 3 * D],
                [P, D])
            kcol = self.sb(here, "kcol", [P, 2])
            kdiag = self.sb(here, "kdiag", [P, 2, P])
            tp = self.ps(here, "tp", [P, 2, 512])
            pz, pqk = self.ps(here, "pz", [P, 2, 512]), self.ps(here, "pqk", [P, 2, 512])
            pv = self.ps(here, "pv", [P, 2, 512])
            names = ("att_clear", "w_loaded", "w_turned", "w_ready", "xn_ready", "turned", "xt_ready", "projected",
                     "z_evac", "qk_evac", "km_ready", "k_turned", "k_diag", "k_spread")
            (att_clear, w_loaded, w_turned, w_ready, xn_ready, turned, xt_ready, projected,
             z_evac, qk_evac, km_ready, k_turned, k_diag, k_spread) = (self.sem(here, n) for n in names)
            z_out = [self.sem(here, f"z_out{s}") for s in range(2)]
            qkv_out = [self.sem(here, f"qkv_out{s}") for s in range(2)]
            block = here.enter_context(nc.Block())

            @block.sync
            def _(sp):
                sp.dma_start(w_rows[:, :, :], io["L0_gnn_W"].rearrange("h o i -> (h o) i").rearrange("(k p) i -> p k i", p=P)) \
                  .then_inc(w_loaded, 16)
                sp.dma_start(wqkv[:, :, :], io["L0_mix_Wqkv"].rearrange("(k p) c -> p k c", p=P)).then_inc(w_loaded, 16)
                sp.wait_ge(att_clear, 1)
                for h in range(H):
                    rows = slice(64 * (h % 2), 64 * (h % 2) + 64)
                    for side in range(2):
                        sp.dma_start(att[rows, h // 2, side * H + h:side * H + h + 1],
                                     io["L0_gnn_att"][h, 64 * side:64 * side + 64].rearrange("(o a) -> o a", a=1)) \
                          .then_inc(w_loaded, 16)
                sp.wait_ge(w_loaded, 160)

                def store(t, i, s):
                    sp.wait_ge(z_evac, t + 1)
                    sp.dma_start(self.row_dram["gnn"][bass.ds(t * P, P), :], z_row[:, s, 0:GNN.row]).then_inc(z_out[s], 16)
                    sp.wait_ge(qk_evac, t + 1)
                    sp.dma_start(self.qkv_dram[bass.ds(t * P, P), :], qkv[:, s, :]).then_inc(qkv_out[s], 16)
                in_pairs(sp, NT, store)
                for s in range(2):
                    sp.wait_ge(z_out[s], 16 * ((NT + 1 - s) // 2))
                    sp.wait_ge(qkv_out[s], 16 * ((NT + 1 - s) // 2))

            @block.tensor
            def _(pe):
                pe.wait_ge(w_loaded, 160)
                for k in range(2):
                    for r in range(2):
                        pe.transpose(pz[:, k, r * P:(r + 1) * P], w_rows[:, r, k * P:(k + 1) * P], ident[:, :])
                for k in range(2):
                    for r in range(2):
                        mm = pe.matmul(pqk[:, k, 0:2 * H], w_rows[:, r, k * P:(k + 1) * P], att[:, r, :],
                                       start=(r == 0), stop=(r == 1))
                mm.then_inc(w_turned, 1)
                pe.wait_ge(w_ready, 1)

                def step(t, i, s):
                    pe.wait_ge(xn_ready, t + 1)
                    if not first(i):
                        pe.wait_ge(xt_ready, t - 1)
                    for k in range(2):
                        mm = pe.transpose(tp[:, s, k * P:(k + 1) * P], xn[:, s, k * P:(k + 1) * P], ident[:, :])
                    mm.then_inc(turned, 1)
                    pe.wait_ge(xt_ready, t + 1)
                    if not first(i):
                        pe.wait_ge(z_evac, t - 1)
                        pe.wait_ge(qk_evac, t - 1)
                    for k in range(2):
                        pe.matmul(pz[:, s, 0:D + 2 * H], xt[:, s, k, :], wz[:, k, :], start=(k == 0), stop=(k == 1))
                    for k in range(2):
                        pe.matmul(pqk[:, s, :], xt[:, s, k, :], wqkv[:, k, 0:2 * D], start=(k == 0), stop=(k == 1))
                    for k in range(2):
                        mm = pe.matmul(pv[:, s, 0:D], xt[:, s, k, :], wqkv[:, k, 2 * D:3 * D], start=(k == 0), stop=(k == 1))
                    mm.then_inc(projected, 1)
                in_pairs(pe, NT, step)
                pe.wait_ge(km_ready, 1)
                for k in range(2):
                    mm = pe.transpose(tp[:, k, 0:P], km[:, k * P:(k + 1) * P], ident[:, :])
                mm.then_inc(k_turned, 1)
                pe.wait_ge(k_diag, 1)
                pe.wait_ge(z_evac, NT)
                for k in range(2):
                    mm = pe.matmul(pz[:, 0, k * P:(k + 1) * P], ones[:, :], kdiag[:, k, :], start=True, stop=True)
                mm.then_inc(k_spread, 1)

            @block.scalar
            def _(act):
                act.wait_ge(w_turned, 1)
                for k in range(2):
                    act.activation(wz[:, k, 0:D], pz[:, k, 0:D], ACT.Copy)
                    ins = act.activation(wz[:, k, D:D + 2 * H], pqk[:, k, 0:2 * H], ACT.Copy)
                ins.then_inc(w_ready, 1)

                def step(t, i, s):
                    act.wait_ge(turned, t + 1)
                    if not first(i):
                        act.wait_ge(projected, t - 1)
                    act.activation(xt[:, s, :, :].rearrange("p k n -> p (k n)"), tp[:, s, 0:D], ACT.Copy).then_inc(xt_ready, 1)
                    act.wait_ge(projected, t + 1)
                    if not first(i):
                        act.wait_ge(z_out[s], i * 16)
                        act.wait_ge(qkv_out[s], i * 16)
                    act.activation(z_row[:, s, :], pz[:, s, 0:D + 2 * H], ACT.Copy)
                    act.activation(self.ed["gnn"][:, bass.ds(t, 1), :].rearrange("p a h -> p (a h)"),
                                   pz[:, s, D + H:D + 2 * H], ACT.Copy)
                    act.activation(qkv[:, s, 2 * D:3 * D], pv[:, s, 0:D], ACT.Copy).then_inc(z_evac, 1)
                in_pairs(act, NT, step)

            @block.vector
            def _(dve):
                dve.memset(att[:, :, :], 0.0).then_inc(att_clear, 1)
                dve.memset(km[:, :], NEG)

                def step(t, i, s):
                    if not first(i):
                        dve.wait_ge(turned, t - 1)
                    dve.tensor_scalar(xn[:, s, :], self.X[:, bass.ds(t, 1), :].rearrange("p a d -> p (a d)"),
                                      mean[:, bass.ds(t, 1)], rstd[:, bass.ds(t, 1)], ALU.subtract, ALU.mult) \
                       .then_inc(xn_ready, 1)
                    dve.drain()
                    dve.wait_ge(projected, t + 1)
                    if not first(i):
                        dve.wait_ge(qkv_out[s], i * 16)
                    rows = tile_rows(t)
                    dve.tensor_tensor(km[0:rows, :], km[0:rows, :], pqk[0:rows, s, D:2 * D], ALU.max)
                    dve.tensor_copy(qkv[:, s, 0:2 * D], pqk[:, s, :]).then_inc(qk_evac, 1)
                in_pairs(dve, NT, step)
                dve.drain()
                dve.sem_inc(km_ready, 1)
                dve.wait_ge(k_turned, 1)
                dve.tensor_reduce(kcol[:, :], tp[:, :, 0:P], AX, ALU.max)
                dve.drain()
                for k in range(2):
                    ins = dve.tensor_scalar(kdiag[:, k, :], ident[:, :], kcol[:, k:k + 1], None, ALU.mult)
                ins.then_inc(k_diag, 1)
                dve.wait_ge(k_spread, 1)
                dve.tensor_copy(kmax[:, :], pz[:, 0, 0:D])

    def mix(self):
        nc, io = self.nc, self.io
        ident, ones, kmax = self.ident, self.ones, self.kmax
        SCALE = MIX_DIM ** -0.5
        with ExitStack() as here:
            (kv, ke, wout, gamma, bmask, ctx, rden, cw, q, qe, qt, mx, sm, st, mv, mv1, std, eps) = self.several(
                here, "mix_parts",
                [P, 2, 2 * D],
                [P, 2, D],
                [P, 2, D],
                [P, D],
                [P, P],
                [P, 2, P],
                [P, 2],
                [P, 2, D],
                [P, 2, D],
                [P, 2, D],
                [P, 2, D],
                [P, 2, MIX_HEADS],
                [P, 2, MIX_HEADS],
                [P, 6],
                [P, NT, 2],
                [P, 2],
                [P, NT],
                [P, 1])
            out = self.sb(here, "mix_out", [P, NT, D])
            pc = [self.ps(here, f"pc{j}", [P, 512]) for j in range(2)]
            pd = [self.ps(here, f"pd{j}", [P, 512]) for j in range(2)]
            pt, pm = self.ps(here, "pt", [P, 2, 512]), self.ps(here, "pm", [P, 2, 512])
            names = ("w_loaded", "shifted", "k_exp", "summed", "ctx_ready", "cw_made", "cw_ready", "q_shifted", "q_exp",
                     "q_ready", "q_turned", "qt_ready", "mixed", "mix_evac", "var_ready", "std_ready")
            (w_loaded, shifted, k_exp, summed, ctx_ready, cw_made, cw_ready, q_shifted, q_exp,
             q_ready, q_turned, qt_ready, mixed, mix_evac, var_ready, std_ready) = (self.sem(here, n) for n in names)
            kv_in = [self.sem(here, f"kv_in{s}") for s in range(2)]
            q_in = [self.sem(here, f"q_in{s}") for s in range(2)]
            block = here.enter_context(nc.Block())

            @block.sync
            def _(sp):
                sp.dma_start(wout[:, :, :], io["L0_mix_Wout"].rearrange("(k p) c -> p k c", p=P)).then_inc(w_loaded, 16)
                sp.dma_start(gamma[:, :], io["L0_mix_gamma"].partition_broadcast(P)).then_inc(w_loaded, 16)

                def load_kv(t, i, s):
                    if not first(i):
                        sp.wait_ge(summed, t - 1)
                    sp.dma_start(kv[:, s, :], self.qkv_dram[bass.ds(t * P, P), D:3 * D]).then_inc(kv_in[s], 16)
                in_pairs(sp, NT, load_kv)

                def load_q(t, i, s):
                    if not first(i):
                        sp.wait_ge(q_shifted, t - 1)
                    sp.dma_start(q[:, s, :], self.qkv_dram[bass.ds(t * P, P), 0:D]).then_inc(q_in[s], 16)
                in_pairs(sp, NT, load_q)

            @block.tensor
            def _(pe):
                def context(t, i, s):
                    rows = tile_rows(t)
                    pe.wait_ge(k_exp, t + 1)
                    head, tail = first(i) and s == 0, isinstance(t, int) and t == NT - 1
                    for j in range(2):
                        cols = slice(j * P, (j + 1) * P)
                        pe.matmul(pc[j][:, 0:P], kv[0:rows, s, D + j * P:D + (j + 1) * P], ke[0:rows, s, cols],
                                  start=head, stop=tail, skip_group_check=True)
                        mm = pe.matmul(pd[j][:, 0:1], ke[0:rows, s, cols], ones[0:rows, 0:1], start=head, stop=tail,
                                       skip_group_check=True)
                    mm.then_inc(summed, 1)
                in_pairs(pe, NT, context)
                pe.wait_ge(w_loaded, 32)
                pe.wait_ge(ctx_ready, 1)
                for j in range(2):
                    mm = pe.matmul(pm[:, j, 0:D], ctx[:, j, :], wout[:, j, :], start=True, stop=True)
                mm.then_inc(cw_made, 1)
                pe.wait_ge(cw_ready, 1)

                def rows_out(t, i, s):
                    pe.wait_ge(q_ready, t + 1)
                    if not first(i):
                        pe.wait_ge(qt_ready, t - 1)
                    for j in range(2):
                        mm = pe.transpose(pt[:, s, j * P:(j + 1) * P], qe[:, s, j * P:(j + 1) * P], ident[:, :])
                    mm.then_inc(q_turned, 1)
                    pe.wait_ge(qt_ready, t + 1)
                    if not first(i):
                        pe.wait_ge(mix_evac, t - 1)
                    for j in range(2):
                        mm = pe.matmul(pm[:, s, 0:D], qt[:, s, j * P:(j + 1) * P], cw[:, j, :], start=(j == 0), stop=(j == 1))
                    mm.then_inc(mixed, 1)
                in_pairs(pe, NT, rows_out)

            @block.scalar
            def _(act):
                def exp_k(t, i, s):
                    act.wait_ge(shifted, t + 1)
                    act.activation(ke[:, s, :], ke[:, s, :], ACT.Exp).then_inc(k_exp, 1)
                in_pairs(act, NT, exp_k)

                def step(t, i, s):
                    act.wait_ge(q_shifted, t + 1)
                    act.activation(qe[:, s, :], qe[:, s, :], ACT.Exp).then_inc(q_exp, 1)
                    act.wait_ge(q_turned, t + 1)
                    if not first(i):
                        act.wait_ge(mixed, t - 1)
                    act.activation(qt[:, s, :], pt[:, s, 0:D], ACT.Copy).then_inc(qt_ready, 1)
                in_pairs(act, NT, step)
                act.wait_ge(var_ready, 1)
                act.activation(std[:, :], mv[:, :, 1], ACT.Sqrt, bias=eps[:, 0:1]).then_inc(std_ready, 1)

            @block.vector
            def _(dve):
                dve.memset(eps[:, :], EPS)
                dve.memset(bmask[:, :], 0.0)
                dve.drain()
                for a in range(P // MIX_DIM):
                    b = slice(a * MIX_DIM, (a + 1) * MIX_DIM)
                    dve.memset(bmask[b, b], 1.0)

                def shift_k(t, i, s):
                    dve.wait_ge(kv_in[s], i * 16 + 16)
                    if not first(i):
                        dve.wait_ge(summed, t - 1)
                    dve.tensor_tensor(ke[:, s, :], kv[:, s, 0:D], kmax[:, :], ALU.subtract).then_inc(shifted, 1)
                in_pairs(dve, NT, shift_k)
                dve.wait_ge(summed, NT)
                for j in range(2):
                    dve.tensor_tensor(ctx[:, j, :], pc[j][:, 0:P], bmask[:, :], ALU.mult)
                    ins = dve.reciprocal(rden[:, j:j + 1], pd[j][:, 0:1])
                ins.then_inc(ctx_ready, 1)
                dve.drain()
                dve.wait_ge(cw_made, 1)
                for j in range(2):
                    ins = dve.tensor_scalar(cw[:, j, :], pm[:, j, 0:D], rden[:, j:j + 1], SCALE, ALU.mult, ALU.mult)
                ins.then_inc(cw_ready, 1)
                dve.wait_ge(w_loaded, 32)

                def by_head(ap):
                    return ap.rearrange("p (h d) -> p h d", d=MIX_DIM)

                def each(ap):
                    return ap.unsqueeze(2).to_broadcast([P, MIX_HEADS, MIX_DIM])

                def step(t, i, s):
                    dve.wait_ge(q_in[s], i * 16 + 16)
                    if not first(i):
                        dve.wait_ge(q_turned, t - 1)
                    dve.tensor_reduce(mx[:, s, :], by_head(q[:, s, :]), AX, ALU.max)
                    dve.drain()
                    dve.tensor_tensor(by_head(qe[:, s, :]), by_head(q[:, s, :]), each(mx[:, s, :]), ALU.subtract) \
                       .then_inc(q_shifted, 1)
                    dve.wait_ge(q_exp, t + 1)
                    dve.tensor_reduce(sm[:, s, :], by_head(qe[:, s, :]), AX, ALU.add)
                    dve.drain()
                    dve.reciprocal(sm[:, s, :], sm[:, s, :])
                    dve.drain()
                    dve.tensor_tensor(by_head(qe[:, s, :]), by_head(qe[:, s, :]), each(sm[:, s, :]), ALU.mult) \
                       .then_inc(q_ready, 1)
                    dve.wait_ge(mixed, t + 1)
                    dve.bn_stats(st[:, :], pm[:, s, 0:D])
                    dve.tensor_copy(row(out, t), pm[:, s, 0:D]).then_inc(mix_evac, 1)
                    dve.drain()
                    dve.bn_aggr(mv1[:, :], st[:, :])
                    dve.drain()
                    dve.tensor_copy(row(mv, t), mv1[:, :])
                    dve.drain()

                def row(tensor, t):
                    return tensor[:, bass.ds(t, 1), :].rearrange("p a d -> p (a d)")
                in_pairs(dve, NT, step)
                dve.sem_inc(var_ready, 1)
                dve.wait_ge(std_ready, 1)
                dve.reciprocal(std[:, :], std[:, :])
                dve.drain()
                with dve.Fori(0, NT // 7) as i:
                    for u in range(7):
                        t = i * 7 + u
                        dve.tensor_scalar(row(out, t), row(out, t), mv[:, bass.ds(t, 1), 0], std[:, bass.ds(t, 1)],
                                          ALU.subtract, ALU.mult)
                    dve.drain()
                    block7 = out[:, bass.ds(i * 7, 7), :]
                    dve.tensor_tensor(block7, block7, gamma[:, :].unsqueeze(1).to_broadcast([P, 7, D]), ALU.mult)
                    dve.drain()
                    x7 = self.X[:, bass.ds(i * 7, 7), :]
                    dve.tensor_tensor(x7, x7, block7, ALU.add)

    def sort_columns(self, stack):
        nc, io = self.nc, self.io
        W, T = FFN.width, SORT_TILES
        ident = self.ident
        dst, src = io["L0_ffn_edge_index"][1, :], io["L0_ffn_edge_index"][0, :]
        flat = "p a b -> p (a b)"
        self.dcol, self.src_lo, self.src_hi = self.several(stack, "columns", [P, T, P], [P, T, P], [P, T, P])
        self.lo, self.hi = self.sb(stack, "lo", [P, T, P], BF16), self.sb(stack, "hi", [P, T, P], BF16)
        dcol, src_lo, src_hi, lo, hi = self.dcol, self.src_lo, self.src_hi, self.lo, self.hi
        with ExitStack() as here:
            raw, rawf = self.sb(here, "raw", [P, W], I32), self.sb(here, "rawf", [P, W])
            di, hif = self.sb(here, "di", [P, W], I32), self.sb(here, "hif", [P, W])
            tp = self.ps(here, "tp", [P, 2, 512])
            names = ("raw_loaded", "raw_ready", "raw_turned", "cols_ready")
            raw_loaded, raw_ready, raw_turned, cols_ready = (self.sem(here, n) for n in names)
            block = here.enter_context(nc.Block())

            @block.sync
            def _(sp):
                sp.dma_start(raw[:, :], dst.rearrange("(p w) -> p w", w=W)).then_inc(raw_loaded, 16)
                sp.wait_ge(raw_ready, 1)
                sp.dma_start(raw[:, :], src.rearrange("(p w) -> p w", w=W)).then_inc(raw_loaded, 16)

            @block.tensor
            def _(pe):
                for n in range(2):
                    pe.wait_ge(raw_ready, n + 1)
                    for j in range(T):
                        mm = pe.transpose(tp[:, j // 4, (j % 4) * P:(j % 4 + 1) * P], rawf[:, j * P:(j + 1) * P], ident[:, :])
                    mm.then_inc(raw_turned, 1)

            @block.vector
            def _(dve):
                turned = tp[:, :, :].rearrange(flat)
                dve.wait_ge(raw_loaded, 16)
                dve.tensor_copy(rawf[:, :], raw[:, :]).then_inc(raw_ready, 1)
                dve.wait_ge(raw_turned, 1)
                dve.tensor_copy(dcol[:, :, :].rearrange(flat), turned)
                dve.tensor_copy(di[:, :], turned)
                dve.drain()
                dve.tensor_scalar(di[:, :], di[:, :], 7, None, ALU.logical_shift_right)
                dve.drain()
                dve.tensor_copy(hif[:, :], di[:, :])
                dve.drain()
                dve.tensor_copy(hi[:, :, :].rearrange(flat), hif[:, :])
                dve.scalar_tensor_tensor(lo[:, :, :].rearrange(flat), hif[:, :], -float(P),
                                         dcol[:, :, :].rearrange(flat), ALU.mult, ALU.add)
                dve.wait_ge(raw_loaded, 32)
                dve.tensor_scalar(rawf[:, :], raw[:, :], float(N - 1), None, ALU.min).then_inc(raw_ready, 1)
                dve.wait_ge(raw_turned, 2)
                dve.tensor_copy(di[:, :], turned)
                dve.tensor_copy(src_lo[:, :, :].rearrange(flat), turned)
                dve.drain()
                dve.tensor_scalar(di[:, :], di[:, :], (HIS - 1) * P, None, ALU.bitwise_and)
                dve.drain()
                dve.tensor_copy(src_hi[:, :, :].rearrange(flat), di[:, :])
                dve.drain()
                dve.tensor_tensor(src_lo[:, :, :].rearrange(flat), src_lo[:, :, :].rearrange(flat),
                                  src_hi[:, :, :].rearrange(flat), ALU.subtract)


    def sort_parts(self, stack):
        nc, io = self.nc, self.io
        W, T = FFN.width, SORT_TILES
        assert W == 1 << 10
        dst = io["L0_ffn_edge_index"][1, :]
        dcol, src_lo, src_hi, lo, hi = self.dcol, self.src_lo, self.src_hi, self.lo, self.hi
        iota_w, iota_b, iota_p, earlier = self.iota_w, self.iota_b, self.iota_p, self.earlier
        (oht, intra, slot, to_p, to_w, free_sb, looked) = self.several(
            stack, "sort_small",
            [P, 2, W],
            [P, 2, T],
            [P, 2, T],
            [P, PUT_TILES],
            [P, PUT_TILES],
            [P, 2, HIS],
            [P, T, HIS])
        row_d, row_lo = self.sb(stack, "row_d", [P, 2, W], I32), self.sb(stack, "row_lo", [P, 2, W], I32)
        oh_lo, oh_hi = self.sb(stack, "oh_lo", [P, 2, T, P], BF16), self.sb(stack, "oh_hi", [P, 2, T, HIS], BF16)
        equal = self.sb(stack, "equal", [P, T, P], BF16)
        pos_i, part_i, low_i = (self.sb(stack, n, [P, PUT_TILES], I32) for n in ("pos_i", "part_i", "low_i"))
        S, Q = T - PUT_TILES, PUT_TILES
        oh_w = self.sb(stack, "oh_w", [P, 2 * Q, W], FP16)
        oh_p, put_lo, put_hi = (self.sb(stack, n, [P, 2 * Q, P], FP16) for n in ("oh_p", "put_lo", "put_hi"))
        away_at, away_src = self.sb(stack, "away_at", [P, 2, S], I32), self.sb(stack, "away_src", [P, 2, S], I32)
        free = self.ps(stack, "free", [P, 512])
        at = self.ps(stack, "at", [P, 2, T, HIS])
        placed = self.ps(stack, "placed", [P, W])
        names = ("hot", "table_ready", "looked_up", "table_next", "hot_w", "put_ready", "away_ready",
                 "scatter_begun", "back_in")
        (hot, table_ready, looked_up, table_next, hot_w, put_ready, away_ready, scatter_begun, back_in) = \
            (self.sem(stack, n) for n in names)
        put_done = [self.sem(stack, f"put_done{s}") for s in range(2)]
        scattered = [self.sem(stack, f"scattered{s}") for s in range(2)]
        rows_in = [self.sem(stack, f"rows_in{s}") for s in range(2)]

        class Steps:
            def sp_load(sp, b, i, s):
                if not first(i):
                    sp.wait_ge(hot, b - 1)
                sp.dma_start(row_d[:, s, :], dst[bass.ds(b * W, W)].partition_broadcast(P)).then_inc(rows_in[s], 16)
                sp.dma_start(row_lo[:, s, :], self.lo_dram[bass.ds(b, 1), :].rearrange("a w -> (a w)")
                             .partition_broadcast(P)).then_inc(rows_in[s], 16)

            def dve_prepare(dve, b, i, s):
                dve.drain()
                dve.wait_ge(rows_in[s], i * 32 + 32)
                if not first(i):
                    dve.wait_ge(looked_up, b * T - T)
                dve.tensor_scalar(oht[:, s, :], row_lo[:, s, :], iota_p[:, 0:1], None, ALU.is_equal)
                for out, part, size in ((oh_lo, lo, P), (oh_hi, hi, HIS)):
                    dve.tensor_tensor(out[:, s, :, :], iota_b[:, 0:size].unsqueeze(1).to_broadcast([P, T, size]),
                                      part[:, :, bass.ds(b, 1)].to_broadcast([P, T, size]), ALU.is_equal)
                for j in range(T):
                    ins = dve.scalar_tensor_tensor(equal[:, j, :], row_d[:, s, j * P:(j + 1) * P], dcol[:, j, bass.ds(b, 1)],
                                                   earlier[:, :], ALU.is_equal, ALU.mult, accum_out=intra[:, s, j:j + 1])
                ins.then_inc(hot, 1)

            def pe_start(pe):
                pe.matmul(free[:, 0:HIS], self.ident[:, :], self.base_ffn[:, :], start=True, stop=False,
                          skip_group_check=True).then_inc(table_next, 1)

            def pe_rank(pe, b, s):
                pe.wait_ge(hot, b + 1)
                for j in range(T):
                    pe.wait_ge(table_ready, b * T + (j + 1))
                    pe.matmul(free[:, 0:HIS], oh_lo[:, s, j, :], oh_hi[:, s, j, :], start=False, stop=False,
                              skip_group_check=True).then_inc(table_next, 1)
                    pe.matmul(at[:, s, j, :], oht[:, s, j * P:(j + 1) * P], free_sb[:, j % 2, :],
                              start=True, stop=True, skip_group_check=True).then_inc(looked_up, 1)

            def act_tables(act, b):
                for j in range(T):
                    act.wait_ge(table_next, b * T + (j + 1))
                    act.activation(free_sb[:, j % 2, :], free[:, 0:HIS], ACT.Copy).then_inc(table_ready, 1)

            def dve_positions(dve, b, s, turn):
                dve.wait_ge(looked_up, b * T + T)
                for j in range(T):
                    dve.tensor_tensor_reduce(looked[:, j, :], at[:, s, j, :], oh_hi[:, s, j, :], 1.0, 0.0,
                                             ALU.mult, ALU.add, slot[:, s, j:j + 1])
                dve.drain()
                dve.tensor_tensor(pos_i[:, :], slot[:, s, 0:Q], intra[:, s, 0:Q], ALU.add)
                if not first(turn):
                    dve.wait_ge(scattered[s], turn * (16 * S))
                dve.tensor_tensor(away_at[:, s, :], slot[:, s, Q:T], intra[:, s, Q:T], ALU.add)
                dve.tensor_tensor(away_src[:, s, :], src_lo[:, Q:T, bass.ds(b, 1)].rearrange("p t b -> p (t b)"),
                                  src_hi[:, Q:T, bass.ds(b, 1)].rearrange("p t b -> p (t b)"), ALU.add) \
                   .then_inc(away_ready, 1)
                dve.drain()
                dve.tensor_scalar(part_i[:, :], pos_i[:, :], 10, None, ALU.logical_shift_right)
                dve.tensor_scalar(low_i[:, :], pos_i[:, :], W - 1, None, ALU.bitwise_and)
                dve.drain()
                dve.tensor_copy(to_p[:, :], part_i[:, :])
                dve.tensor_copy(to_w[:, :], low_i[:, :])
                dve.drain()
                if not first(turn):
                    dve.wait_ge(put_done[s], turn)
                for n in range(Q):
                    dve.tensor_scalar(oh_w[:, s * Q + n, :], iota_w[:, :], to_w[:, n:n + 1], None, ALU.is_equal)
                    dve.tensor_scalar(oh_p[:, s * Q + n, :], iota_w[:, 0:P], to_p[:, n:n + 1], None, ALU.is_equal) \
                       .then_inc(hot_w, 1)

            def act_sources(act, b, s):
                for n in range(Q):
                    act.wait_ge(hot_w, b * Q + (n + 1))
                    act.activation(put_hi[:, s * Q + n, :], oh_p[:, s * Q + n, :], ACT.Copy, scale=src_hi[:, n, bass.ds(b, 1)])
                    act.activation(put_lo[:, s * Q + n, :], oh_p[:, s * Q + n, :], ACT.Copy, scale=src_lo[:, n, bass.ds(b, 1)]) \
                       .then_inc(put_ready, 1)

            def pool_scatter(pool, bound, b, s):
                pool.wait_ge(away_ready, b + 1)
                pool.sem_inc(scatter_begun, 1)
                for j in range(S):
                    pool.indirect_dma_start(
                        out=self.sorted_dram[:, :], out_offset=bass.IndirectOffsetOnAxis(ap=away_at[:, s, j:j + 1], axis=0),
                        in_=away_src[:, s, j:j + 1], in_offset=None, bounds_check=bound, oob_is_err=False) \
                        .then_inc(scattered[s], 16)

            def pe_put(pe, b, s, head, tail):
                for n in range(Q):
                    pe.wait_ge(put_ready, b * Q + (n + 1))
                    for half in range(2):
                        cols = slice(half * 512, (half + 1) * 512)
                        pe.matmul(placed[:, cols], put_hi[:, s * Q + n, :], oh_w[:, s * Q + n, cols],
                                  start=(head and n == 0), stop=False, skip_group_check=True)
                        mm = pe.matmul(placed[:, cols], put_lo[:, s * Q + n, :], oh_w[:, s * Q + n, cols],
                                       start=False, stop=(tail and n == Q - 1), skip_group_check=True)
                mm.then_inc(put_done[s], 1)

            def sp_back(sp):
                for s in range(2):
                    sp.wait_ge(scattered[s], SORT_BLOCKS // 2 * (16 * S))
                sp.dma_start(row_d[:, 0, :], self.sorted_dram.rearrange("(p w) a -> p (w a)", w=W)).then_inc(back_in, 16)

            def dve_take(dve):
                for s in range(2):
                    dve.wait_ge(put_done[s], SORT_BLOCKS // 2)
                dve.tensor_copy(row_lo[:, 0, :], placed[:, :])
                dve.wait_ge(back_in, 16)
                dve.drain()
                dve.tensor_tensor(self.edge_src["ffn"][:, 0:W], row_lo[:, 0, :], row_d[:, 0, :], ALU.add)
        return Steps

    def starts(self, g, stack):
        nc = self.nc
        W = g.width
        ident, ones = self.ident, self.ones
        seg_dram = self.seg_dram[g.name]
        neg = self.sb(stack, "neg", [P, W])
        ed = self.sb(stack, "ed_edge", [P, H, W])
        whole, whole_neg = self.sb(stack, "whole", [P, 1]), self.sb(stack, "whole_neg", [P, 1])
        diag = self.sb(stack, "diag", [P, P])
        whole_row = self.sb(stack, "whole_row", [H, P])
        self.neg, self.ed_edge, self.whole_neg = neg, ed, whole_neg
        with ExitStack() as mine:
            (seg_rows, seg, same, last, chain, carry_in, lastt) = self.several(
                mine, "start_parts",
                [P, NT, 1 + H],
                [P, W, 1 + H],
                [P, W],
                [P, H],
                [H, P + 1],
                [P, H],
                [H, P])
            pa, pb = self.ps(mine, "pa", [P, P]), self.ps(mine, "pb", [P, P])
            names = ("zeroed", "cleared", "rows_ready", "scattered", "seg_loaded", "last_ready", "spread", "chained", "turned")
            zeroed, cleared, rows_ready, scattered, seg_loaded, last_ready, spread, chained, turned = \
                (self.sem(mine, n) for n in names)
            block = mine.enter_context(nc.Block())

            @block.sync
            def _(sp):
                sp.wait_ge(zeroed, 1)
                sp.dma_start(seg_dram.rearrange("(p w) c -> p (w c)", w=W), seg[:, :, :].rearrange("p w c -> p (w c)")) \
                  .then_inc(cleared, 16)
                sp.wait_ge(scattered, 16 * NT)
                sp.dma_start(seg[:, :, :].rearrange("p w c -> p (w c)"), seg_dram.rearrange("(p w) c -> p (w c)", w=W)) \
                  .then_inc(seg_loaded, 16)
                sp.wait_ge(seg_loaded, 16)

            @block.gpsimd
            def _(pool):
                bound = pool.to_reg(P * W - 1)
                pool.wait_ge(rows_ready, 1)
                pool.wait_ge(cleared, 16)
                for t in range(NT):
                    pool.indirect_dma_start(
                        out=seg_dram[:, :], out_offset=bass.IndirectOffsetOnAxis(ap=self.seg_at[g.name][:, t:t + 1], axis=0),
                        in_=seg_rows[:, t, :], in_offset=None, bounds_check=bound, oob_is_err=False).then_inc(scattered, 16)
                pool.wait_ge(scattered, 16 * NT)

            @block.vector
            def _(dve):
                dve.memset(seg[:, :, :], 0.0).then_inc(zeroed, 1)
                dve.memset(seg_rows[:, :, 0:1], 1.0)
                dve.tensor_copy(seg_rows[:, :, 1:1 + H], self.ed[g.name][:, :, :]).then_inc(rows_ready, 1)
                dve.wait_ge(seg_loaded, 16)
                dve.tensor_scalar(neg[:, :], seg[:, :, 0], NEG, None, ALU.mult)
                dve.tensor_scalar(same[:, :], seg[:, :, 0], -1.0, 1.0, ALU.mult, ALU.add)
                dve.tensor_reduce(whole[:, :], seg[:, :, 0], AX, ALU.max)
                dve.drain()
                dve.tensor_scalar(whole[:, :], whole[:, :], -1.0, 1.0, ALU.mult, ALU.add)
                for h in range(H):
                    dve.tensor_tensor_scan(ed[:, h, :], same[:, :], seg[:, :, 1 + h], 0.0, ALU.mult, ALU.add)
                dve.drain()
                dve.tensor_copy(last[:, :], ed[:, :, W - 1])
                dve.tensor_scalar(whole_neg[:, :], whole[:, :], -NEG, NEG, ALU.mult, ALU.add)
                dve.tensor_scalar(diag[:, :], ident[:, :], whole[:, 0:1], None, ALU.mult)
                dve.drain()
                dve.sem_inc(last_ready, 1)
                dve.wait_ge(spread, 1)
                dve.tensor_copy(whole_row[:, :], pb[0:H, :])
                dve.tensor_copy(lastt[:, :], pa[0:H, :])
                dve.memset(chain[:, 0:1], 0.0)
                dve.drain()
                dve.tensor_tensor_scan(chain[:, 1:P + 1], whole_row[:, :], lastt[:, :], 0.0, ALU.mult, ALU.add).then_inc(chained, 1)
                dve.wait_ge(turned, 1)
                dve.tensor_copy(carry_in[:, :], pa[:, 0:H])
                dve.drain()
                for h in range(H):
                    dve.tensor_tensor_scan(ed[:, h, :], same[:, :], seg[:, :, 1 + h], carry_in[:, h:h + 1], ALU.mult, ALU.add)

            @block.tensor
            def _(pe):
                pe.wait_ge(last_ready, 1)
                pe.transpose(pa[0:H, :], last[:, :], ident[:, :])
                pe.matmul(pb[0:H, :], ones[:, 0:H], diag[:, :], start=True, stop=True).then_inc(spread, 1)
                pe.wait_ge(chained, 1)
                pe.transpose(pa[:, 0:H], chain[:, 0:P], ident[0:H, 0:H]).then_inc(turned, 1)

    def chunk_parts(self, g, stack, fin, finm):
        W, T, C, R, S, K = g.width, g.chunk, g.cols, g.row, g.state, g.per_head
        neg, ed, src = self.neg, self.ed_edge, self.edge_src[g.name]
        idx = self.sb(stack, "idx", [P, 2, T], I32)
        (e, m, dl, pm, w, r) = self.several(
            stack, "chunk_parts",
            [P, H, T],
            [P, 2, H, T + 1],
            [P, H, T + 1],
            [P, H, T],
            [P, H, T],
            [P, C + H, T + 1])
        got = self.sb(stack, "got", [P, 2, T, R])
        y = self.sb(stack, "y", [P, 2, C + H, T + 1])
        rows = self.sb(stack, "rows", [P, 2, T, S])
        names = ("idx_ready", "gather_begun", "logits_ready", "w_ready", "r_ready", "scanned", "rows_ready")
        idx_ready, gather_begun, logits_ready, w_ready, r_ready, scanned, rows_ready = (self.sem(stack, n) for n in names)
        gathered = [self.sem(stack, f"gathered{s}") for s in range(2)]
        stored = [self.sem(stack, f"stored{s}") for s in range(2)]
        by_part = self.state_dram[g.name].rearrange("(p w) s -> p w s", w=W)

        class Steps:
            def pool_gather(pool, bound, c, s):
                pool.wait_ge(idx_ready, c + 1)
                pool.sem_inc(gather_begun, 1)
                for t in range(T):
                    pool.indirect_dma_start(
                        out=got[:, s, t, :], out_offset=None, in_=self.row_dram[g.name][:, :],
                        in_offset=bass.IndirectOffsetOnAxis(ap=idx[:, s, t:t + 1], axis=0),
                        bounds_check=bound, oob_is_err=False).then_inc(gathered[s], 16)

            def dve_start(dve):
                for s in range(2):
                    dve.tensor_copy(idx[:, s, :], src[:, s * T:(s + 1) * T]).then_inc(idx_ready, 1)
                dve.memset(m[:, 1, :, T:T + 1], NEG)
                dve.memset(dl[:, :, 0:1], NEG)
                dve.memset(y[:, 1, :, T:T + 1], 0.0)
                dve.drain()

            def dve_logits(dve, c, i, s):
                at = bass.ds(c * T, T)
                neg_h = neg[:, at].unsqueeze(1).to_broadcast([P, H, T])
                dve.wait_ge(gathered[s], i * (16 * T) + 16 * T)
                dve.tensor_tensor(e[:, :, :], got[:, s, :, C:C + H].rearrange("p t h -> p h t"), ed[:, :, at], ALU.add)
                if not first(i):
                    dve.wait_ge(rows_ready, c - 1)
                dve.tensor_copy(m[:, s, :, 0:1], m[:, 1 - s, :, T:T + 1])
                dve.drain()
                dve.scalar_tensor_tensor(e[:, :, :], e[:, :, :], g.slope, e[:, :, :], ALU.mult, ALU.max)
                dve.drain()
                for h in range(H):
                    dve.tensor_tensor_scan(m[:, s, h, 1:T + 1], neg[:, at], e[:, h, :], m[:, s, h, 0:1], ALU.add, ALU.max)
                dve.drain()
                dve.tensor_tensor(pm[:, :, :], e[:, :, :], m[:, s, :, 1:T + 1], ALU.subtract)
                dve.tensor_tensor(dl[:, :, 1:T + 1], m[:, s, :, 0:T], neg_h, ALU.add)
                dve.drain()
                dve.tensor_tensor(dl[:, :, 1:T + 1], dl[:, :, 1:T + 1], m[:, s, :, 1:T + 1], ALU.subtract) \
                   .then_inc(logits_ready, 1)
                dve.tensor_copy(y[:, s, :, 0:1], y[:, 1 - s, :, T:T + 1])

            def act_exps(act, c):
                act.wait_ge(logits_ready, c + 1)
                act.activation(w[:, :, :], pm[:, :, :], ACT.Exp).then_inc(w_ready, 1)
                if not (isinstance(c, int) and c == 0):
                    act.wait_ge(scanned, c)
                for h in range(H):
                    act.activation(r[:, h * K:(h + 1) * K, :], dl[:, h, :].unsqueeze(1).to_broadcast([P, K, T + 1]), ACT.Exp)
                act.activation(r[:, C:C + H, :], dl[:, :, :], ACT.Exp).then_inc(r_ready, 1)

            def dve_weigh(dve, c, s):
                dve.wait_ge(w_ready, c + 1)
                for h in range(H):
                    dve.tensor_tensor(y[:, s, h * K:(h + 1) * K, 1:T + 1],
                                      got[:, s, :, h * K:(h + 1) * K].rearrange("p t k -> p k t"),
                                      w[:, h, :].unsqueeze(1).to_broadcast([P, K, T]), ALU.mult)
                dve.tensor_copy(y[:, s, C:C + H, 1:T + 1], w[:, :, :])
                dve.drain()
                dve.tensor_copy(idx[:, s, :], src[:, bass.ds((c + 2) * T, T)]).then_inc(idx_ready, 1)

            def dve_scan(dve, c, s):
                dve.wait_ge(r_ready, c + 1)
                flat = y[:, s, :, :].rearrange("p c t -> p (c t)")
                dve.tensor_tensor_scan(flat, r[:, :, :].rearrange("p c t -> p (c t)"), flat, 0.0, ALU.mult, ALU.add) \
                   .then_inc(scanned, 1)
                dve.drain()

            def act_rows(act, c, i, s):
                act.wait_ge(scanned, c + 1)
                if not first(i):
                    act.wait_ge(stored[s], i * 16)
                act.activation(rows[:, s, :, 0:C + H].rearrange("p t c -> p c t"), y[:, s, :, 1:T + 1], ACT.Copy)
                act.activation(rows[:, s, :, C + H:S].rearrange("p t h -> p h t"), m[:, s, :, 1:T + 1], ACT.Copy) \
                   .then_inc(rows_ready, 1)

            def sp_store(sp, c, s):
                sp.wait_ge(rows_ready, c + 1)
                sp.dma_start(by_part[:, bass.ds(c * T, T), :], rows[:, s, :, :]).then_inc(stored[s], 16)

            def sp_end(sp):
                for s in range(2):
                    sp.wait_ge(stored[s], 16 * (g.chunks // 2))

            def dve_end(dve):
                dve.tensor_copy(fin[:, :], y[:, 1, :, T])
                dve.tensor_copy(finm[:, :], m[:, 1, :, T])
        return Steps

    def carry(self, g, fin, finm):
        nc = self.nc
        C, S, K = g.cols, g.state, g.per_head
        ident, ones, whole_neg, carry_dram = self.ident, self.ones, self.whole_neg, self.carry_dram[g.name]
        with ExitStack() as mine:
            groups = [(a, min(a + P, C)) for a in range(0, C, P)] + [(C, C + H)]
            (mt, ms, wn_row, f0, f1, f1c, diag2, spread_w, acc, keep_row, run, table) = self.several(
                mine, "carry_parts",
                [H, P],
                [H, P + 1],
                [H, P],
                [H, P],
                [H, P],
                [P, H],
                [P, P],
                [H, C + H],
                [P, P],
                [P, P],
                [P, len(groups), P + 1],
                [P, S])
            pa, pb, pc = (self.ps(mine, n, [P, 512]) for n in ("pa", "pb", "pc"))
            names = ("sel_made", "diag_ready", "spread", "max_ready", "f_ready", "f_turned", "fin_ready", "fin_turned", "run_ready",
                     "run_turned", "table_ready", "table_out")
            sel_made, diag_ready, spread, max_ready, f_ready, f_turned, fin_ready, fin_turned, run_ready, run_turned, table_ready, table_out = \
                (self.sem(mine, n) for n in names)
            block = mine.enter_context(nc.Block())

            @block.gpsimd
            def _(pool):
                pool.memset(spread_w[:, :], 1.0)
                pool.drain()
                pool.affine_select(out=spread_w[:, 0:C], in_=spread_w[:, 0:C], compare_op=ALU.is_ge, fill=0.0,
                                   base=0, pattern=[[1, C]], channel_multiplier=-K)
                pool.drain()
                pool.affine_select(out=spread_w[:, 0:C], in_=spread_w[:, 0:C], compare_op=ALU.is_gt, fill=0.0,
                                   base=K, pattern=[[-1, C]], channel_multiplier=K)
                pool.affine_select(out=spread_w[:, C:C + H], in_=spread_w[:, C:C + H], compare_op=ALU.is_equal, fill=0.0,
                                   base=0, pattern=[[1, H]], channel_multiplier=-1).then_inc(sel_made, 1)

            @block.tensor
            def _(pe):
                pe.wait_ge(diag_ready, 1)
                pe.transpose(pa[0:H, 0:P], finm[:, :], ident[:, :])
                pe.matmul(pb[0:H, 0:P], ones[:, 0:H], diag2[:, :], start=True, stop=True).then_inc(spread, 1)
                pe.wait_ge(max_ready, 1)
                pe.transpose(pc[:, 0:H], ms[:, 0:P], ident[0:H, 0:H])
                pe.wait_ge(f_ready, 1)
                pe.transpose(pc[:, H:2 * H], f1[:, :], ident[0:H, 0:H]).then_inc(f_turned, 1)
                pe.wait_ge(sel_made, 1)
                pe.wait_ge(fin_ready, 1)
                for n, (a, b) in enumerate(groups):
                    if n:
                        pe.wait_ge(run_ready, n)
                    pe.transpose(pa[0:b - a, 0:P], fin[:, a:b], ident[:, :])
                    pe.matmul(pb[0:b - a, 0:P], spread_w[:, a:b], f0[:, :], start=True, stop=True).then_inc(fin_turned, 1)
                pe.wait_ge(run_ready, len(groups))
                for n, (a, b) in enumerate(groups):
                    mm = pe.transpose(pc[:, a:b], run[0:b - a, n, 0:P], ident[0:b - a, 0:b - a])
                mm.then_inc(run_turned, 1)

            @block.vector
            def _(dve):
                dve.tensor_scalar(diag2[:, :], ident[:, :], whole_neg[:, 0:1], None, ALU.mult).then_inc(diag_ready, 1)
                dve.memset(ms[:, 0:1], NEG)
                dve.memset(run[:, :, 0:1], 0.0)
                dve.wait_ge(spread, 1)
                dve.tensor_copy(wn_row[:, :], pb[0:H, 0:P])
                dve.tensor_copy(mt[:, :], pa[0:H, 0:P])
                dve.drain()
                dve.tensor_tensor_scan(ms[:, 1:P + 1], wn_row[:, :], mt[:, :], NEG, ALU.add, ALU.max)
                dve.drain()
                dve.tensor_tensor(f1[:, :], mt[:, :], ms[:, 1:P + 1], ALU.subtract)
                dve.tensor_tensor(f0[:, :], ms[:, 0:P], wn_row[:, :], ALU.add)
                dve.drain()
                dve.tensor_tensor(f0[:, :], f0[:, :], ms[:, 1:P + 1], ALU.subtract).then_inc(max_ready, 1)
                dve.wait_ge(f_turned, 1)
                dve.tensor_copy(f1c[:, :], pc[:, H:2 * H])
                dve.tensor_copy(table[:, C + H:S], pc[:, 0:H])
                dve.drain()
                by_head = fin[:, 0:C].rearrange("p (h k) -> p h k", k=K)
                dve.tensor_tensor(by_head, by_head, heads(f1c[:, :], K), ALU.mult)
                dve.tensor_tensor(fin[:, C:C + H], fin[:, C:C + H], f1c[:, :], ALU.mult).then_inc(fin_ready, 1)
                for n, (a, b) in enumerate(groups):
                    dve.wait_ge(fin_turned, n + 1)
                    dve.tensor_copy(acc[0:b - a, :], pa[0:b - a, 0:P])
                    dve.tensor_copy(keep_row[0:b - a, :], pb[0:b - a, 0:P])
                    dve.drain()
                    dve.tensor_tensor_scan(run[0:b - a, n, 1:P + 1], keep_row[0:b - a, :], acc[0:b - a, :], 0.0,
                                           ALU.mult, ALU.add).then_inc(run_ready, 1)
                    dve.drain()
                dve.wait_ge(run_turned, 1)
                dve.tensor_copy(table[:, 0:C + H], pc[:, 0:C + H]).then_inc(table_ready, 1)

            @block.scalar
            def _(act):
                act.wait_ge(max_ready, 1)
                act.activation(f0[:, :], f0[:, :], ACT.Exp)
                act.activation(f1[:, :], f1[:, :], ACT.Exp).then_inc(f_ready, 1)

            @block.sync
            def _(sp):
                sp.wait_ge(table_ready, 1)
                sp.dma_start(carry_dram[:, :], table[:, :]).then_inc(table_out, 16)
                sp.wait_ge(table_out, 16)

    def gnn_and_sort(self, fin, finm):
        nc = self.nc
        W = FFN.width
        steps = SORT_BLOCKS // 2 - 1
        both = GNN.chunks // 2 - 1
        assert 2 * both <= steps
        with ExitStack() as here:
            iota_i, iota_pi = self.sb(here, "iota_i", [P, P], I32), self.sb(here, "iota_pi", [P, 1], I32)
            self.iota_w, self.iota_b = self.sb(here, "iota_w", [P, W], FP16), self.sb(here, "iota_b", [P, P], BF16)
            self.iota_p, self.earlier = self.several(here, "sort_constants", [P, 1], [P, P])
            iota_w = self.iota_w
            with ExitStack() as mine:
                iota_l, nothing = self.sb(mine, "iota_l", [P, W], I32), self.sb(mine, "nothing", [P, W], I32)
                zeroed, cleared = self.sem(mine, "zeroed"), self.sem(mine, "cleared")
                block = mine.enter_context(nc.Block())

                @block.vector
                def _(dve):
                    dve.memset(nothing[:, :], 0).then_inc(zeroed, 1)

                @block.sync
                def _(sp):
                    sp.wait_ge(zeroed, 1)
                    sp.dma_start(self.sorted_dram.rearrange("(p w) a -> p (w a)", w=W), nothing[:, :]).then_inc(cleared, 16)
                    sp.wait_ge(cleared, 16)

                @block.gpsimd
                def _(pool):
                    pool.iota(iota_l[:, :], pattern=[[1, W]], base=0, channel_multiplier=0)
                    pool.iota(iota_pi[:, :], pattern=[[0, 1]], base=0, channel_multiplier=1)
                    pool.affine_select(out=self.earlier[:, :], in_=self.ones[:, :], compare_op=ALU.is_gt, fill=0.0,
                                       base=0, pattern=[[-1, P]], channel_multiplier=1)
                    pool.drain()
                    pool.tensor_copy(iota_w[:, :], iota_l[:, :])
                    pool.tensor_copy(self.iota_b[:, :], iota_l[:, 0:P])
                    pool.tensor_copy(self.iota_p[:, :], iota_pi[:, :])

            self.part = "stage1"
            edge = self.chunk_parts(GNN, here, fin, finm)
            sort = self.sort_parts(here)
            block = here.enter_context(nc.Block())

            @block.gpsimd
            def _(pool):
                bound, places = pool.to_reg(NPAD - 1), pool.to_reg(P * W - 1)
                for s in range(2):
                    edge.pool_gather(pool, bound, s, s)
                sort.pool_scatter(pool, places, 0, 0)
                edge.pool_gather(pool, bound, 2, 0)
                with pool.Fori(1, both) as i:
                    for s in range(2):
                        k = i * 2 + (s - 1)
                        edge.pool_gather(pool, bound, i * 2 + (s + 1), 1 - s)
                        sort.pool_scatter(pool, places, k * 2 - 1, 1)
                        sort.pool_scatter(pool, places, k * 2, 0)
                edge.pool_gather(pool, bound, GNN.chunks - 1, 1)
                with pool.Fori(2 * both - 1, steps + 1) as k:
                    sort.pool_scatter(pool, places, k * 2 - 1, 1)
                    sort.pool_scatter(pool, places, k * 2, 0)
                sort.pool_scatter(pool, places, SORT_BLOCKS - 1, 1)

            @block.sync
            def _(sp):
                for k in range(2):
                    for s in range(2):
                        sort.sp_load(sp, 2 * k + s, k, s)
                for s in range(2):
                    edge.sp_store(sp, s, s)
                with sp.Fori(1, both + 1) as i:
                    for s in range(2):
                        k = i * 2 + s
                        sort.sp_load(sp, k * 2, k, 0)
                        sort.sp_load(sp, k * 2 + 1, k, 1)
                        edge.sp_store(sp, i * 2 + s, s)
                with sp.Fori(2 * both + 2, steps + 1) as k:
                    sort.sp_load(sp, k * 2, k, 0)
                    sort.sp_load(sp, k * 2 + 1, k, 1)
                edge.sp_end(sp)
                sort.sp_back(sp)

            @block.tensor
            def _(pe):
                sort.pe_start(pe)
                sort.pe_rank(pe, 0, 0)
                sort.pe_rank(pe, 1, 1)
                sort.pe_put(pe, 0, 0, True, False)
                with pe.Fori(1, steps + 1) as k:
                    sort.pe_rank(pe, k * 2, 0)
                    sort.pe_put(pe, k * 2 - 1, 1, False, False)
                    sort.pe_rank(pe, k * 2 + 1, 1)
                    sort.pe_put(pe, k * 2, 0, False, False)
                sort.pe_put(pe, SORT_BLOCKS - 1, 1, False, True)

            @block.scalar
            def _(act):
                def sort_pair(k):
                    sort.act_tables(act, k * 2)
                    sort.act_sources(act, k * 2 - 1, 1)
                    sort.act_tables(act, k * 2 + 1)
                    sort.act_sources(act, k * 2, 0)
                sort.act_tables(act, 0)
                sort.act_tables(act, 1)
                sort.act_sources(act, 0, 0)
                for c in range(2):
                    edge.act_exps(act, c)
                    edge.act_rows(act, c, 0, c)
                with act.Fori(1, both + 1) as i:
                    for s in range(2):
                        edge.act_exps(act, i * 2 + s)
                        sort_pair(i * 2 + (s - 1))
                        edge.act_rows(act, i * 2 + s, i, s)
                with act.Fori(2 * both + 1, steps + 1) as k:
                    sort_pair(k)
                sort.act_sources(act, SORT_BLOCKS - 1, 1)

            @block.vector
            def _(dve):
                edge.dve_start(dve)
                sort.dve_prepare(dve, 0, 0, 0)
                sort.dve_prepare(dve, 1, 0, 1)
                sort.dve_positions(dve, 0, 0, 0)
                for c in range(2):
                    edge.dve_logits(dve, c, 0, c)
                    edge.dve_weigh(dve, c, c)
                    edge.dve_scan(dve, c, c)

                def two_steps(i):
                    for s in range(2):
                        c, k = i * 2 + s, i * 2 + (s - 1)
                        edge.dve_logits(dve, c, i, s)
                        sort.dve_prepare(dve, k * 2, k, 0)
                        sort.dve_positions(dve, k * 2 - 1, 1, k - 1)
                        edge.dve_weigh(dve, c, s)
                        sort.dve_prepare(dve, k * 2 + 1, k, 1)
                        sort.dve_positions(dve, k * 2, 0, k)
                        edge.dve_scan(dve, c, s)
                two_steps(1)
                with dve.Fori(2, both + 1) as i:
                    two_steps(i)
                edge.dve_end(dve)
                with dve.Fori(2 * both + 1, steps + 1) as k:
                    sort.dve_prepare(dve, k * 2, k, 0)
                    sort.dve_positions(dve, k * 2 - 1, 1, k - 1)
                    sort.dve_prepare(dve, k * 2 + 1, k, 1)
                    sort.dve_positions(dve, k * 2, 0, k)
                sort.dve_positions(dve, SORT_BLOCKS - 1, 1, SORT_BLOCKS // 2 - 1)
                sort.dve_take(dve)

    def ffn_and_experts(self, fin, finm, xt_all):
        nc, io = self.nc, self.io
        FT = HIDDEN // P
        B = FFN_BLOCK
        HALF = B * P // 2
        blocks = NT // B
        EH = FT * 2
        pairs = FFN.chunks // 2
        assert blocks * EXPERTS <= pairs
        with ExitStack() as here:
            w1 = self.sb(here, "w1", [P, EXPERTS, 2, HIDDEN])
            w2 = self.sb(here, "w2", [P, EXPERTS, FT, D])
            b1, b2 = self.sb(here, "b1", [P, EXPERTS, FT]), self.sb(here, "b2", [1, EXPERTS, D])
            hid = self.sb(here, "hid", [P, FT, B * P])
            yrow = self.sb(here, "yrow", [P, 2, B, D])
            ph, po = self.ps(here, "ph", [P, 4, 512]), self.ps(here, "po", [P, 4, 512])
            names = ("w_loaded", "hid_made", "hid_ready", "out_made", "out_used")
            w_loaded, hid_made, hid_ready, out_made, out_used = (self.sem(here, n) for n in names)
            y_out = [self.sem(here, f"y_out{s}") for s in range(2)]
            edge = self.chunk_parts(FFN, here, fin, finm)
            by_tile = self.y_dram.rearrange("(t p) e d -> p t e d", p=P)
            block = here.enter_context(nc.Block())

            def begun(q, e):
                return isinstance(q, int) and q == 0 and e == 0

            def walk(eng, step, rest):
                for e in range(EXPERTS):
                    step(0, e, e)
                with eng.Fori(1, blocks) as b:
                    for e in range(EXPERTS):
                        step(b, e, b * EXPERTS + e)
                if rest is not None:
                    with eng.Fori(blocks * EXPERTS, pairs) as i:
                        rest(i)

            @block.gpsimd
            def _(pool):
                bound = pool.to_reg(NPAD - 1)
                in_pairs(pool, FFN.chunks, lambda c, i, s: edge.pool_gather(pool, bound, c, s))

            @block.sync
            def _(sp):
                for e in range(EXPERTS):
                    sp.dma_start(w1[:, e, :, :], io["L0_ffn_W1"][e, :, :].rearrange("(k p) f -> p k f", p=P)).then_inc(w_loaded, 16)
                    sp.dma_start(w2[:, e, :, :], io["L0_ffn_W2"][e, :, :].rearrange("(f p) d -> p f d", p=P)).then_inc(w_loaded, 16)
                    sp.dma_start(b2[:, e, :], io["L0_ffn_b2"][e, :].rearrange("(a d) -> a d", a=1)).then_inc(w_loaded, 16)
                    for f in range(FT):
                        sp.dma_start(b1[:, e, f:f + 1], io["L0_ffn_b1"][e, f * P:(f + 1) * P].rearrange("(p a) -> p a", a=1)) \
                          .then_inc(w_loaded, 16)

                def step(b, e, q):
                    edge.sp_store(sp, q * 2, 0)
                    edge.sp_store(sp, q * 2 + 1, 1)
                    sp.wait_ge(out_used, q * B + B)
                    sp.dma_start(by_tile[:, bass.ds(b * B, B), e, :], yrow[:, e % 2, :, :]).then_inc(y_out[e % 2], 16)

                def rest(i):
                    edge.sp_store(sp, i * 2, 0)
                    edge.sp_store(sp, i * 2 + 1, 1)
                walk(sp, step, rest)
                edge.sp_end(sp)
                for s in range(2):
                    sp.wait_ge(y_out[s], 16 * blocks * EXPERTS // 2)

            @block.tensor
            def _(pe):
                pe.wait_ge(w_loaded, 16 * EXPERTS * (3 + FT))

                def step(b, e, q):
                    for f in range(FT):
                        for half in range(2):
                            n = f * 2 + half
                            if not (begun(q, e) and n < 4):
                                pe.wait_ge(hid_ready, q * EH + (n - 3))
                            for k in range(2):
                                mm = pe.matmul(ph[:, n % 4, 0:HALF], w1[:, e, k, f * P:(f + 1) * P],
                                               xt_all[:, k, bass.ds(b * (B * P) + half * HALF, HALF)],
                                               start=(k == 0), stop=(k == 1))
                            mm.then_inc(hid_made, 1)
                    pe.wait_ge(hid_ready, q * EH + EH)
                    for t in range(B):
                        slot = (e * B + t) % 4
                        if not (begun(q, e) and t < 4):
                            pe.wait_ge(out_used, q * B + (t - 3))
                        pe.matmul(po[:, slot, 0:D], self.ones[0:1, :], b2[:, e, :], start=True, stop=False)
                        for f in range(FT):
                            mm = pe.matmul(po[:, slot, 0:D], hid[:, f, t * P:(t + 1) * P], w2[:, e, f, :],
                                           start=False, stop=(f == FT - 1))
                        mm.then_inc(out_made, 1)
                walk(pe, step, None)

            @block.scalar
            def _(act):
                act.wait_ge(w_loaded, 16 * EXPERTS * (3 + FT))

                def chunk(c, i, s):
                    edge.act_exps(act, c)
                    edge.act_rows(act, c, i, s)

                def step(b, e, q):
                    chunk(q * 2, q, 0)
                    if not begun(q, e):
                        act.wait_ge(out_made, q * B)
                    for f in range(FT):
                        for half in range(2):
                            n = f * 2 + half
                            act.wait_ge(hid_made, q * EH + (n + 1))
                            act.activation(hid[:, f, half * HALF:(half + 1) * HALF], ph[:, n % 4, 0:HALF],
                                           ACT.Gelu, bias=b1[:, e, f:f + 1]).then_inc(hid_ready, 1)
                    chunk(q * 2 + 1, q, 1)

                def rest(i):
                    chunk(i * 2, i, 0)
                    chunk(i * 2 + 1, i, 1)
                walk(act, step, rest)

            @block.vector
            def _(dve):
                def chunk(c, i, s):
                    edge.dve_logits(dve, c, i, s)
                    edge.dve_weigh(dve, c, s)
                    edge.dve_scan(dve, c, s)
                edge.dve_start(dve)

                def step(b, e, q):
                    chunk(q * 2, q, 0)
                    chunk(q * 2 + 1, q, 1)
                    if not (isinstance(q, int) and q < 2):
                        dve.wait_ge(y_out[e % 2], (b * (EXPERTS // 2) + e // 2) * 16)
                    for t in range(B):
                        dve.wait_ge(out_made, q * B + (t + 1))
                        dve.tensor_copy(yrow[:, e % 2, t, :], po[:, (e * B + t) % 4, 0:D]).then_inc(out_used, 1)

                def rest(i):
                    chunk(i * 2, i, 0)
                    chunk(i * 2 + 1, i, 1)
                walk(dve, step, rest)
                edge.dve_end(dve)

    def combine(self, gate, out):
        nc = self.nc
        B = FFN_BLOCK
        blocks = NT // B
        with ExitStack() as here:
            x, y = self.sb(here, "x", [P, 2, B, D]), self.sb(here, "y", [P, 2, B, EXPERTS, D])
            ready = self.sem(here, "ready")
            loaded, stored = [self.sem(here, f"loaded{s}") for s in range(2)], [self.sem(here, f"stored{s}") for s in range(2)]
            block = here.enter_context(nc.Block())
            x_view = self.x1_dram.rearrange("(t p) d -> p t d", p=P)
            y_view = self.y_dram.rearrange("(t p) e d -> p t (e d)", p=P)

            @block.sync
            def _(sp):
                for b in range(blocks):
                    s = b % 2
                    if b >= 2:
                        sp.wait_ge(stored[s], 16 * (b // 2))
                    tiles = slice(b * B, (b + 1) * B)
                    sp.dma_start(x[:, s, :, :], x_view[:, tiles, :]).then_inc(loaded[s], 16)
                    sp.dma_start(y[:, s, :, :, :].rearrange("p t e d -> p t (e d)"), y_view[:, tiles, :]).then_inc(loaded[s], 16)

            @block.scalar
            def _(act):
                for b in range(blocks):
                    s = b % 2
                    act.wait_ge(ready, b + 1)
                    a, full = b * B, (B if b < blocks - 1 else B - 1)
                    act.dma_start(out[a * P:(a + full) * P, :].rearrange("(t p) d -> p t d", p=P), x[:, s, 0:full, :]) \
                       .then_inc(stored[s], 16)
                s = (blocks - 1) % 2
                act.dma_start(out[(NT - 1) * P:N, :], x[0:LAST, s, B - 1, :]).then_inc(stored[s], 16)
                act.wait_ge(stored[s], 16 * ((blocks + 1) // 2) + 16)
                act.wait_ge(stored[1 - s], 16 * (blocks // 2))

            @block.vector
            def _(dve):
                for b in range(blocks):
                    s = b % 2
                    dve.wait_ge(loaded[s], 32 * (b // 2) + 32)
                    for e in range(EXPERTS):
                        for t in range(B):
                            ins = dve.scalar_tensor_tensor(x[:, s, t, :], y[:, s, t, e, :], gate[:, b * B + t, e:e + 1],
                                                           x[:, s, t, :], ALU.mult, ALU.add)
                        if e < EXPERTS - 1:
                            dve.drain()
                    ins.then_inc(ready, 1)

    def gather_nodes(self, g, own=None, agg=None):
        nc = self.nc
        C, S, K = g.cols, g.state, g.per_head
        parts = 2 if own is None else 3
        with ExitStack() as here:
            idx = self.sb(here, "idx", [P, 2, 2], I32)
            st = self.sb(here, "st", [P, 2, 2, S])
            (mstar, d, ya, yb, den, den2) = self.several(
                here, "node_parts",
                [P, H],
                [P, 2, 3, H],
                [P, C],
                [P, C],
                [P, H],
                [P, 3, H])
            names = ("ready", "begun", "shift_ready", "exp_ready")
            ready, begun, shift_ready, exp_ready = (self.sem(here, n) for n in names)
            got = [self.sem(here, f"got{s}") for s in range(2)]
            block = here.enter_context(nc.Block())

            @block.gpsimd
            def _(pool):
                bound, bound_c = pool.to_reg(P * g.width - 1), pool.to_reg(P - 1)

                def gather(t, i, s):
                    pool.wait_ge(ready, t + 1)
                    pool.sem_inc(begun, 1)
                    for n, (table, last) in enumerate(((self.state_dram[g.name], bound), (self.carry_dram[g.name], bound_c))):
                        pool.indirect_dma_start(out=st[:, s, n, :], out_offset=None, in_=table[:, :],
                                                in_offset=bass.IndirectOffsetOnAxis(ap=idx[:, s, n:n + 1], axis=0),
                                                bounds_check=last, oob_is_err=False).then_inc(got[s], 16)
                in_pairs(pool, NT, gather)

            @block.scalar
            def _(act):
                def step(t, i, s):
                    act.wait_ge(shift_ready, t + 1)
                    act.activation(d[:, s, 0:parts, :], d[:, s, 0:parts, :], ACT.Exp).then_inc(exp_ready, 1)
                in_pairs(act, NT, step)

            @block.vector
            def _(dve):
                def prefill(t, s):
                    dve.memset(st[:, s, :, 0:C + H], 0.0)
                    dve.memset(st[:, s, :, C + H:S], NEG)
                    dve.tensor_copy(idx[:, s, 0:1], self.end_at[g.name][:, bass.ds(t, 1)])
                    dve.tensor_copy(idx[:, s, 1:2], self.carry_at[g.name][:, bass.ds(t, 1)]).then_inc(ready, 1)
                prefill(0, 0)
                prefill(1, 1)

                def head_view(ap):
                    return ap.rearrange("p (h k) -> p h k", k=K)

                def step(t, i, s):
                    at = bass.ds(t, 1)
                    dve.drain()
                    dve.wait_ge(got[s], i * 32 + 32)
                    m0, m1 = st[:, s, 0, C + H:S], st[:, s, 1, C + H:S]
                    dve.tensor_tensor(mstar[:, :], m0, m1, ALU.max)
                    dve.drain()
                    if own is not None:
                        own_m = own[1][:, at, :].rearrange("p a h -> p (a h)")
                        dve.tensor_tensor(mstar[:, :], mstar[:, :], own_m, ALU.max)
                        dve.drain()
                        dve.tensor_tensor(d[:, s, 2, :], own_m, mstar[:, :], ALU.subtract)
                    dve.tensor_tensor(d[:, s, 0, :], m0, mstar[:, :], ALU.subtract)
                    dve.tensor_tensor(d[:, s, 1, :], m1, mstar[:, :], ALU.subtract)
                    dve.drain()
                    dve.sem_inc(shift_ready, 1)
                    dve.wait_ge(exp_ready, t + 1)
                    dve.tensor_tensor(head_view(ya[:, :]), head_view(st[:, s, 0, 0:C]), heads(d[:, s, 0, :], K), ALU.mult)
                    dve.tensor_tensor(head_view(yb[:, :]), head_view(st[:, s, 1, 0:C]), heads(d[:, s, 1, :], K), ALU.mult)
                    dve.tensor_tensor(den2[:, 0, :], st[:, s, 0, C:C + H], d[:, s, 0, :], ALU.mult)
                    dve.tensor_tensor(den2[:, 1, :], st[:, s, 1, C:C + H], d[:, s, 1, :], ALU.mult)
                    dve.drain()
                    dve.tensor_tensor(ya[:, :], ya[:, :], yb[:, :], ALU.add)
                    dve.tensor_tensor(den[:, :], den2[:, 0, :], den2[:, 1, :], ALU.add)
                    dve.drain()
                    if own is not None:
                        own_h = own[0][:, at, :].rearrange("p a c -> p (a c)")
                        dve.tensor_tensor(head_view(yb[:, :]), head_view(own_h), heads(d[:, s, 2, :], K), ALU.mult)
                        dve.tensor_tensor(den[:, :], den[:, :], d[:, s, 2, :], ALU.add)
                        dve.drain()
                        dve.tensor_tensor(ya[:, :], ya[:, :], yb[:, :], ALU.add)
                        dve.tensor_scalar(den[:, :], den[:, :], 1e-16, None, ALU.add)
                    else:
                        dve.tensor_scalar(den[:, :], den[:, :], 1e-16, None, ALU.max)
                    dve.drain()
                    dve.reciprocal(den[:, :], den[:, :])
                    dve.drain()
                    if own is None:
                        dve.tensor_tensor(head_view(ya[:, :]), head_view(ya[:, :]), heads(den[:, :], K), ALU.mult)
                        dve.drain()
                        x = self.X[:, at, :].rearrange("p a d -> p (a d)")
                        dve.tensor_tensor(x, x, ya[:, :], ALU.add)
                    else:
                        dve.tensor_tensor(head_view(agg[:, at, :].rearrange("p a c -> p (a c)")), head_view(ya[:, :]),
                                          heads(den[:, :], K), ALU.mult)
                    if not (isinstance(t, int) and t == NT - 1):
                        prefill(t + 2, s)
                in_pairs(dve, NT, step)

    def project_ffn(self, own_h, own_m, xt_all):
        nc, io = self.nc, self.io
        C = FFN.cols
        ident = self.ident
        with ExitStack() as here:
            mean, rstd = self.norm_stats(here)
            att = self.sb(here, "att", [C, 2 * H])
            w = self.sb(here, "w_ffn", [P, 2, C + 2 * H])
            wt = self.sb(here, "w_turned_sb", [C, 2, P])
            (xn, xt, rows, own) = self.several(
                here, "row_parts",
                [P, 2, D],
                [P, 2, 2, P],
                [P, 2, C + 2 * H],
                [P, NT, H])
            tp, pz, pw = self.ps(here, "tp", [P, 2, 512]), self.ps(here, "pz", [P, 2, 512]), self.ps(here, "pw", [P, 512])
            names = ("att_clear", "w_loaded", "w_turned", "wt_ready", "w_made", "w_ready", "xn_ready", "turned", "xt_ready",
                     "projected", "evac")
            (att_clear, w_loaded, w_turned, wt_ready, w_made, w_ready, xn_ready, turned, xt_ready, projected, evac) = \
                (self.sem(here, n) for n in names)
            stored = [self.sem(here, f"stored{s}") for s in range(2)]
            block = here.enter_context(nc.Block())

            @block.sync
            def _(sp):
                sp.dma_start(w[:, :, 0:C], io["L0_ffn_W_gat"].rearrange("(k p) c -> p k c", p=P)).then_inc(w_loaded, 16)
                sp.wait_ge(att_clear, 1)
                for side, name in enumerate(("L0_ffn_att_src", "L0_ffn_att_dst")):
                    for h in range(H):
                        sp.dma_start(att[h * EXPERTS:(h + 1) * EXPERTS, side * H + h:side * H + h + 1],
                                     io[name][h, :].rearrange("(e a) -> e a", a=1)).then_inc(w_loaded, 16)
                sp.wait_ge(w_loaded, 144)

                def store(t, i, s):
                    sp.wait_ge(evac, t + 1)
                    sp.dma_start(self.row_dram["ffn"][bass.ds(t * P, P), :], rows[:, s, 0:FFN.row]).then_inc(stored[s], 16)
                in_pairs(sp, NT, store)
                for s in range(2):
                    sp.wait_ge(stored[s], 16 * ((NT + 1 - s) // 2))

            @block.tensor
            def _(pe):
                pe.wait_ge(w_loaded, 144)
                for k in range(2):
                    mm = pe.transpose(tp[0:C, k, 0:P], w[:, k, 0:C], ident[:, :])
                mm.then_inc(w_turned, 1)
                pe.wait_ge(wt_ready, 1)
                for k in range(2):
                    mm = pe.matmul(pw[:, k * 2 * H:(k + 1) * 2 * H], wt[:, k, :], att[:, :], start=True, stop=True)
                mm.then_inc(w_made, 1)
                pe.wait_ge(w_ready, 1)

                def step(t, i, s):
                    pe.wait_ge(xn_ready, t + 1)
                    if not first(i):
                        pe.wait_ge(xt_ready, t - 1)
                    for k in range(2):
                        mm = pe.transpose(tp[:, s, k * P:(k + 1) * P], xn[:, s, k * P:(k + 1) * P], ident[:, :])
                    mm.then_inc(turned, 1)
                    pe.wait_ge(xt_ready, t + 1)
                    if not first(i):
                        pe.wait_ge(evac, t - 1)
                    for k in range(2):
                        mm = pe.matmul(pz[:, s, 0:C + 2 * H], xt[:, s, k, :], w[:, k, :], start=(k == 0), stop=(k == 1))
                    mm.then_inc(projected, 1)
                in_pairs(pe, NT, step)

            @block.scalar
            def _(act):
                act.wait_ge(w_turned, 1)
                for k in range(2):
                    ins = act.activation(wt[:, k, :], tp[0:C, k, 0:P], ACT.Copy)
                ins.then_inc(wt_ready, 1)
                act.wait_ge(w_made, 1)
                for k in range(2):
                    ins = act.activation(w[:, k, C:C + 2 * H], pw[:, k * 2 * H:(k + 1) * 2 * H], ACT.Copy)
                ins.then_inc(w_ready, 1)

                def step(t, i, s):
                    act.wait_ge(turned, t + 1)
                    if not first(i):
                        act.wait_ge(projected, t - 1)
                    act.activation(xt[:, s, :, :].rearrange("p k n -> p (k n)"), tp[:, s, 0:D], ACT.Copy).then_inc(xt_ready, 1)
                    act.activation(xt_all[:, :, bass.ds(t * P, P)], tp[:, s, 0:D].rearrange("p (k n) -> p k n", k=2), ACT.Copy)
                    act.wait_ge(projected, t + 1)
                    if not first(i):
                        act.wait_ge(stored[s], i * 16)
                    act.activation(rows[:, s, :], pz[:, s, 0:C + 2 * H], ACT.Copy)
                    flat = "p a h -> p (a h)"
                    act.activation(own_h[:, bass.ds(t, 1), :].rearrange(flat), pz[:, s, 0:C], ACT.Copy)
                    act.activation(own[:, bass.ds(t, 1), :].rearrange(flat), pz[:, s, C:C + H], ACT.Copy)
                    act.activation(self.ed["ffn"][:, bass.ds(t, 1), :].rearrange(flat), pz[:, s, C + H:C + 2 * H], ACT.Copy) \
                       .then_inc(evac, 1)
                in_pairs(act, NT, step)

            @block.vector
            def _(dve):
                dve.memset(att[:, :], 0.0).then_inc(att_clear, 1)

                def step(t, i, s):
                    if not first(i):
                        dve.wait_ge(turned, t - 1)
                    dve.tensor_scalar(xn[:, s, :], self.X[:, bass.ds(t, 1), :].rearrange("p a d -> p (a d)"),
                                      mean[:, bass.ds(t, 1)], rstd[:, bass.ds(t, 1)], ALU.subtract, ALU.mult) \
                       .then_inc(xn_ready, 1)
                in_pairs(dve, NT, step)
                dve.wait_ge(evac, NT)
                dve.tensor_tensor(own[:, :, :], own[:, :, :], self.ed["ffn"][:, :, :], ALU.add)
                dve.drain()
                dve.scalar_tensor_tensor(own_m[:, :, :], own[:, :, :], FFN.slope, own[:, :, :], ALU.mult, ALU.max)

    def route(self, agg, gate):
        nc, io = self.nc, self.io
        C = FFN.cols
        with ExitStack() as here:
            (par, y, sq, mean, var, std, eps, sc, rank, cmp, tops, is_top, ex, ws) = self.several(
                here, "route_parts",
                [P, 3, C],
                [P, NT, C],
                [P, NT, C],
                [P, NT],
                [P, NT],
                [P, NT],
                [P, 1],
                [P, NT, EXPERTS],
                [P, NT, EXPERTS],
                [P, NT, EXPERTS],
                [P, 2, NT],
                [P, 2, NT, EXPERTS],
                [P, NT],
                [P, 2, NT])
            par_in, var_ready, std_ready, diff_ready, ex_ready = \
                (self.sem(here, n) for n in ("par_in", "var_ready", "std_ready", "diff_ready", "ex_ready"))
            block = here.enter_context(nc.Block())

            @block.sync
            def _(sp):
                for n, name in enumerate(("L0_ffn_b_gat", "L0_ffn_ln_gamma", "L0_ffn_ln_beta")):
                    sp.dma_start(par[:, n, :], io[name].partition_broadcast(P)).then_inc(par_in, 16)

            @block.scalar
            def _(act):
                act.wait_ge(var_ready, 1)
                act.activation(std[:, :], var[:, :], ACT.Sqrt, bias=eps[:, 0:1], scale=1.0 / C).then_inc(std_ready, 1)
                act.wait_ge(diff_ready, 1)
                act.activation(ex[:, :], ex[:, :], ACT.Exp).then_inc(ex_ready, 1)

            @block.vector
            def _(dve):
                def op(call, *args):
                    call(*args)
                    dve.drain()

                def over_nodes(ap):
                    return ap.unsqueeze(1).to_broadcast([P, NT, C])

                def over(ap, n):
                    return ap.unsqueeze(2).to_broadcast([P, NT, n])
                dve.memset(eps[:, :], EPS)
                dve.wait_ge(par_in, 48)
                op(dve.tensor_tensor, y[:, :, :], agg[:, 0:NT, :], over_nodes(par[:, 0, :]), ALU.add)
                op(dve.tensor_reduce, mean[:, :], y[:, :, :], AX, ALU.add)
                op(dve.tensor_scalar, mean[:, :], mean[:, :], 1.0 / C, None, ALU.mult)
                op(dve.tensor_tensor, y[:, :, :], y[:, :, :], over(mean[:, :], C), ALU.subtract)
                op(dve.tensor_tensor, sq[:, :, :], y[:, :, :], y[:, :, :], ALU.mult)
                dve.tensor_reduce(var[:, :], sq[:, :, :], AX, ALU.add).then_inc(var_ready, 1)
                dve.wait_ge(std_ready, 1)
                op(dve.reciprocal, std[:, :], std[:, :])
                op(dve.tensor_tensor, y[:, :, :], y[:, :, :], over(std[:, :], C), ALU.mult)
                op(dve.tensor_tensor, y[:, :, :], y[:, :, :], over_nodes(par[:, 1, :]), ALU.mult)
                op(dve.tensor_tensor, y[:, :, :], y[:, :, :], over_nodes(par[:, 2, :]), ALU.add)
                op(dve.tensor_tensor, sc[:, :, :], y[:, :, 0:EXPERTS], y[:, :, EXPERTS:2 * EXPERTS], ALU.add)
                for h in range(2, H):
                    op(dve.tensor_tensor, sc[:, :, :], sc[:, :, :], y[:, :, h * EXPERTS:(h + 1) * EXPERTS], ALU.add)
                op(dve.tensor_scalar, sc[:, :, :], sc[:, :, :], 1.0 / H, None, ALU.mult)
                op(dve.memset, rank[:, :, :], 0.0)
                for a in range(EXPERTS):
                    for lo, hi, rel in ((0, a, ALU.is_gt), (a + 1, EXPERTS, ALU.is_ge)):
                        if lo < hi:
                            op(dve.tensor_tensor, cmp[:, :, lo:hi], over(sc[:, :, a], hi - lo), sc[:, :, lo:hi], rel)
                            op(dve.tensor_tensor, rank[:, :, lo:hi], rank[:, :, lo:hi], cmp[:, :, lo:hi], ALU.add)
                for k in range(2):
                    op(dve.tensor_scalar, is_top[:, k, :, :], rank[:, :, :], float(k), None, ALU.is_equal)
                    op(dve.tensor_tensor, cmp[:, :, :], is_top[:, k, :, :], sc[:, :, :], ALU.mult)
                    op(dve.tensor_reduce, tops[:, k, :], cmp[:, :, :], AX, ALU.add)
                dve.tensor_tensor(ex[:, :], tops[:, 1, :], tops[:, 0, :], ALU.subtract).then_inc(diff_ready, 1)
                dve.wait_ge(ex_ready, 1)
                op(dve.tensor_scalar, ws[:, 0, :], ex[:, :], 1.0, None, ALU.add)
                op(dve.reciprocal, ws[:, 0, :], ws[:, 0, :])
                op(dve.tensor_tensor, ws[:, 1, :], ws[:, 0, :], ex[:, :], ALU.mult)
                op(dve.tensor_tensor, gate[:, :, :], is_top[:, 0, :, :], over(ws[:, 0, :], EXPERTS), ALU.mult)
                op(dve.tensor_tensor, cmp[:, :, :], is_top[:, 1, :, :], over(ws[:, 1, :], EXPERTS), ALU.mult)
                op(dve.tensor_tensor, gate[:, :, :], gate[:, :, :], cmp[:, :, :], ALU.add)

    def store_x(self):
        nc = self.nc
        with ExitStack() as here:
            stored = self.sem(here, "stored")
            block = here.enter_context(nc.Block())

            @block.sync
            def _(sp):
                sp.dma_start(self.x1_dram.rearrange("(t p) d -> p t d", p=P), self.X[:, :, :]).then_inc(stored, 16)
                sp.wait_ge(stored, 16)

    def run(self, out):
        def begin(part):
            self.part = part
        with self.keep:
            begin("setup")
            self.setup()
            self.x1_dram, self.y_dram = self.dram("x1", [NPAD, D]), self.dram("y", [NPAD, EXPERTS, D])
            with ExitStack() as with_x:
                self.load_x(with_x)
                begin("project")
                self.project()
            begin("segments_gnn")
            self.segments(GNN, self.io["dst"])
            begin("segments_ffn")
            self.segments(FFN, self.io["L0_ffn_edge_index"][1, :])
            with ExitStack() as mine:
                begin("sort")
                self.sort_columns(mine)
                begin("starts_gnn")
                self.starts(GNN, mine)
                fin, finm = self.several(mine, "last_states", [P, GNN.cols + H], [P, H])
                begin("iotas")
                self.gnn_and_sort(fin, finm)
                begin("carry_gnn")
                self.carry(GNN, fin, finm)
            with ExitStack() as later:
                own_h, own_m, agg, gate = self.several(
                    later, "by_node",
                    [P, NT, FFN.cols],
                    [P, NT, H],
                    [P, NT, FFN.cols],
                    [P, NT, EXPERTS])
                begin("ffn")
                xt_all = self.sb(later, "xt_all", [P, 2, NPAD])
                with ExitStack() as with_x:
                    begin("x_again")
                    self.load_x(with_x)
                    begin("mix")
                    self.mix()
                    begin("nodes_gnn")
                    self.gather_nodes(GNN)
                    begin("project_ffn")
                    self.project_ffn(own_h, own_m, xt_all)
                    begin("x_stored")
                    self.store_x()
                with ExitStack() as mine:
                    begin("starts_ffn")
                    self.starts(FFN, mine)
                    fin, finm = self.several(mine, "last_states", [P, FFN.cols + H], [P, H])
                    begin("stage2")
                    self.ffn_and_experts(fin, finm, xt_all)
                    begin("carry_ffn")
                    self.carry(FFN, fin, finm)
                begin("nodes_ffn")
                self.gather_nodes(FFN, (own_h, own_m), agg)
                begin("route")
                self.route(agg, gate)
                begin("combine")
                self.combine(gate, out)


_INS = ['x', 'src', 'dst', 'L0_gnn_W', 'L0_gnn_att', 'L0_mix_Wqkv', 'L0_mix_Wout', 'L0_mix_gamma', 'L0_ffn_W_gat',
        'L0_ffn_att_src', 'L0_ffn_att_dst', 'L0_ffn_b_gat', 'L0_ffn_ln_gamma', 'L0_ffn_ln_beta', 'L0_ffn_W1',
        'L0_ffn_b1', 'L0_ffn_W2', 'L0_ffn_b2', 'L0_ffn_edge_index']


def kernel(**inputs):
    import numpy as _np
    import concourse.bacc as _bacc
    from concourse import mybir as _mybir
    from concourse.bass_utils import run_bass_kernel_spmd as _run

    nc = _bacc.Bacc("TRN2", target_bir_lowering=False, num_devices=1)
    arrays, io = {}, {}
    for name in _INS:
        a = _np.ascontiguousarray(inputs[name])
        arrays[f"in_{name}_dram"] = a
        io[name] = nc.dram_tensor(f"in_{name}_dram", a.shape, _mybir.dt.from_np(a.dtype), kind="ExternalInput").ap()
    out = nc.dram_tensor("out_0_dram", (N, D), _mybir.dt.float32, kind="ExternalOutput").ap()
    Kernel(nc, io).run(out)
    r = _run(nc, [arrays], core_ids=[0])
    return r.results[0]["out_0_dram"]
```

```python
from contextlib import ExitStack

import concourse.bass as bass
from concourse import mybir

P = 128
N = 6250
NT = (N + P - 1) // P
NPAD = NT * P
LAST = N - (NT - 1) * P
D = 256
H = 4
EPS = 1e-5
NEG = -1.0e30
NOWHERE = 1 << 20
HIS = 64

MIX_HEADS, MIX_DIM = 8, 32
EXPERTS, HIDDEN = 4, 512
FFN_BLOCK = 7
F32 = mybir.dt.float32
BF16 = mybir.dt.bfloat16
FP16 = mybir.dt.float16
I32 = mybir.dt.int32
ALU = mybir.AluOpType
ACT = mybir.ActivationFunctionType
AX = mybir.AxisListType.X


class Graph:

    def __init__(self, name, edges, width, chunk, cols, slope):
        self.name, self.edges, self.width, self.chunk, self.cols, self.slope = name, edges, width, chunk, cols, slope
        self.per_head = cols // H
        self.chunks = width // chunk
        self.row = cols + H
        self.state = cols + 2 * H
        assert width % chunk == 0 and self.chunks % 2 == 0 and P * width >= edges


GNN = Graph("gnn", 100000, 784, 14, 256, 0.01)
FFN = Graph("ffn", 131072, 1024, 16, 16, 0.2)
SORT_BLOCKS = P
SORT_TILES = FFN.width // P
PUT_TILES = 2


def first(i):
    return isinstance(i, int) and i == 0


def in_pairs(eng, count, step):
    for s in range(2):
        step(s, 0, s)
    with eng.Fori(1, count // 2) as i:
        for s in range(2):
            step(i * 2 + s, i, s)
    if count % 2:
        step(count - 1, count // 2, 0)


def in_two_stages(eng, count, front, back):
    def step(t, i, s):
        front(t, i, s)
        if not first(t):
            back(t - 1, i - 1 if s == 0 else i, 1 - s)
    in_pairs(eng, count, step)
    back(count - 1, (count - 1) // 2, (count - 1) % 2)


def tile_rows(t):
    return LAST if isinstance(t, int) and t == NT - 1 else P


def heads(ap, per_head):
    return ap.unsqueeze(2).to_broadcast([P, H, per_head])


class Kernel:
    def __init__(self, nc, io):
        self.nc, self.io = nc, io
        self.keep = ExitStack()
        self.scratch, self.sems = {}, {}
        self.part = "all"

    def sb(self, stack, name, shape, dt=F32):
        return stack.enter_context(self.nc.sbuf_tensor(f"{self.part}_{name}", list(shape), dt))

    def several(self, stack, name, *shapes):
        sizes = [1] * len(shapes)
        for n, shape in enumerate(shapes):
            for d in shape[1:]:
                sizes[n] *= d
        whole, at, views = self.sb(stack, name, [P, sum(sizes)]), 0, []
        for shape, size in zip(shapes, sizes):
            view = whole[0:shape[0], at:at + size]
            if len(shape) == 3:
                view = view.rearrange("p (a b) -> p a b", b=shape[2])
            elif len(shape) == 4:
                view = view.rearrange("p (a b c) -> p a b c", b=shape[2], c=shape[3])
            views.append(view)
            at += size
        return views

    def ps(self, stack, name, shape, dt=F32):
        return stack.enter_context(self.nc.psum_tensor(f"{self.part}_{name}", list(shape), dt))

    def sem(self, stack, name):
        sem = self.nc.alloc_semaphore(f"{self.part}_{name}")
        if stack not in self.sems:
            self.sems[stack] = []
            stack.callback(self.clear_sems, stack)
        self.sems[stack].append(sem)
        return sem

    def clear_sems(self, stack):
        self.nc.clear_and_free_semaphores(self.sems.pop(stack))
        self.nc.all_engine_barrier()

    def dram(self, name, shape, dt=F32):
        t = self.nc.dram_tensor(name, list(shape), dt, kind="Internal").ap()
        self.scratch[name] = t
        return t

    def setup(self):
        nc, io, keep = self.nc, self.io, self.keep
        self.ident = self.sb(keep, "ident", [P, P])
        self.ones = self.sb(keep, "ones", [P, P])
        self.below = self.sb(keep, "below", [P, P])
        self.ed = {g.name: self.sb(keep, f"ed_{g.name}", [P, NT, H]) for g in (GNN, FFN)}
        self.seg_at = {g.name: self.sb(keep, f"seg_at_{g.name}", [P, NT + 1], I32) for g in (GNN, FFN)}
        self.end_at = {g.name: self.sb(keep, f"end_at_{g.name}", [P, NT + 7], I32) for g in (GNN, FFN)}
        self.carry_at = {g.name: self.sb(keep, f"carry_at_{g.name}", [P, NT + 7], I32) for g in (GNN, FFN)}
        self.base_ffn = self.sb(keep, "base_ffn", [P, HIS])
        self.counts = {g.name: self.sb(keep, f"counts_{g.name}", [P, HIS]) for g in (GNN, FFN)}
        self.edge_src = {g.name: self.sb(keep, f"src_{g.name}", [P, g.width + 2 * g.chunk], I32)
                         for g in (GNN, FFN)}
        self.row_dram = {"gnn": self.dram("gnn_rows", [NPAD, GNN.row]), "ffn": self.dram("ffn_rows", [NPAD, FFN.row])}
        self.qkv_dram = self.dram("qkv", [NPAD, 3 * D])
        self.seg_dram = {g.name: self.dram(f"seg_{g.name}", [P * g.width, 1 + H]) for g in (GNN, FFN)}
        self.state_dram = {g.name: self.dram(f"state_{g.name}", [P * g.width, g.state]) for g in (GNN, FFN)}
        self.carry_dram = {g.name: self.dram(f"carry_{g.name}", [P, g.state]) for g in (GNN, FFN)}
        self.lo_dram = self.dram("dst_lo", [P, FFN.width], I32)
        self.sorted_dram = self.dram("sorted_src", [P * FFN.width, 1], I32)
        self.kmax = self.sb(keep, "kmax", [P, D])
        ident, ones, below = self.ident, self.ones, self.below

        with ExitStack() as here:
            block = here.enter_context(nc.Block())

            @block.gpsimd
            def _(pool):
                pool.memset(ident[:, :], 0.0)
                pool.memset(ones[:, :], 1.0)
                pool.drain()
                pool.affine_select(out=ident[:, :], in_=ident[:, :], compare_op=ALU.not_equal, fill=1.0,
                                   base=0, pattern=[[-1, P]], channel_multiplier=1)
                pool.affine_select(out=below[:, :], in_=ones[:, :], compare_op=ALU.is_gt, fill=0.0,
                                   base=0, pattern=[[1, P]], channel_multiplier=-1)

            @block.vector
            def _(dve):
                for g in (GNN, FFN):
                    dve.memset(self.edge_src[g.name][:, :], 0)
                    dve.memset(self.end_at[g.name][:, NT:NT + 7], NOWHERE)
                    dve.memset(self.carry_at[g.name][:, NT:NT + 7], NOWHERE)

    def load_x(self, stack):
        nc, x = self.nc, self.io["x"]
        self.X = self.sb(stack, "X", [P, NT, D])
        X = self.X
        with ExitStack() as here:
            cleared, loaded = self.sem(here, "cleared"), self.sem(here, "loaded")
            block = here.enter_context(nc.Block())

            @block.vector
            def _(dve):
                dve.memset(X[:, NT - 1, :], 0.0).then_inc(cleared, 1)

            @block.sync
            def _(sp):
                sp.dma_start(X[:, 0:NT - 1, :], x[0:(NT - 1) * P, :].rearrange("(t p) d -> p t d", p=P)).then_inc(loaded, 16)
                sp.wait_ge(cleared, 1)
                sp.dma_start(X[0:LAST, NT - 1, :], x[(NT - 1) * P:N, :]).then_inc(loaded, 16)
                sp.wait_ge(loaded, 32)

    def counting_parts(self, g, dst, stack):
        W = g.width
        U = 16
        full = g.edges // W
        padding = g.edges != P * W
        loads = 4 if padding else 1
        dst_i = self.sb(stack, "dst_i", [P, W], I32)
        part_i = self.sb(stack, "part_i", [P, W], I32)
        lo, hi = self.sb(stack, "lo", [P, W], BF16), self.sb(stack, "hi", [P, W], BF16)
        iota_i = self.sb(stack, "iota_i", [P, P], I32)
        iota = self.sb(stack, "iota", [P, P], BF16)
        oh_lo, oh_hi = self.sb(stack, "oh_lo", [P, 2, U, P], BF16), self.sb(stack, "oh_hi", [P, 2, U, HIS], BF16)
        hist = self.ps(stack, "hist", [P, 512])
        names = ("padded", "dst_loaded", "iota_made", "hot", "counted", "lo_ready", "lo_stored")
        padded, loaded, iota_made, hot, counted, lo_ready, lo_stored = (self.sem(stack, n) for n in names)

        class Steps:
            groups = W // U

            def sp_load(sp):
                if padding:
                    sp.dma_start(self.edge_src[g.name][0:full, 0:W],
                                 self.io["src"][0:full * W].rearrange("(p w) -> p w", w=W)).then_inc(loaded, 16)
                    sp.dma_start(self.edge_src[g.name][full:full + 1, 0:g.edges - full * W],
                                 self.io["src"][full * W:g.edges].rearrange("(p w) -> p w", p=1)).then_inc(loaded, 16)
                    sp.wait_ge(padded, 1)
                    sp.dma_start(dst_i[0:full, :], dst[0:full * W].rearrange("(p w) -> p w", w=W)).then_inc(loaded, 16)
                    sp.dma_start(dst_i[full:full + 1, 0:g.edges - full * W],
                                 dst[full * W:g.edges].rearrange("(p w) -> p w", p=1)).then_inc(loaded, 16)
                else:
                    sp.dma_start(dst_i[:, :], dst.rearrange("(p w) -> p w", w=W)).then_inc(loaded, 16)

            def sp_end(sp, store_lo):
                sp.wait_ge(loaded, 16 * loads)
                if store_lo:
                    sp.wait_ge(lo_ready, 1)
                    sp.dma_start(self.lo_dram[:, :], part_i[:, :]).then_inc(lo_stored, 16)
                    sp.wait_ge(lo_stored, 16)

            def pool_iota(pool):
                pool.iota(iota_i[:, :], pattern=[[1, P]], base=0, channel_multiplier=0)
                pool.drain()
                pool.tensor_copy(iota[:, :], iota_i[:, :]).then_inc(iota_made, 1)

            def pe_count(pe, n, i, s):
                pe.wait_ge(hot, n + 1)
                for u in range(U):
                    mm = pe.matmul(hist[:, 0:HIS], oh_lo[:, s, u, :], oh_hi[:, s, u, :],
                                   start=(first(n) and u == 0), stop=False, skip_group_check=True)
                mm.then_inc(counted, 1)

            def dve_pad(dve):
                if padding:
                    dve.memset(dst_i[:, :], HIS * P - 1).then_inc(padded, 1)

            def dve_split(dve):
                dve.wait_ge(loaded, 16 * loads)
                dve.tensor_scalar(part_i[:, :], dst_i[:, :], 7, None, ALU.logical_shift_right)
                dve.drain()
                dve.tensor_copy(hi[:, :], part_i[:, :])
                dve.drain()
                dve.tensor_scalar(part_i[:, :], dst_i[:, :], P - 1, None, ALU.bitwise_and).then_inc(lo_ready, 1)
                dve.drain()
                dve.tensor_copy(lo[:, :], part_i[:, :])
                dve.drain()
                dve.wait_ge(iota_made, 1)

            def dve_hot(dve, n, i, s):
                if not first(i):
                    dve.wait_ge(counted, n - 1)
                for out, part, size in ((oh_lo, lo, P), (oh_hi, hi, HIS)):
                    ins = dve.tensor_tensor(out[:, s, :, :], iota[:, 0:size].unsqueeze(1).to_broadcast([P, U, size]),
                                            part[:, bass.ds(n * U, U)].unsqueeze(2).to_broadcast([P, U, size]),
                                            ALU.is_equal)
                ins.then_inc(hot, 1)

            def dve_take(dve):
                dve.wait_ge(counted, W // U)
                dve.tensor_copy(self.counts[g.name][:, :], hist[:, 0:HIS])
        return Steps

    def count_ffn(self):
        nc = self.nc
        with ExitStack() as here:
            count = self.counting_parts(FFN, self.io["L0_ffn_edge_index"][1, :], here)
            block = here.enter_context(nc.Block())

            @block.sync
            def _(sp):
                count.sp_load(sp)
                count.sp_end(sp, True)

            @block.gpsimd
            def _(pool):
                count.pool_iota(pool)

            @block.tensor
            def _(pe):
                in_pairs(pe, count.groups, lambda n, i, s: count.pe_count(pe, n, i, s))

            @block.vector
            def _(dve):
                count.dve_pad(dve)
                count.dve_split(dve)
                in_pairs(dve, count.groups, lambda n, i, s: count.dve_hot(dve, n, i, s))
                count.dve_take(dve)

    def segments(self, g):
        nc = self.nc
        W = g.width
        cnt = self.counts[g.name]
        with ExitStack() as here:
            (tot, run, base, nz, end, t1, t2, q1, q2) = self.several(
                here, "nodes_small",
                [P, HIS],
                [P, HIS],
                [P, NT],
                [P, NT],
                [P, NT],
                [P, NT],
                [P, NT],
                [P, NT],
                [P, NT])
            qi = self.sb(here, "qi", [P, NT], I32)
            pre, total = self.ps(here, "pre", [P, HIS]), self.ps(here, "total", [P, HIS])
            prefixed = self.sem(here, "prefixed")
            block = here.enter_context(nc.Block())

            @block.tensor
            def _(pe):
                pe.matmul(pre[:, :], self.below[:, :], cnt[:, :], start=True, stop=True)
                pe.matmul(total[:, :], self.ones[:, :], cnt[:, :], start=True, stop=True).then_inc(prefixed, 1)

            @block.vector
            def _(dve):
                dve.wait_ge(prefixed, 1)
                dve.tensor_copy(tot[:, :], total[:, :])
                dve.drain()
                dve.tensor_tensor_scan(run[:, :], self.ones[:, 0:HIS], tot[:, :], 0.0, ALU.mult, ALU.add)
                dve.drain()
                dve.tensor_tensor(run[:, :], run[:, :], tot[:, :], ALU.subtract)
                dve.drain()
                dve.tensor_tensor(run[:, :], run[:, :], pre[:, :], ALU.add)
                dve.drain()
                if g is FFN:
                    dve.tensor_copy(self.base_ffn[:, :], run[:, :])
                dve.tensor_copy(base[:, :], run[:, 0:NT])
                dve.tensor_scalar(nz[:, :], cnt[:, 0:NT], 1.0, None, ALU.min)
                dve.tensor_tensor(end[:, :], run[:, 0:NT], cnt[:, 0:NT], ALU.add)
                dve.drain()
                dve.tensor_scalar(end[:, :], end[:, :], -1.0, 0.0, ALU.add, ALU.max)
                dve.drain()

                def row_of(q, x):
                    dve.tensor_scalar(t1[:, :], x[:, :], 1.0 / W, None, ALU.mult)
                    dve.drain()
                    dve.tensor_copy(qi[:, :], t1[:, :])
                    dve.drain()
                    dve.tensor_copy(q[:, :], qi[:, :])
                    dve.drain()
                    dve.scalar_tensor_tensor(t1[:, :], q[:, :], -float(W), x[:, :], ALU.mult, ALU.add)
                    dve.drain()
                    dve.tensor_scalar(t2[:, :], t1[:, :], 0.0, None, ALU.is_lt)
                    dve.tensor_scalar(t1[:, :], t1[:, :], float(W), None, ALU.is_ge)
                    dve.drain()
                    dve.tensor_tensor(t1[:, :], t1[:, :], t2[:, :], ALU.subtract)
                    dve.drain()
                    dve.tensor_tensor(q[:, :], q[:, :], t1[:, :], ALU.add)
                    dve.drain()

                def index(out, value, valid):
                    dve.tensor_tensor(t1[:, :], value[:, :], valid[:, :], ALU.mult)
                    dve.tensor_scalar(t2[:, :], valid[:, :], -float(NOWHERE), float(NOWHERE), ALU.mult, ALU.add)
                    dve.drain()
                    dve.tensor_tensor(t1[:, :], t1[:, :], t2[:, :], ALU.add)
                    dve.drain()
                    dve.tensor_copy(out[:, 0:NT], t1[:, :])
                    dve.drain()

                row_of(q1, base)
                row_of(q2, end)
                index(self.seg_at[g.name], base, nz)
                index(self.end_at[g.name], end, nz)
                dve.tensor_tensor(q1[:, :], q2[:, :], q1[:, :], ALU.is_gt)
                dve.drain()
                dve.tensor_tensor(nz[:, :], nz[:, :], q1[:, :], ALU.mult)
                dve.drain()
                index(self.carry_at[g.name], q2, nz)

    def norm_stats(self, stack):
        nc = self.nc
        mean = self.sb(stack, "mean", [P, NT])
        rstd = self.sb(stack, "rstd", [P, NT])
        with ExitStack() as here:
            (mv, st, mv7, eps, std) = self.several(
                here, "stat_parts",
                [P, NT, 2],
                [P, 7, 6],
                [P, 7, 2],
                [P, 1],
                [P, NT])
            stats_done, root_done = self.sem(here, "stats_done"), self.sem(here, "root_done")
            block = here.enter_context(nc.Block())

            @block.vector
            def _(dve):
                dve.memset(eps[:, :], EPS)
                with dve.Fori(0, NT // 7) as i:
                    for u in range(7):
                        dve.bn_stats(st[:, u, :], self.X[:, bass.ds(i * 7 + u, 1), :].rearrange("p a d -> p (a d)"))
                    dve.drain()
                    for u in range(7):
                        dve.bn_aggr(mv7[:, u, :], st[:, u, :])
                    dve.drain()
                    dve.tensor_copy(mv[:, bass.ds(i * 7, 7), :], mv7[:, :, :])
                    dve.drain()
                dve.tensor_copy(mean[:, :], mv[:, :, 0]).then_inc(stats_done, 1)
                dve.wait_ge(root_done, 1)
                dve.reciprocal(rstd[:, :], std[:, :])

            @block.scalar
            def _(act):
                act.wait_ge(stats_done, 1)
                act.activation(std[:, :], mv[:, :, 1], ACT.Sqrt, bias=eps[:, 0:1]).then_inc(root_done, 1)
        return mean, rstd

    def project(self):
        nc, io = self.nc, self.io
        ident, ones = self.ident, self.ones
        kmax = self.kmax
        with ExitStack() as here:
            mean, rstd = self.norm_stats(here)
            w_rows = self.sb(here, "w_rows", [P, 2, D])
            att = self.sb(here, "att", [P, 2, 2 * H])
            wz = self.sb(here, "wz", [P, 2, D + 2 * H])
            wqkv = self.sb(here, "wqkv", [P, 2, 3 * D])
            (xn, xt) = self.several(
                here, "turned_rows",
                [P, 2, D],
                [P, 2, 2, P])
            (z_row, qkv, km) = self.several(
                here, "kmax_parts",
                [P, 2, D + 2 * H],
                [P, 2, 3 * D],
                [P, D])
            kcol = self.sb(here, "kcol", [P, 2])
            kdiag = self.sb(here, "kdiag", [P, 2, P])
            tp = self.ps(here, "tp", [P, 2, 512])
            pz, pqk = self.ps(here, "pz", [P, 2, 512]), self.ps(here, "pqk", [P, 2, 512])
            pv = self.ps(here, "pv", [P, 512])
            count = self.counting_parts(GNN, io["dst"], here)
            assert count.groups == NT
            names = ("att_clear", "w_loaded", "w_turned", "w_ready", "xn_ready", "turned", "xt_ready", "projected",
                     "z_evac", "qk_evac", "km_ready", "k_turned", "k_diag", "k_spread")
            (att_clear, w_loaded, w_turned, w_ready, xn_ready, turned, xt_ready, projected,
             z_evac, qk_evac, km_ready, k_turned, k_diag, k_spread) = (self.sem(here, n) for n in names)
            z_out = [self.sem(here, f"z_out{s}") for s in range(2)]
            qkv_out = [self.sem(here, f"qkv_out{s}") for s in range(2)]
            block = here.enter_context(nc.Block())

            @block.sync
            def _(sp):
                count.sp_load(sp)
                sp.dma_start(w_rows[:, :, :], io["L0_gnn_W"].rearrange("h o i -> (h o) i").rearrange("(k p) i -> p k i", p=P)) \
                  .then_inc(w_loaded, 16)
                sp.dma_start(wqkv[:, :, :], io["L0_mix_Wqkv"].rearrange("(k p) c -> p k c", p=P)).then_inc(w_loaded, 16)
                sp.wait_ge(att_clear, 1)
                for h in range(H):
                    rows = slice(64 * (h % 2), 64 * (h % 2) + 64)
                    for side in range(2):
                        sp.dma_start(att[rows, h // 2, side * H + h:side * H + h + 1],
                                     io["L0_gnn_att"][h, 64 * side:64 * side + 64].rearrange("(o a) -> o a", a=1)) \
                          .then_inc(w_loaded, 16)
                sp.wait_ge(w_loaded, 160)

                def store(t, i, s):
                    sp.wait_ge(z_evac, t + 1)
                    sp.dma_start(self.row_dram["gnn"][bass.ds(t * P, P), :], z_row[:, s, 0:GNN.row]).then_inc(z_out[s], 16)
                    sp.wait_ge(qk_evac, t + 1)
                    sp.dma_start(self.qkv_dram[bass.ds(t * P, P), :], qkv[:, s, :]).then_inc(qkv_out[s], 16)
                in_pairs(sp, NT, store)
                count.sp_end(sp, False)
                for s in range(2):
                    sp.wait_ge(z_out[s], 16 * ((NT + 1 - s) // 2))
                    sp.wait_ge(qkv_out[s], 16 * ((NT + 1 - s) // 2))

            @block.gpsimd
            def _(pool):
                count.pool_iota(pool)

            @block.tensor
            def _(pe):
                pe.wait_ge(w_loaded, 160)
                for k in range(2):
                    for r in range(2):
                        pe.transpose(pz[:, k, r * P:(r + 1) * P], w_rows[:, r, k * P:(k + 1) * P], ident[:, :])
                for k in range(2):
                    for r in range(2):
                        mm = pe.matmul(pqk[:, k, 0:2 * H], w_rows[:, r, k * P:(k + 1) * P], att[:, r, :],
                                       start=(r == 0), stop=(r == 1))
                mm.then_inc(w_turned, 1)
                pe.wait_ge(w_ready, 1)

                def turn(t, i, s):
                    pe.wait_ge(xn_ready, t + 1)
                    if not first(i):
                        pe.wait_ge(xt_ready, t - 1)
                    for k in range(2):
                        mm = pe.transpose(tp[:, s, k * P:(k + 1) * P], xn[:, s, k * P:(k + 1) * P], ident[:, :])
                    mm.then_inc(turned, 1)

                def products(t, i, s):
                    count.pe_count(pe, t, i, s)
                    pe.wait_ge(xt_ready, t + 1)
                    if not first(i):
                        pe.wait_ge(z_evac, t - 1)
                        pe.wait_ge(qk_evac, t - 1)
                    for k in range(2):
                        pe.matmul(pz[:, s, 0:D + 2 * H], xt[:, s, k, :], wz[:, k, :], start=(k == 0), stop=(k == 1))
                    for k in range(2):
                        pe.matmul(pqk[:, s, :], xt[:, s, k, :], wqkv[:, k, 0:2 * D], start=(k == 0), stop=(k == 1))
                    if not first(t):
                        pe.wait_ge(z_evac, t)
                    for k in range(2):
                        mm = pe.matmul(pv[:, 0:D], xt[:, s, k, :], wqkv[:, k, 2 * D:3 * D], start=(k == 0), stop=(k == 1))
                    mm.then_inc(projected, 1)
                in_two_stages(pe, NT, turn, products)
                pe.wait_ge(km_ready, 1)
                for k in range(2):
                    mm = pe.transpose(tp[:, k, 0:P], km[:, k * P:(k + 1) * P], ident[:, :])
                mm.then_inc(k_turned, 1)
                pe.wait_ge(k_diag, 1)
                pe.wait_ge(z_evac, NT)
                for k in range(2):
                    mm = pe.matmul(pz[:, 0, k * P:(k + 1) * P], ones[:, :], kdiag[:, k, :], start=True, stop=True)
                mm.then_inc(k_spread, 1)

            @block.scalar
            def _(act):
                act.wait_ge(w_turned, 1)
                for k in range(2):
                    act.activation(wz[:, k, 0:D], pz[:, k, 0:D], ACT.Copy)
                    ins = act.activation(wz[:, k, D:D + 2 * H], pqk[:, k, 0:2 * H], ACT.Copy)
                ins.then_inc(w_ready, 1)

                def copy_turned(t, i, s):
                    act.wait_ge(turned, t + 1)
                    if not first(i):
                        act.wait_ge(projected, t - 1)
                    act.activation(xt[:, s, :, :].rearrange("p k n -> p (k n)"), tp[:, s, 0:D], ACT.Copy).then_inc(xt_ready, 1)

                def copy_products(t, i, s):
                    act.wait_ge(projected, t + 1)
                    if not first(i):
                        act.wait_ge(z_out[s], i * 16)
                        act.wait_ge(qkv_out[s], i * 16)
                    act.activation(z_row[:, s, :], pz[:, s, 0:D + 2 * H], ACT.Copy)
                    act.activation(self.ed["gnn"][:, bass.ds(t, 1), :].rearrange("p a h -> p (a h)"),
                                   pz[:, s, D + H:D + 2 * H], ACT.Copy)
                    act.activation(qkv[:, s, 2 * D:3 * D], pv[:, 0:D], ACT.Copy).then_inc(z_evac, 1)
                in_two_stages(act, NT, copy_turned, copy_products)

            @block.vector
            def _(dve):
                dve.memset(att[:, :, :], 0.0).then_inc(att_clear, 1)
                dve.memset(km[:, :], NEG)
                count.dve_pad(dve)
                count.dve_split(dve)

                def normalise(t, i, s):
                    if not first(i):
                        dve.wait_ge(turned, t - 1)
                    dve.tensor_scalar(xn[:, s, :], self.X[:, bass.ds(t, 1), :].rearrange("p a d -> p (a d)"),
                                      mean[:, bass.ds(t, 1)], rstd[:, bass.ds(t, 1)], ALU.subtract, ALU.mult) \
                       .then_inc(xn_ready, 1)
                    count.dve_hot(dve, t, i, s)

                def take_products(t, i, s):
                    dve.drain()
                    dve.wait_ge(projected, t + 1)
                    if not first(i):
                        dve.wait_ge(qkv_out[s], i * 16)
                    rows = tile_rows(t)
                    dve.tensor_tensor(km[0:rows, :], km[0:rows, :], pqk[0:rows, s, D:2 * D], ALU.max)
                    dve.tensor_copy(qkv[:, s, 0:2 * D], pqk[:, s, :]).then_inc(qk_evac, 1)
                in_two_stages(dve, NT, normalise, take_products)
                count.dve_take(dve)
                dve.drain()
                dve.sem_inc(km_ready, 1)
                dve.wait_ge(k_turned, 1)
                dve.tensor_reduce(kcol[:, :], tp[:, :, 0:P], AX, ALU.max)
                dve.drain()
                for k in range(2):
                    ins = dve.tensor_scalar(kdiag[:, k, :], ident[:, :], kcol[:, k:k + 1], None, ALU.mult)
                ins.then_inc(k_diag, 1)
                dve.wait_ge(k_spread, 1)
                dve.tensor_copy(kmax[:, :], pz[:, 0, 0:D])

    def mix(self, room):
        nc, io = self.nc, self.io
        ident, ones, kmax = self.ident, self.ones, self.kmax
        SCALE = MIX_DIM ** -0.5
        G = 7
        groups = NT // G
        assert groups * G == NT
        out = room.rearrange("p k n -> p (k n)").rearrange("p (t d) -> p t d", d=D)
        with ExitStack() as here:
            (loaded, made, wout, gamma, bmask, ctx, rden, cw, qt, mx, sm, st, mv, mv7, std, eps) = self.several(
                here, "mix_parts",
                [P, 2, G * 2 * D],
                [P, 2, G * D],
                [P, 2, D],
                [P, D],
                [P, P],
                [P, 2, P],
                [P, 2],
                [P, 2, D],
                [P, 2, D],
                [P, 2, G * MIX_HEADS],
                [P, 2, G * MIX_HEADS],
                [P, G, 6],
                [P, NT, 2],
                [P, G, 2],
                [P, NT],
                [P, 1])
            pc = [self.ps(here, f"pc{j}", [P, 512]) for j in range(2)]
            pd = [self.ps(here, f"pd{j}", [P, 512]) for j in range(2)]
            pt, pm = self.ps(here, "pt", [P, 2, 512]), self.ps(here, "pm", [P, 2, 512])
            names = ("w_loaded", "shifted", "k_exp", "summed", "ctx_ready", "cw_made", "cw_ready", "q_shifted", "q_exp",
                     "q_ready", "q_turned", "qt_ready", "mixed", "mix_evac", "var_ready", "std_ready")
            (w_loaded, shifted, k_exp, summed, ctx_ready, cw_made, cw_ready, q_shifted, q_exp,
             q_ready, q_turned, qt_ready, mixed, mix_evac, var_ready, std_ready) = (self.sem(here, n) for n in names)
            kv_in = [self.sem(here, f"kv_in{s}") for s in range(2)]
            q_in = [self.sem(here, f"q_in{s}") for s in range(2)]
            block = here.enter_context(nc.Block())

            def kv(s):
                return loaded[:, s, :].rearrange("p (t d) -> p t d", d=2 * D)

            def tiles(tensor, s):
                return tensor[:, s, :].rearrange("p (t d) -> p t d", d=D)

            def q(s):
                return loaded[:, s, 0:G * D]

            def rows_of(g):
                return bass.ds(g * (G * P), G * P)

            def row(tensor, t):
                return tensor[:, bass.ds(t, 1), :].rearrange("p a d -> p (a d)")

            @block.sync
            def _(sp):
                sp.dma_start(wout[:, :, :], io["L0_mix_Wout"].rearrange("(k p) c -> p k c", p=P)).then_inc(w_loaded, 16)
                sp.dma_start(gamma[:, :], io["L0_mix_gamma"].partition_broadcast(P)).then_inc(w_loaded, 16)

                def load_kv(g, i, s):
                    if not first(i):
                        sp.wait_ge(summed, g - 1)
                    sp.dma_start(kv(s), self.qkv_dram[rows_of(g), D:3 * D].rearrange("(t p) d -> p t d", p=P)) \
                      .then_inc(kv_in[s], 16)
                in_pairs(sp, groups, load_kv)

                def load_q(g, i, s):
                    if first(i):
                        sp.wait_ge(summed, groups - (groups - 1 + s) % 2)
                    else:
                        sp.wait_ge(q_shifted, g - 1)
                    sp.dma_start(tiles(loaded[:, :, 0:G * D], s), self.qkv_dram[rows_of(g), 0:D]
                                 .rearrange("(t p) d -> p t d", p=P)).then_inc(q_in[s], 16)
                in_pairs(sp, groups, load_q)

            @block.tensor
            def _(pe):
                def context(g, i, s):
                    pe.wait_ge(k_exp, g + 1)
                    for u in range(G):
                        head = first(g) and u == 0
                        tail = isinstance(g, int) and g == groups - 1 and u == G - 1
                        rows = LAST if tail else P
                        for j in range(2):
                            cols = slice(j * P, (j + 1) * P)
                            pe.matmul(pc[j][:, 0:P], kv(s)[0:rows, u, D + j * P:D + (j + 1) * P], tiles(made, s)[0:rows, u, cols],
                                      start=head, stop=tail, skip_group_check=True)
                            mm = pe.matmul(pd[j][:, 0:1], tiles(made, s)[0:rows, u, cols], ones[0:rows, 0:1],
                                           start=head, stop=tail, skip_group_check=True)
                    mm.then_inc(summed, 1)
                in_pairs(pe, groups, context)
                pe.wait_ge(w_loaded, 32)
                pe.wait_ge(ctx_ready, 1)
                for j in range(2):
                    mm = pe.matmul(pm[:, j, 0:D], ctx[:, j, :], wout[:, j, :], start=True, stop=True)
                mm.then_inc(cw_made, 1)
                pe.wait_ge(cw_ready, 1)

                def rows_out(g, i, s):
                    def turn(u):
                        for j in range(2):
                            mm = pe.transpose(pt[:, (s + u) % 2, j * P:(j + 1) * P], tiles(made, s)[:, u, j * P:(j + 1) * P],
                                              ident[:, :])
                        mm.then_inc(q_turned, 1)
                    pe.wait_ge(q_ready, g + 1)
                    turn(0)
                    for u in range(G):
                        t, slot = g * G + u, (s + u) % 2
                        if u < G - 1:
                            turn(u + 1)
                        pe.wait_ge(qt_ready, t + 1)
                        if not (first(g) and u < 2):
                            pe.wait_ge(mix_evac, t - 1)
                        for j in range(2):
                            mm = pe.matmul(pm[:, slot, 0:D], qt[:, slot, j * P:(j + 1) * P], cw[:, j, :],
                                           start=(j == 0), stop=(j == 1))
                        mm.then_inc(mixed, 1)
                in_pairs(pe, groups, rows_out)

            @block.scalar
            def _(act):
                def exp_k(g, i, s):
                    act.wait_ge(shifted, g + 1)
                    act.activation(made[:, s, :], made[:, s, :], ACT.Exp).then_inc(k_exp, 1)
                in_pairs(act, groups, exp_k)

                def copies(g, s):
                    for u in range(G):
                        t, slot = g * G + u, (s + u) % 2
                        act.wait_ge(q_turned, t + 1)
                        if not (first(g) and u < 2):
                            act.wait_ge(mixed, t - 1)
                        act.activation(qt[:, slot, :], pt[:, slot, 0:D], ACT.Copy).then_inc(qt_ready, 1)
                        act.wait_ge(mixed, t + 1)
                        act.activation(row(out, t), pm[:, slot, 0:D], ACT.Copy).then_inc(mix_evac, 1)

                def step(g, i, s):
                    act.wait_ge(q_shifted, g + 1)
                    act.activation(made[:, s, :], made[:, s, :], ACT.Exp).then_inc(q_exp, 1)
                    if not first(g):
                        copies(g - 1, 1 - s)
                in_pairs(act, groups, step)
                copies(groups - 1, (groups - 1) % 2)
                act.wait_ge(var_ready, 1)
                act.activation(std[:, :], mv[:, :, 1], ACT.Sqrt, bias=eps[:, 0:1]).then_inc(std_ready, 1)

            @block.vector
            def _(dve):
                dve.memset(eps[:, :], EPS)
                dve.memset(bmask[:, :], 0.0)
                dve.drain()
                for a in range(P // MIX_DIM):
                    b = slice(a * MIX_DIM, (a + 1) * MIX_DIM)
                    dve.memset(bmask[b, b], 1.0)

                def shift_k(g, i, s):
                    dve.wait_ge(kv_in[s], i * 16 + 16)
                    if not first(i):
                        dve.wait_ge(summed, g - 1)
                    dve.tensor_tensor(tiles(made, s), kv(s)[:, :, 0:D], kmax[:, :].unsqueeze(1).to_broadcast([P, G, D]),
                                      ALU.subtract).then_inc(shifted, 1)
                in_pairs(dve, groups, shift_k)
                dve.wait_ge(summed, groups)
                for j in range(2):
                    dve.tensor_tensor(ctx[:, j, :], pc[j][:, 0:P], bmask[:, :], ALU.mult)
                    ins = dve.reciprocal(rden[:, j:j + 1], pd[j][:, 0:1])
                ins.then_inc(ctx_ready, 1)
                dve.drain()
                dve.wait_ge(cw_made, 1)
                for j in range(2):
                    ins = dve.tensor_scalar(cw[:, j, :], pm[:, j, 0:D], rden[:, j:j + 1], SCALE, ALU.mult, ALU.mult)
                ins.then_inc(cw_ready, 1)

                def by_head(ap):
                    return ap.rearrange("p (h d) -> p h d", d=MIX_DIM)

                def each(ap):
                    return ap.unsqueeze(2).to_broadcast([P, G * MIX_HEADS, MIX_DIM])

                def shift_q(g, i, s):
                    dve.wait_ge(q_in[s], i * 16 + 16)
                    dve.tensor_reduce(mx[:, s, :], by_head(q(s)), AX, ALU.max)
                    dve.drain()
                    if not first(i):
                        dve.wait_ge(q_turned, g * G - G)
                    dve.tensor_tensor(by_head(made[:, s, :]), by_head(q(s)), each(mx[:, s, :]), ALU.subtract) \
                       .then_inc(q_shifted, 1)

                def normalise_q(g, s):
                    dve.wait_ge(q_exp, g + 1)
                    dve.tensor_reduce(sm[:, s, :], by_head(made[:, s, :]), AX, ALU.add)
                    dve.drain()
                    dve.reciprocal(sm[:, s, :], sm[:, s, :])
                    dve.drain()
                    dve.tensor_tensor(by_head(made[:, s, :]), by_head(made[:, s, :]), each(sm[:, s, :]), ALU.mult) \
                       .then_inc(q_ready, 1)

                def stats(g):
                    dve.wait_ge(mix_evac, g * G + G)
                    for u in range(G):
                        dve.bn_stats(st[:, u, :], row(out, g * G + u))
                    dve.drain()
                    for u in range(G):
                        dve.bn_aggr(mv7[:, u, :], st[:, u, :])
                    dve.drain()
                    dve.tensor_copy(mv[:, bass.ds(g * G, G), :], mv7[:, :, :])
                    dve.drain()

                def step(g, i, s):
                    shift_q(g, i, s)
                    if not first(g):
                        normalise_q(g - 1, 1 - s)
                    if not first(i):
                        stats(g - 2)
                in_pairs(dve, groups, step)
                normalise_q(groups - 1, (groups - 1) % 2)
                stats(groups - 2)
                stats(groups - 1)
                dve.sem_inc(var_ready, 1)
                dve.wait_ge(std_ready, 1)
                dve.reciprocal(std[:, :], std[:, :])
                dve.wait_ge(w_loaded, 32)
                dve.drain()
                with dve.Fori(0, groups) as g:
                    for u in range(G):
                        t = g * G + u
                        dve.tensor_scalar(row(out, t), row(out, t), mv[:, bass.ds(t, 1), 0], std[:, bass.ds(t, 1)],
                                          ALU.subtract, ALU.mult)
                    dve.drain()
                    block7 = out[:, bass.ds(g * G, G), :]
                    dve.tensor_tensor(block7, block7, gamma[:, :].unsqueeze(1).to_broadcast([P, G, D]), ALU.mult)
                    dve.drain()
                    x7 = self.X[:, bass.ds(g * G, G), :]
                    dve.tensor_tensor(x7, x7, block7, ALU.add)

    def sort_columns(self, stack):
        nc, io = self.nc, self.io
        W, T = FFN.width, SORT_TILES
        ident = self.ident
        dst, src = io["L0_ffn_edge_index"][1, :], io["L0_ffn_edge_index"][0, :]
        flat = "p a b -> p (a b)"
        self.dcol, self.src_lo, self.src_hi = self.several(stack, "columns", [P, T, P], [P, T, P], [P, T, P])
        self.lo, self.hi = self.sb(stack, "lo", [P, T, P], BF16), self.sb(stack, "hi", [P, T, P], BF16)
        dcol, src_lo, src_hi, lo, hi = self.dcol, self.src_lo, self.src_hi, self.lo, self.hi
        with ExitStack() as here:
            raw, rawf = self.sb(here, "raw", [P, W], I32), self.sb(here, "rawf", [P, W])
            di, hif = self.sb(here, "di", [P, W], I32), self.sb(here, "hif", [P, W])
            tp = self.ps(here, "tp", [P, 2, 512])
            names = ("raw_loaded", "raw_ready", "raw_turned", "cols_ready")
            raw_loaded, raw_ready, raw_turned, cols_ready = (self.sem(here, n) for n in names)
            block = here.enter_context(nc.Block())

            @block.sync
            def _(sp):
                sp.dma_start(raw[:, :], dst.rearrange("(p w) -> p w", w=W)).then_inc(raw_loaded, 16)
                sp.wait_ge(raw_ready, 1)
                sp.dma_start(raw[:, :], src.rearrange("(p w) -> p w", w=W)).then_inc(raw_loaded, 16)

            @block.tensor
            def _(pe):
                for n in range(2):
                    pe.wait_ge(raw_ready, n + 1)
                    for j in range(T):
                        mm = pe.transpose(tp[:, j // 4, (j % 4) * P:(j % 4 + 1) * P], rawf[:, j * P:(j + 1) * P], ident[:, :])
                    mm.then_inc(raw_turned, 1)

            @block.vector
            def _(dve):
                turned = tp[:, :, :].rearrange(flat)
                dve.wait_ge(raw_loaded, 16)
                dve.tensor_copy(rawf[:, :], raw[:, :]).then_inc(raw_ready, 1)
                dve.wait_ge(raw_turned, 1)
                dve.tensor_copy(dcol[:, :, :].rearrange(flat), turned)
                dve.tensor_copy(di[:, :], turned)
                dve.drain()
                dve.tensor_scalar(di[:, :], di[:, :], 7, None, ALU.logical_shift_right)
                dve.drain()
                dve.tensor_copy(hif[:, :], di[:, :])
                dve.drain()
                dve.tensor_copy(hi[:, :, :].rearrange(flat), hif[:, :])
                dve.scalar_tensor_tensor(lo[:, :, :].rearrange(flat), hif[:, :], -float(P),
                                         dcol[:, :, :].rearrange(flat), ALU.mult, ALU.add)
                dve.wait_ge(raw_loaded, 32)
                dve.tensor_scalar(rawf[:, :], raw[:, :], float(N - 1), None, ALU.min).then_inc(raw_ready, 1)
                dve.wait_ge(raw_turned, 2)
                dve.tensor_copy(di[:, :], turned)
                dve.tensor_copy(src_lo[:, :, :].rearrange(flat), turned)
                dve.drain()
                dve.tensor_scalar(di[:, :], di[:, :], (HIS - 1) * P, None, ALU.bitwise_and)
                dve.drain()
                dve.tensor_copy(src_hi[:, :, :].rearrange(flat), di[:, :])
                dve.drain()
                dve.tensor_tensor(src_lo[:, :, :].rearrange(flat), src_lo[:, :, :].rearrange(flat),
                                  src_hi[:, :, :].rearrange(flat), ALU.subtract)


    def sort_parts(self, stack):
        nc, io = self.nc, self.io
        W, T = FFN.width, SORT_TILES
        assert W == 1 << 10
        dst = io["L0_ffn_edge_index"][1, :]
        dcol, src_lo, src_hi, lo, hi = self.dcol, self.src_lo, self.src_hi, self.lo, self.hi
        iota_w, iota_b, minus_p, earlier = self.iota_w, self.iota_b, self.minus_p, self.earlier
        (oht, intra, slot, to_p, to_w, free_sb, looked) = self.several(
            stack, "sort_small",
            [P, 2, W],
            [P, 2, T],
            [P, 2, T],
            [P, PUT_TILES],
            [P, PUT_TILES],
            [P, 2, HIS],
            [P, T, HIS])
        row_d, row_lo = self.sb(stack, "row_d", [P, 2, W], I32), self.sb(stack, "row_lo", [P, 2, W], I32)
        oh_lo, oh_hi = self.sb(stack, "oh_lo", [P, 2, T, P], BF16), self.sb(stack, "oh_hi", [P, 2, T, HIS], BF16)
        equal = self.sb(stack, "equal", [P, T, P], BF16)
        pos_i, part_i, low_i = (self.sb(stack, n, [P, PUT_TILES], I32) for n in ("pos_i", "part_i", "low_i"))
        S, Q = T - PUT_TILES, PUT_TILES
        oh_w = self.sb(stack, "oh_w", [P, 2 * Q, W], FP16)
        oh_p, put_lo, put_hi = (self.sb(stack, n, [P, 2 * Q, P], FP16) for n in ("oh_p", "put_lo", "put_hi"))
        away_at, away_src = self.sb(stack, "away_at", [P, 2, S], I32), self.sb(stack, "away_src", [P, 2, S], I32)
        free = self.ps(stack, "free", [P, 512])
        at = self.ps(stack, "at", [P, 2, T, HIS])
        placed = self.ps(stack, "placed", [P, W])
        names = ("hot", "oht_ready", "table_ready", "looked_up", "table_next", "hot_w", "put_ready", "away_ready",
                 "scatter_begun", "back_in")
        (hot, oht_ready, table_ready, looked_up, table_next, hot_w, put_ready, away_ready, scatter_begun, back_in) = \
            (self.sem(stack, n) for n in names)
        put_done = [self.sem(stack, f"put_done{s}") for s in range(2)]
        scattered = [self.sem(stack, f"scattered{s}") for s in range(2)]
        rows_in = [self.sem(stack, f"rows_in{s}") for s in range(2)]

        class Steps:
            def sp_load(sp, b, i, s):
                if not first(i):
                    sp.wait_ge(hot, b - 1)
                    sp.wait_ge(oht_ready, b - 1)
                sp.dma_start(row_d[:, s, :], dst[bass.ds(b * W, W)].partition_broadcast(P)).then_inc(rows_in[s], 16)
                sp.dma_start(row_lo[:, s, :], self.lo_dram[bass.ds(b, 1), :].rearrange("a w -> (a w)")
                             .partition_broadcast(P)).then_inc(rows_in[s], 16)

            def dve_prepare(dve, b, i, s):
                dve.drain()
                dve.wait_ge(rows_in[s], i * 32 + 32)
                if not first(i):
                    dve.wait_ge(looked_up, b * T - T)
                for out, part, size in ((oh_lo, lo, P), (oh_hi, hi, HIS)):
                    dve.tensor_tensor(out[:, s, :, :], iota_b[:, 0:size].unsqueeze(1).to_broadcast([P, T, size]),
                                      part[:, :, bass.ds(b, 1)].to_broadcast([P, T, size]), ALU.is_equal)
                for j in range(T):
                    ins = dve.scalar_tensor_tensor(equal[:, j, :], row_d[:, s, j * P:(j + 1) * P], dcol[:, j, bass.ds(b, 1)],
                                                   earlier[:, :], ALU.is_equal, ALU.mult, accum_out=intra[:, s, j:j + 1])
                ins.then_inc(hot, 1)

            def act_onehot(act, b, i, s):
                act.wait_ge(rows_in[s], i * 32 + 32)
                if not first(i):
                    act.wait_ge(looked_up, b * T - T)
                act.activation(oht[:, s, :], row_lo[:, s, :], ACT.Square, bias=minus_p[:, 0:1])
                act.drain()
                act.activation(oht[:, s, :], oht[:, s, :], ACT.Relu, scale=-1.0, bias=self.ones[:, 0:1]).then_inc(oht_ready, 1)

            def pe_start(pe):
                pe.matmul(free[:, 0:HIS], self.ident[:, :], self.base_ffn[:, :], start=True, stop=False,
                          skip_group_check=True).then_inc(table_next, 1)

            def pe_rank(pe, b, s):
                pe.wait_ge(hot, b + 1)
                pe.wait_ge(oht_ready, b + 1)
                for j in range(T):
                    pe.wait_ge(table_ready, b * T + (j + 1))
                    pe.matmul(free[:, 0:HIS], oh_lo[:, s, j, :], oh_hi[:, s, j, :], start=False, stop=False,
                              skip_group_check=True).then_inc(table_next, 1)
                    pe.matmul(at[:, s, j, :], oht[:, s, j * P:(j + 1) * P], free_sb[:, j % 2, :],
                              start=True, stop=True, skip_group_check=True).then_inc(looked_up, 1)

            def act_tables(act, b):
                for j in range(T):
                    act.wait_ge(table_next, b * T + (j + 1))
                    act.activation(free_sb[:, j % 2, :], free[:, 0:HIS], ACT.Copy).then_inc(table_ready, 1)

            def dve_positions(dve, b, s, turn):
                dve.wait_ge(looked_up, b * T + T)
                for j in range(T):
                    dve.tensor_tensor_reduce(looked[:, j, :], at[:, s, j, :], oh_hi[:, s, j, :], 1.0, 0.0,
                                             ALU.mult, ALU.add, slot[:, s, j:j + 1])
                dve.drain()
                dve.tensor_tensor(pos_i[:, :], slot[:, s, 0:Q], intra[:, s, 0:Q], ALU.add)
                if not first(turn):
                    dve.wait_ge(scattered[s], turn * (16 * S))
                dve.tensor_tensor(away_at[:, s, :], slot[:, s, Q:T], intra[:, s, Q:T], ALU.add)
                dve.tensor_tensor(away_src[:, s, :], src_lo[:, Q:T, bass.ds(b, 1)].rearrange("p t b -> p (t b)"),
                                  src_hi[:, Q:T, bass.ds(b, 1)].rearrange("p t b -> p (t b)"), ALU.add) \
                   .then_inc(away_ready, 1)
                dve.drain()
                dve.tensor_scalar(part_i[:, :], pos_i[:, :], 10, None, ALU.logical_shift_right)
                dve.tensor_scalar(low_i[:, :], pos_i[:, :], W - 1, None, ALU.bitwise_and)
                dve.drain()
                dve.tensor_copy(to_p[:, :], part_i[:, :])
                dve.tensor_copy(to_w[:, :], low_i[:, :])
                dve.drain()
                if not first(turn):
                    dve.wait_ge(put_done[s], turn)
                for n in range(Q):
                    dve.tensor_scalar(oh_w[:, s * Q + n, :], iota_w[:, :], to_w[:, n:n + 1], None, ALU.is_equal)
                    dve.tensor_scalar(oh_p[:, s * Q + n, :], iota_w[:, 0:P], to_p[:, n:n + 1], None, ALU.is_equal) \
                       .then_inc(hot_w, 1)

            def act_sources(act, b, s):
                for n in range(Q):
                    act.wait_ge(hot_w, b * Q + (n + 1))
                    act.activation(put_hi[:, s * Q + n, :], oh_p[:, s * Q + n, :], ACT.Copy, scale=src_hi[:, n, bass.ds(b, 1)])
                    act.activation(put_lo[:, s * Q + n, :], oh_p[:, s * Q + n, :], ACT.Copy, scale=src_lo[:, n, bass.ds(b, 1)]) \
                       .then_inc(put_ready, 1)

            def pool_scatter(pool, bound, b, s):
                pool.wait_ge(away_ready, b + 1)
                pool.sem_inc(scatter_begun, 1)
                for j in range(S):
                    pool.indirect_dma_start(
                        out=self.sorted_dram[:, :], out_offset=bass.IndirectOffsetOnAxis(ap=away_at[:, s, j:j + 1], axis=0),
                        in_=away_src[:, s, j:j + 1], in_offset=None, bounds_check=bound, oob_is_err=False) \
                        .then_inc(scattered[s], 16)

            def pe_put(pe, b, s, head, tail):
                for n in range(Q):
                    pe.wait_ge(put_ready, b * Q + (n + 1))
                    for half in range(2):
                        cols = slice(half * 512, (half + 1) * 512)
                        pe.matmul(placed[:, cols], put_hi[:, s * Q + n, :], oh_w[:, s * Q + n, cols],
                                  start=(head and n == 0), stop=False, skip_group_check=True)
                        mm = pe.matmul(placed[:, cols], put_lo[:, s * Q + n, :], oh_w[:, s * Q + n, cols],
                                       start=False, stop=(tail and n == Q - 1), skip_group_check=True)
                mm.then_inc(put_done[s], 1)

            def sp_back(sp):
                for s in range(2):
                    sp.wait_ge(scattered[s], SORT_BLOCKS // 2 * (16 * S))
                sp.dma_start(row_d[:, 0, :], self.sorted_dram.rearrange("(p w) a -> p (w a)", w=W)).then_inc(back_in, 16)

            def dve_take(dve):
                for s in range(2):
                    dve.wait_ge(put_done[s], SORT_BLOCKS // 2)
                dve.tensor_copy(row_lo[:, 0, :], placed[:, :])
                dve.wait_ge(back_in, 16)
                dve.drain()
                dve.tensor_tensor(self.edge_src["ffn"][:, 0:W], row_lo[:, 0, :], row_d[:, 0, :], ALU.add)
        return Steps

    def starts(self, g, stack):
        nc = self.nc
        W = g.width
        ident, ones = self.ident, self.ones
        seg_dram = self.seg_dram[g.name]
        neg = self.sb(stack, "neg", [P, W])
        ed = self.sb(stack, "ed_edge", [P, H, W])
        whole, whole_neg = self.sb(stack, "whole", [P, 1]), self.sb(stack, "whole_neg", [P, 1])
        diag = self.sb(stack, "diag", [P, P])
        whole_row = self.sb(stack, "whole_row", [H, P])
        self.neg, self.ed_edge, self.whole_neg = neg, ed, whole_neg
        with ExitStack() as mine:
            (seg_rows, seg, same, last, chain, carry_in, lastt) = self.several(
                mine, "start_parts",
                [P, NT, 1 + H],
                [P, W, 1 + H],
                [P, W],
                [P, H],
                [H, P + 1],
                [P, H],
                [H, P])
            pa, pb = self.ps(mine, "pa", [P, P]), self.ps(mine, "pb", [P, P])
            names = ("zeroed", "cleared", "rows_ready", "scattered", "seg_loaded", "last_ready", "spread", "chained", "turned")
            zeroed, cleared, rows_ready, scattered, seg_loaded, last_ready, spread, chained, turned = \
                (self.sem(mine, n) for n in names)
            block = mine.enter_context(nc.Block())

            @block.sync
            def _(sp):
                sp.wait_ge(zeroed, 1)
                sp.dma_start(seg_dram.rearrange("(p w) c -> p (w c)", w=W), seg[:, :, :].rearrange("p w c -> p (w c)")) \
                  .then_inc(cleared, 16)
                sp.wait_ge(scattered, 16 * NT)
                sp.dma_start(seg[:, :, :].rearrange("p w c -> p (w c)"), seg_dram.rearrange("(p w) c -> p (w c)", w=W)) \
                  .then_inc(seg_loaded, 16)
                sp.wait_ge(seg_loaded, 16)

            @block.gpsimd
            def _(pool):
                bound = pool.to_reg(P * W - 1)
                pool.wait_ge(rows_ready, 1)
                pool.wait_ge(cleared, 16)
                for t in range(NT):
                    pool.indirect_dma_start(
                        out=seg_dram[:, :], out_offset=bass.IndirectOffsetOnAxis(ap=self.seg_at[g.name][:, t:t + 1], axis=0),
                        in_=seg_rows[:, t, :], in_offset=None, bounds_check=bound, oob_is_err=False).then_inc(scattered, 16)
                pool.wait_ge(scattered, 16 * NT)

            @block.vector
            def _(dve):
                dve.memset(seg[:, :, :], 0.0).then_inc(zeroed, 1)
                dve.memset(seg_rows[:, :, 0:1], 1.0)
                dve.tensor_copy(seg_rows[:, :, 1:1 + H], self.ed[g.name][:, :, :]).then_inc(rows_ready, 1)
                dve.wait_ge(seg_loaded, 16)
                dve.tensor_scalar(neg[:, :], seg[:, :, 0], NEG, None, ALU.mult)
                dve.tensor_scalar(same[:, :], seg[:, :, 0], -1.0, 1.0, ALU.mult, ALU.add)
                dve.tensor_reduce(whole[:, :], seg[:, :, 0], AX, ALU.max)
                dve.drain()
                dve.tensor_scalar(whole[:, :], whole[:, :], -1.0, 1.0, ALU.mult, ALU.add)
                for h in range(H):
                    dve.tensor_tensor_scan(ed[:, h, :], same[:, :], seg[:, :, 1 + h], 0.0, ALU.mult, ALU.add)
                dve.drain()
                dve.tensor_copy(last[:, :], ed[:, :, W - 1])
                dve.tensor_scalar(whole_neg[:, :], whole[:, :], -NEG, NEG, ALU.mult, ALU.add)
                dve.tensor_scalar(diag[:, :], ident[:, :], whole[:, 0:1], None, ALU.mult)
                dve.drain()
                dve.sem_inc(last_ready, 1)
                dve.wait_ge(spread, 1)
                dve.tensor_copy(whole_row[:, :], pb[0:H, :])
                dve.tensor_copy(lastt[:, :], pa[0:H, :])
                dve.memset(chain[:, 0:1], 0.0)
                dve.drain()
                dve.tensor_tensor_scan(chain[:, 1:P + 1], whole_row[:, :], lastt[:, :], 0.0, ALU.mult, ALU.add).then_inc(chained, 1)
                dve.wait_ge(turned, 1)
                dve.tensor_copy(carry_in[:, :], pa[:, 0:H])
                dve.drain()
                for h in range(H):
                    dve.tensor_tensor_scan(ed[:, h, :], same[:, :], seg[:, :, 1 + h], carry_in[:, h:h + 1], ALU.mult, ALU.add)

            @block.tensor
            def _(pe):
                pe.wait_ge(last_ready, 1)
                pe.transpose(pa[0:H, :], last[:, :], ident[:, :])
                pe.matmul(pb[0:H, :], ones[:, 0:H], diag[:, :], start=True, stop=True).then_inc(spread, 1)
                pe.wait_ge(chained, 1)
                pe.transpose(pa[:, 0:H], chain[:, 0:P], ident[0:H, 0:H]).then_inc(turned, 1)

    def chunk_parts(self, g, stack, fin, finm):
        W, T, C, R, S, K = g.width, g.chunk, g.cols, g.row, g.state, g.per_head
        neg, ed, src = self.neg, self.ed_edge, self.edge_src[g.name]
        idx = self.sb(stack, "idx", [P, 2, T], I32)
        (e, m, dl, pm, w, r) = self.several(
            stack, "chunk_parts",
            [P, H, T],
            [P, 2, H, T + 1],
            [P, H, T + 1],
            [P, H, T],
            [P, H, T],
            [P, C + H, T + 1])
        got = self.sb(stack, "got", [P, 2, T, R])
        y = self.sb(stack, "y", [P, 2, C + H, T + 1])
        rows = self.sb(stack, "rows", [P, 2, T, S])
        names = ("idx_ready", "gather_begun", "logits_ready", "w_ready", "r_ready", "scanned", "rows_ready")
        idx_ready, gather_begun, logits_ready, w_ready, r_ready, scanned, rows_ready = (self.sem(stack, n) for n in names)
        gathered = [self.sem(stack, f"gathered{s}") for s in range(2)]
        stored = [self.sem(stack, f"stored{s}") for s in range(2)]
        by_part = self.state_dram[g.name].rearrange("(p w) s -> p w s", w=W)

        class Steps:
            def pool_gather(pool, bound, c, s):
                pool.wait_ge(idx_ready, c + 1)
                pool.sem_inc(gather_begun, 1)
                for t in range(T):
                    pool.indirect_dma_start(
                        out=got[:, s, t, :], out_offset=None, in_=self.row_dram[g.name][:, :],
                        in_offset=bass.IndirectOffsetOnAxis(ap=idx[:, s, t:t + 1], axis=0),
                        bounds_check=bound, oob_is_err=False).then_inc(gathered[s], 16)

            def dve_start(dve):
                for s in range(2):
                    dve.tensor_copy(idx[:, s, :], src[:, s * T:(s + 1) * T]).then_inc(idx_ready, 1)
                dve.memset(m[:, 1, :, T:T + 1], NEG)
                dve.memset(dl[:, :, 0:1], NEG)
                dve.memset(y[:, 1, :, T:T + 1], 0.0)
                dve.drain()

            def dve_logits(dve, c, i, s):
                at = bass.ds(c * T, T)
                neg_h = neg[:, at].unsqueeze(1).to_broadcast([P, H, T])
                dve.wait_ge(gathered[s], i * (16 * T) + 16 * T)
                dve.tensor_tensor(e[:, :, :], got[:, s, :, C:C + H].rearrange("p t h -> p h t"), ed[:, :, at], ALU.add)
                if not first(i):
                    dve.wait_ge(rows_ready, c - 1)
                dve.tensor_copy(m[:, s, :, 0:1], m[:, 1 - s, :, T:T + 1])
                dve.drain()
                dve.scalar_tensor_tensor(e[:, :, :], e[:, :, :], g.slope, e[:, :, :], ALU.mult, ALU.max)
                dve.drain()
                for h in range(H):
                    dve.tensor_tensor_scan(m[:, s, h, 1:T + 1], neg[:, at], e[:, h, :], m[:, s, h, 0:1], ALU.add, ALU.max)
                dve.drain()
                dve.tensor_tensor(pm[:, :, :], e[:, :, :], m[:, s, :, 1:T + 1], ALU.subtract)
                dve.tensor_tensor(dl[:, :, 1:T + 1], m[:, s, :, 0:T], neg_h, ALU.add)
                dve.drain()
                dve.tensor_tensor(dl[:, :, 1:T + 1], dl[:, :, 1:T + 1], m[:, s, :, 1:T + 1], ALU.subtract) \
                   .then_inc(logits_ready, 1)
                dve.tensor_copy(y[:, s, :, 0:1], y[:, 1 - s, :, T:T + 1])

            def act_exps(act, c):
                act.wait_ge(logits_ready, c + 1)
                act.activation(w[:, :, :], pm[:, :, :], ACT.Exp).then_inc(w_ready, 1)
                if not (isinstance(c, int) and c == 0):
                    act.wait_ge(scanned, c)
                for h in range(H):
                    act.activation(r[:, h * K:(h + 1) * K, :], dl[:, h, :].unsqueeze(1).to_broadcast([P, K, T + 1]), ACT.Exp)
                act.activation(r[:, C:C + H, :], dl[:, :, :], ACT.Exp).then_inc(r_ready, 1)

            def dve_weigh(dve, c, s):
                dve.wait_ge(w_ready, c + 1)
                for h in range(H):
                    dve.tensor_tensor(y[:, s, h * K:(h + 1) * K, 1:T + 1],
                                      got[:, s, :, h * K:(h + 1) * K].rearrange("p t k -> p k t"),
                                      w[:, h, :].unsqueeze(1).to_broadcast([P, K, T]), ALU.mult)
                dve.tensor_copy(y[:, s, C:C + H, 1:T + 1], w[:, :, :])
                dve.drain()
                dve.tensor_copy(idx[:, s, :], src[:, bass.ds((c + 2) * T, T)]).then_inc(idx_ready, 1)

            def dve_scan(dve, c, s):
                dve.wait_ge(r_ready, c + 1)
                flat = y[:, s, :, :].rearrange("p c t -> p (c t)")
                dve.tensor_tensor_scan(flat, r[:, :, :].rearrange("p c t -> p (c t)"), flat, 0.0, ALU.mult, ALU.add) \
                   .then_inc(scanned, 1)
                dve.drain()

            def act_rows(act, c, i, s):
                act.wait_ge(scanned, c + 1)
                if not first(i):
                    act.wait_ge(stored[s], i * 16)
                act.activation(rows[:, s, :, 0:C + H].rearrange("p t c -> p c t"), y[:, s, :, 1:T + 1], ACT.Copy)
                act.activation(rows[:, s, :, C + H:S].rearrange("p t h -> p h t"), m[:, s, :, 1:T + 1], ACT.Copy) \
                   .then_inc(rows_ready, 1)

            def sp_store(sp, c, s):
                sp.wait_ge(rows_ready, c + 1)
                sp.dma_start(by_part[:, bass.ds(c * T, T), :], rows[:, s, :, :]).then_inc(stored[s], 16)

            def sp_end(sp):
                for s in range(2):
                    sp.wait_ge(stored[s], 16 * (g.chunks // 2))

            def dve_end(dve):
                dve.tensor_copy(fin[:, :], y[:, 1, :, T])
                dve.tensor_copy(finm[:, :], m[:, 1, :, T])
        return Steps

    def carry(self, g, fin, finm):
        nc = self.nc
        C, S, K = g.cols, g.state, g.per_head
        ident, ones, whole_neg, carry_dram = self.ident, self.ones, self.whole_neg, self.carry_dram[g.name]
        with ExitStack() as mine:
            groups = [(a, min(a + P, C)) for a in range(0, C, P)] + [(C, C + H)]
            (mt, ms, wn_row, f0, f1, f1c, diag2, spread_w, acc, keep_row, run, table) = self.several(
                mine, "carry_parts",
                [H, P],
                [H, P + 1],
                [H, P],
                [H, P],
                [H, P],
                [P, H],
                [P, P],
                [H, C + H],
                [P, P],
                [P, P],
                [P, len(groups), P + 1],
                [P, S])
            pa, pb, pc = (self.ps(mine, n, [P, 512]) for n in ("pa", "pb", "pc"))
            names = ("sel_made", "diag_ready", "spread", "max_ready", "f_ready", "f_turned", "fin_ready", "fin_turned", "run_ready",
                     "run_turned", "table_ready", "table_out")
            sel_made, diag_ready, spread, max_ready, f_ready, f_turned, fin_ready, fin_turned, run_ready, run_turned, table_ready, table_out = \
                (self.sem(mine, n) for n in names)
            block = mine.enter_context(nc.Block())

            @block.gpsimd
            def _(pool):
                pool.memset(spread_w[:, :], 1.0)
                pool.drain()
                pool.affine_select(out=spread_w[:, 0:C], in_=spread_w[:, 0:C], compare_op=ALU.is_ge, fill=0.0,
                                   base=0, pattern=[[1, C]], channel_multiplier=-K)
                pool.drain()
                pool.affine_select(out=spread_w[:, 0:C], in_=spread_w[:, 0:C], compare_op=ALU.is_gt, fill=0.0,
                                   base=K, pattern=[[-1, C]], channel_multiplier=K)
                pool.affine_select(out=spread_w[:, C:C + H], in_=spread_w[:, C:C + H], compare_op=ALU.is_equal, fill=0.0,
                                   base=0, pattern=[[1, H]], channel_multiplier=-1).then_inc(sel_made, 1)

            @block.tensor
            def _(pe):
                pe.wait_ge(diag_ready, 1)
                pe.transpose(pa[0:H, 0:P], finm[:, :], ident[:, :])
                pe.matmul(pb[0:H, 0:P], ones[:, 0:H], diag2[:, :], start=True, stop=True).then_inc(spread, 1)
                pe.wait_ge(max_ready, 1)
                pe.transpose(pc[:, 0:H], ms[:, 0:P], ident[0:H, 0:H])
                pe.wait_ge(f_ready, 1)
                pe.transpose(pc[:, H:2 * H], f1[:, :], ident[0:H, 0:H]).then_inc(f_turned, 1)
                pe.wait_ge(sel_made, 1)
                pe.wait_ge(fin_ready, 1)
                for n, (a, b) in enumerate(groups):
                    if n:
                        pe.wait_ge(run_ready, n)
                    pe.transpose(pa[0:b - a, 0:P], fin[:, a:b], ident[:, :])
                    pe.matmul(pb[0:b - a, 0:P], spread_w[:, a:b], f0[:, :], start=True, stop=True).then_inc(fin_turned, 1)
                pe.wait_ge(run_ready, len(groups))
                for n, (a, b) in enumerate(groups):
                    mm = pe.transpose(pc[:, a:b], run[0:b - a, n, 0:P], ident[0:b - a, 0:b - a])
                mm.then_inc(run_turned, 1)

            @block.vector
            def _(dve):
                dve.tensor_scalar(diag2[:, :], ident[:, :], whole_neg[:, 0:1], None, ALU.mult).then_inc(diag_ready, 1)
                dve.memset(ms[:, 0:1], NEG)
                dve.memset(run[:, :, 0:1], 0.0)
                dve.wait_ge(spread, 1)
                dve.tensor_copy(wn_row[:, :], pb[0:H, 0:P])
                dve.tensor_copy(mt[:, :], pa[0:H, 0:P])
                dve.drain()
                dve.tensor_tensor_scan(ms[:, 1:P + 1], wn_row[:, :], mt[:, :], NEG, ALU.add, ALU.max)
                dve.drain()
                dve.tensor_tensor(f1[:, :], mt[:, :], ms[:, 1:P + 1], ALU.subtract)
                dve.tensor_tensor(f0[:, :], ms[:, 0:P], wn_row[:, :], ALU.add)
                dve.drain()
                dve.tensor_tensor(f0[:, :], f0[:, :], ms[:, 1:P + 1], ALU.subtract).then_inc(max_ready, 1)
                dve.wait_ge(f_turned, 1)
                dve.tensor_copy(f1c[:, :], pc[:, H:2 * H])
                dve.tensor_copy(table[:, C + H:S], pc[:, 0:H])
                dve.drain()
                by_head = fin[:, 0:C].rearrange("p (h k) -> p h k", k=K)
                dve.tensor_tensor(by_head, by_head, heads(f1c[:, :], K), ALU.mult)
                dve.tensor_tensor(fin[:, C:C + H], fin[:, C:C + H], f1c[:, :], ALU.mult).then_inc(fin_ready, 1)
                for n, (a, b) in enumerate(groups):
                    dve.wait_ge(fin_turned, n + 1)
                    dve.tensor_copy(acc[0:b - a, :], pa[0:b - a, 0:P])
                    dve.tensor_copy(keep_row[0:b - a, :], pb[0:b - a, 0:P])
                    dve.drain()
                    dve.tensor_tensor_scan(run[0:b - a, n, 1:P + 1], keep_row[0:b - a, :], acc[0:b - a, :], 0.0,
                                           ALU.mult, ALU.add).then_inc(run_ready, 1)
                    dve.drain()
                dve.wait_ge(run_turned, 1)
                dve.tensor_copy(table[:, 0:C + H], pc[:, 0:C + H]).then_inc(table_ready, 1)

            @block.scalar
            def _(act):
                act.wait_ge(max_ready, 1)
                act.activation(f0[:, :], f0[:, :], ACT.Exp)
                act.activation(f1[:, :], f1[:, :], ACT.Exp).then_inc(f_ready, 1)

            @block.sync
            def _(sp):
                sp.wait_ge(table_ready, 1)
                sp.dma_start(carry_dram[:, :], table[:, :]).then_inc(table_out, 16)
                sp.wait_ge(table_out, 16)

    def gnn_and_sort(self, fin, finm):
        nc = self.nc
        W = FFN.width
        steps = SORT_BLOCKS // 2 - 1
        both = GNN.chunks // 2 - 1
        assert 2 * both <= steps
        with ExitStack() as here:
            iota_i, iota_pi = self.sb(here, "iota_i", [P, P], I32), self.sb(here, "iota_pi", [P, 1], I32)
            self.iota_w, self.iota_b = self.sb(here, "iota_w", [P, W], FP16), self.sb(here, "iota_b", [P, P], BF16)
            self.minus_p, self.earlier = self.several(here, "sort_constants", [P, 1], [P, P])
            iota_w = self.iota_w
            with ExitStack() as mine:
                iota_l, nothing = self.sb(mine, "iota_l", [P, W], I32), self.sb(mine, "nothing", [P, W], I32)
                zeroed, cleared = self.sem(mine, "zeroed"), self.sem(mine, "cleared")
                block = mine.enter_context(nc.Block())

                @block.vector
                def _(dve):
                    dve.memset(nothing[:, :], 0).then_inc(zeroed, 1)

                @block.sync
                def _(sp):
                    sp.wait_ge(zeroed, 1)
                    sp.dma_start(self.sorted_dram.rearrange("(p w) a -> p (w a)", w=W), nothing[:, :]).then_inc(cleared, 16)
                    sp.wait_ge(cleared, 16)

                @block.gpsimd
                def _(pool):
                    pool.iota(iota_l[:, :], pattern=[[1, W]], base=0, channel_multiplier=0)
                    pool.iota(iota_pi[:, :], pattern=[[0, 1]], base=0, channel_multiplier=-1)
                    pool.affine_select(out=self.earlier[:, :], in_=self.ones[:, :], compare_op=ALU.is_gt, fill=0.0,
                                       base=0, pattern=[[-1, P]], channel_multiplier=1)
                    pool.drain()
                    pool.tensor_copy(iota_w[:, :], iota_l[:, :])
                    pool.tensor_copy(self.iota_b[:, :], iota_l[:, 0:P])
                    pool.tensor_copy(self.minus_p[:, :], iota_pi[:, :])

            self.part = "stage1"
            edge = self.chunk_parts(GNN, here, fin, finm)
            sort = self.sort_parts(here)
            block = here.enter_context(nc.Block())

            @block.gpsimd
            def _(pool):
                bound, places = pool.to_reg(NPAD - 1), pool.to_reg(P * W - 1)
                for s in range(2):
                    edge.pool_gather(pool, bound, s, s)
                sort.pool_scatter(pool, places, 0, 0)
                edge.pool_gather(pool, bound, 2, 0)
                with pool.Fori(1, both) as i:
                    for s in range(2):
                        k = i * 2 + (s - 1)
                        edge.pool_gather(pool, bound, i * 2 + (s + 1), 1 - s)
                        sort.pool_scatter(pool, places, k * 2 - 1, 1)
                        sort.pool_scatter(pool, places, k * 2, 0)
                edge.pool_gather(pool, bound, GNN.chunks - 1, 1)
                with pool.Fori(2 * both - 1, steps + 1) as k:
                    sort.pool_scatter(pool, places, k * 2 - 1, 1)
                    sort.pool_scatter(pool, places, k * 2, 0)
                sort.pool_scatter(pool, places, SORT_BLOCKS - 1, 1)

            @block.sync
            def _(sp):
                for k in range(2):
                    for s in range(2):
                        sort.sp_load(sp, 2 * k + s, k, s)
                for s in range(2):
                    edge.sp_store(sp, s, s)
                with sp.Fori(1, both + 1) as i:
                    for s in range(2):
                        k = i * 2 + s
                        sort.sp_load(sp, k * 2, k, 0)
                        sort.sp_load(sp, k * 2 + 1, k, 1)
                        edge.sp_store(sp, i * 2 + s, s)
                with sp.Fori(2 * both + 2, steps + 1) as k:
                    sort.sp_load(sp, k * 2, k, 0)
                    sort.sp_load(sp, k * 2 + 1, k, 1)
                edge.sp_end(sp)
                sort.sp_back(sp)

            @block.tensor
            def _(pe):
                sort.pe_start(pe)
                sort.pe_rank(pe, 0, 0)
                sort.pe_rank(pe, 1, 1)
                sort.pe_put(pe, 0, 0, True, False)
                with pe.Fori(1, steps + 1) as k:
                    sort.pe_rank(pe, k * 2, 0)
                    sort.pe_put(pe, k * 2 - 1, 1, False, False)
                    sort.pe_rank(pe, k * 2 + 1, 1)
                    sort.pe_put(pe, k * 2, 0, False, False)
                sort.pe_put(pe, SORT_BLOCKS - 1, 1, False, True)

            @block.scalar
            def _(act):
                def sort_pair(k):
                    sort.act_onehot(act, k * 2, k, 0)
                    sort.act_tables(act, k * 2)
                    sort.act_sources(act, k * 2 - 1, 1)
                    sort.act_onehot(act, k * 2 + 1, k, 1)
                    sort.act_tables(act, k * 2 + 1)
                    sort.act_sources(act, k * 2, 0)
                for s in range(2):
                    sort.act_onehot(act, s, 0, s)
                for s in range(2):
                    sort.act_tables(act, s)
                sort.act_sources(act, 0, 0)
                for c in range(2):
                    edge.act_exps(act, c)
                    edge.act_rows(act, c, 0, c)
                with act.Fori(1, both + 1) as i:
                    for s in range(2):
                        edge.act_exps(act, i * 2 + s)
                        sort_pair(i * 2 + (s - 1))
                        edge.act_rows(act, i * 2 + s, i, s)
                with act.Fori(2 * both + 1, steps + 1) as k:
                    sort_pair(k)
                sort.act_sources(act, SORT_BLOCKS - 1, 1)

            @block.vector
            def _(dve):
                edge.dve_start(dve)
                sort.dve_prepare(dve, 0, 0, 0)
                sort.dve_prepare(dve, 1, 0, 1)
                sort.dve_positions(dve, 0, 0, 0)
                for c in range(2):
                    edge.dve_logits(dve, c, 0, c)
                    edge.dve_weigh(dve, c, c)
                    edge.dve_scan(dve, c, c)

                def two_steps(i):
                    for s in range(2):
                        c, k = i * 2 + s, i * 2 + (s - 1)
                        edge.dve_logits(dve, c, i, s)
                        sort.dve_prepare(dve, k * 2, k, 0)
                        sort.dve_positions(dve, k * 2 - 1, 1, k - 1)
                        edge.dve_weigh(dve, c, s)
                        sort.dve_prepare(dve, k * 2 + 1, k, 1)
                        sort.dve_positions(dve, k * 2, 0, k)
                        edge.dve_scan(dve, c, s)
                two_steps(1)
                with dve.Fori(2, both + 1) as i:
                    two_steps(i)
                edge.dve_end(dve)
                with dve.Fori(2 * both + 1, steps + 1) as k:
                    sort.dve_prepare(dve, k * 2, k, 0)
                    sort.dve_positions(dve, k * 2 - 1, 1, k - 1)
                    sort.dve_prepare(dve, k * 2 + 1, k, 1)
                    sort.dve_positions(dve, k * 2, 0, k)
                sort.dve_positions(dve, SORT_BLOCKS - 1, 1, SORT_BLOCKS // 2 - 1)
                sort.dve_take(dve)

    def ffn_and_experts(self, fin, finm, xt_all):
        nc, io = self.nc, self.io
        FT = HIDDEN // P
        B = FFN_BLOCK
        HALF = B * P // 2
        blocks = NT // B
        EH = FT * 2
        pairs = FFN.chunks // 2
        assert blocks * EXPERTS <= pairs
        with ExitStack() as here:
            w1 = self.sb(here, "w1", [P, EXPERTS, 2, HIDDEN])
            w2 = self.sb(here, "w2", [P, EXPERTS, FT, D])
            b1, b2 = self.sb(here, "b1", [P, EXPERTS, FT]), self.sb(here, "b2", [1, EXPERTS, D])
            hid = self.sb(here, "hid", [P, FT, B * P])
            yrow = self.sb(here, "yrow", [P, 2, B, D])
            ph, po = self.ps(here, "ph", [P, 4, 512]), self.ps(here, "po", [P, 4, 512])
            names = ("w_loaded", "hid_made", "hid_ready", "out_made", "out_used")
            w_loaded, hid_made, hid_ready, out_made, out_used = (self.sem(here, n) for n in names)
            y_out = [self.sem(here, f"y_out{s}") for s in range(2)]
            edge = self.chunk_parts(FFN, here, fin, finm)
            by_tile = self.y_dram.rearrange("(t p) e d -> p t e d", p=P)
            block = here.enter_context(nc.Block())

            def begun(q, e):
                return isinstance(q, int) and q == 0 and e == 0

            def walk(eng, step, rest):
                for e in range(EXPERTS):
                    step(0, e, e)
                with eng.Fori(1, blocks) as b:
                    for e in range(EXPERTS):
                        step(b, e, b * EXPERTS + e)
                if rest is not None:
                    with eng.Fori(blocks * EXPERTS, pairs) as i:
                        rest(i)

            @block.gpsimd
            def _(pool):
                bound = pool.to_reg(NPAD - 1)
                in_pairs(pool, FFN.chunks, lambda c, i, s: edge.pool_gather(pool, bound, c, s))

            @block.sync
            def _(sp):
                for e in range(EXPERTS):
                    sp.dma_start(w1[:, e, :, :], io["L0_ffn_W1"][e, :, :].rearrange("(k p) f -> p k f", p=P)).then_inc(w_loaded, 16)
                    sp.dma_start(w2[:, e, :, :], io["L0_ffn_W2"][e, :, :].rearrange("(f p) d -> p f d", p=P)).then_inc(w_loaded, 16)
                    sp.dma_start(b2[:, e, :], io["L0_ffn_b2"][e, :].rearrange("(a d) -> a d", a=1)).then_inc(w_loaded, 16)
                    for f in range(FT):
                        sp.dma_start(b1[:, e, f:f + 1], io["L0_ffn_b1"][e, f * P:(f + 1) * P].rearrange("(p a) -> p a", a=1)) \
                          .then_inc(w_loaded, 16)

                def step(b, e, q):
                    edge.sp_store(sp, q * 2, 0)
                    edge.sp_store(sp, q * 2 + 1, 1)
                    sp.wait_ge(out_used, q * B + B)
                    sp.dma_start(by_tile[:, bass.ds(b * B, B), e, :], yrow[:, e % 2, :, :]).then_inc(y_out[e % 2], 16)

                def rest(i):
                    edge.sp_store(sp, i * 2, 0)
                    edge.sp_store(sp, i * 2 + 1, 1)
                walk(sp, step, rest)
                edge.sp_end(sp)
                for s in range(2):
                    sp.wait_ge(y_out[s], 16 * blocks * EXPERTS // 2)

            @block.tensor
            def _(pe):
                pe.wait_ge(w_loaded, 16 * EXPERTS * (3 + FT))

                def step(b, e, q):
                    for f in range(FT):
                        for half in range(2):
                            n = f * 2 + half
                            if not (begun(q, e) and n < 4):
                                pe.wait_ge(hid_ready, q * EH + (n - 3))
                            for k in range(2):
                                mm = pe.matmul(ph[:, n % 4, 0:HALF], w1[:, e, k, f * P:(f + 1) * P],
                                               xt_all[:, k, bass.ds(b * (B * P) + half * HALF, HALF)],
                                               start=(k == 0), stop=(k == 1))
                            mm.then_inc(hid_made, 1)
                    pe.wait_ge(hid_ready, q * EH + EH)
                    for t in range(B):
                        slot = (e * B + t) % 4
                        if not (begun(q, e) and t < 4):
                            pe.wait_ge(out_used, q * B + (t - 3))
                        pe.matmul(po[:, slot, 0:D], self.ones[0:1, :], b2[:, e, :], start=True, stop=False)
                        for f in range(FT):
                            mm = pe.matmul(po[:, slot, 0:D], hid[:, f, t * P:(t + 1) * P], w2[:, e, f, :],
                                           start=False, stop=(f == FT - 1))
                        mm.then_inc(out_made, 1)
                walk(pe, step, None)

            @block.scalar
            def _(act):
                act.wait_ge(w_loaded, 16 * EXPERTS * (3 + FT))

                def chunk(c, i, s):
                    edge.act_exps(act, c)
                    edge.act_rows(act, c, i, s)

                def step(b, e, q):
                    chunk(q * 2, q, 0)
                    if not begun(q, e):
                        act.wait_ge(out_made, q * B)
                    for f in range(FT):
                        for half in range(2):
                            n = f * 2 + half
                            act.wait_ge(hid_made, q * EH + (n + 1))
                            act.activation(hid[:, f, half * HALF:(half + 1) * HALF], ph[:, n % 4, 0:HALF],
                                           ACT.Gelu, bias=b1[:, e, f:f + 1]).then_inc(hid_ready, 1)
                    chunk(q * 2 + 1, q, 1)

                def rest(i):
                    chunk(i * 2, i, 0)
                    chunk(i * 2 + 1, i, 1)
                walk(act, step, rest)

            @block.vector
            def _(dve):
                def chunk(c, i, s):
                    edge.dve_logits(dve, c, i, s)
                    edge.dve_weigh(dve, c, s)
                    edge.dve_scan(dve, c, s)
                edge.dve_start(dve)

                def step(b, e, q):
                    chunk(q * 2, q, 0)
                    chunk(q * 2 + 1, q, 1)
                    if not (isinstance(q, int) and q < 2):
                        dve.wait_ge(y_out[e % 2], (b * (EXPERTS // 2) + e // 2) * 16)
                    for t in range(B):
                        dve.wait_ge(out_made, q * B + (t + 1))
                        dve.tensor_copy(yrow[:, e % 2, t, :], po[:, (e * B + t) % 4, 0:D]).then_inc(out_used, 1)

                def rest(i):
                    chunk(i * 2, i, 0)
                    chunk(i * 2 + 1, i, 1)
                walk(dve, step, rest)
                edge.dve_end(dve)

    def combine(self, gate, out):
        nc = self.nc
        B = FFN_BLOCK
        blocks = NT // B
        with ExitStack() as here:
            x, y = self.sb(here, "x", [P, 2, B, D]), self.sb(here, "y", [P, 2, B, EXPERTS, D])
            ready = self.sem(here, "ready")
            loaded, stored = [self.sem(here, f"loaded{s}") for s in range(2)], [self.sem(here, f"stored{s}") for s in range(2)]
            block = here.enter_context(nc.Block())
            x_view = self.x1_dram.rearrange("(t p) d -> p t d", p=P)
            y_view = self.y_dram.rearrange("(t p) e d -> p t (e d)", p=P)

            @block.sync
            def _(sp):
                for b in range(blocks):
                    s = b % 2
                    if b >= 2:
                        sp.wait_ge(stored[s], 16 * (b // 2))
                    tiles = slice(b * B, (b + 1) * B)
                    sp.dma_start(x[:, s, :, :], x_view[:, tiles, :]).then_inc(loaded[s], 16)
                    sp.dma_start(y[:, s, :, :, :].rearrange("p t e d -> p t (e d)"), y_view[:, tiles, :]).then_inc(loaded[s], 16)

            @block.scalar
            def _(act):
                for b in range(blocks):
                    s = b % 2
                    act.wait_ge(ready, b + 1)
                    a, full = b * B, (B if b < blocks - 1 else B - 1)
                    act.dma_start(out[a * P:(a + full) * P, :].rearrange("(t p) d -> p t d", p=P), x[:, s, 0:full, :]) \
                       .then_inc(stored[s], 16)
                s = (blocks - 1) % 2
                act.dma_start(out[(NT - 1) * P:N, :], x[0:LAST, s, B - 1, :]).then_inc(stored[s], 16)
                act.wait_ge(stored[s], 16 * ((blocks + 1) // 2) + 16)
                act.wait_ge(stored[1 - s], 16 * (blocks // 2))

            @block.vector
            def _(dve):
                for b in range(blocks):
                    s = b % 2
                    dve.wait_ge(loaded[s], 32 * (b // 2) + 32)
                    for e in range(EXPERTS):
                        for t in range(B):
                            ins = dve.scalar_tensor_tensor(x[:, s, t, :], y[:, s, t, e, :], gate[:, b * B + t, e:e + 1],
                                                           x[:, s, t, :], ALU.mult, ALU.add)
                        if e < EXPERTS - 1:
                            dve.drain()
                    ins.then_inc(ready, 1)

    def gather_nodes(self, g, own=None, agg=None):
        nc = self.nc
        C, S, K = g.cols, g.state, g.per_head
        G = 7
        groups = NT // G
        assert groups * G == NT
        parts = 2 if own is None else 3
        with ExitStack() as here:
            idx = self.sb(here, "idx", [P, 2, 2, G], I32)
            st = self.sb(here, "st", [P, 2, G, 2, S])
            d = self.sb(here, "d", [P, 2, 3, G, H])
            (mstar, ya, yb, den, den2) = self.several(
                here, "node_parts",
                [P, G, H],
                [P, G, C],
                [P, G, C],
                [P, G, H],
                [P, G, H])
            names = ("ready", "begun", "shift_ready", "exp_ready")
            ready, begun, shift_ready, exp_ready = (self.sem(here, n) for n in names)
            got = [self.sem(here, f"got{s}") for s in range(2)]
            block = here.enter_context(nc.Block())

            @block.gpsimd
            def _(pool):
                bound, bound_c = pool.to_reg(P * g.width - 1), pool.to_reg(P - 1)

                def gather(q, i, s):
                    pool.wait_ge(ready, q + 1)
                    pool.sem_inc(begun, 1)
                    for u in range(G):
                        for n, (table, last) in enumerate(((self.state_dram[g.name], bound), (self.carry_dram[g.name], bound_c))):
                            pool.indirect_dma_start(out=st[:, s, u, n, :], out_offset=None, in_=table[:, :],
                                                    in_offset=bass.IndirectOffsetOnAxis(ap=idx[:, s, n, u:u + 1], axis=0),
                                                    bounds_check=last, oob_is_err=False).then_inc(got[s], 16)
                in_pairs(pool, groups, gather)

            @block.scalar
            def _(act):
                def step(q, i, s):
                    act.wait_ge(shift_ready, q + 1)
                    flat = d[:, s, 0:parts, :, :].rearrange("p a g h -> p (a g h)")
                    act.activation(flat, flat, ACT.Exp).then_inc(exp_ready, 1)
                in_pairs(act, groups, step)

            @block.vector
            def _(dve):
                def prefill(q, s):
                    dve.memset(st[:, s, :, :, 0:C + H], 0.0)
                    dve.memset(st[:, s, :, :, C + H:S], NEG)
                    dve.tensor_copy(idx[:, s, 0, :], self.end_at[g.name][:, bass.ds(q * G, G)])
                    dve.tensor_copy(idx[:, s, 1, :], self.carry_at[g.name][:, bass.ds(q * G, G)]).then_inc(ready, 1)
                prefill(0, 0)
                prefill(1, 1)

                def by_head(ap):
                    return ap.rearrange("p g (h k) -> p g h k", k=K)

                def over_head(ap):
                    return ap.unsqueeze(3).to_broadcast([P, G, H, K])

                def step(q, i, s):
                    at = bass.ds(q * G, G)
                    dve.drain()
                    dve.wait_ge(got[s], (i + 1) * (32 * G))
                    m0, m1 = st[:, s, :, 0, C + H:S], st[:, s, :, 1, C + H:S]
                    dve.tensor_tensor(mstar[:, :, :], m0, m1, ALU.max)
                    dve.drain()
                    if own is not None:
                        own_m = own[1][:, at, :]
                        dve.tensor_tensor(mstar[:, :, :], mstar[:, :, :], own_m, ALU.max)
                        dve.drain()
                        dve.tensor_tensor(d[:, s, 2, :, :], own_m, mstar[:, :, :], ALU.subtract)
                    dve.tensor_tensor(d[:, s, 0, :, :], m0, mstar[:, :, :], ALU.subtract)
                    dve.tensor_tensor(d[:, s, 1, :, :], m1, mstar[:, :, :], ALU.subtract)
                    dve.drain()
                    dve.sem_inc(shift_ready, 1)
                    dve.wait_ge(exp_ready, q + 1)
                    dve.tensor_tensor(by_head(ya[:, :, :]), by_head(st[:, s, :, 0, 0:C]), over_head(d[:, s, 0, :, :]), ALU.mult)
                    dve.tensor_tensor(by_head(yb[:, :, :]), by_head(st[:, s, :, 1, 0:C]), over_head(d[:, s, 1, :, :]), ALU.mult)
                    dve.tensor_tensor(den[:, :, :], st[:, s, :, 0, C:C + H], d[:, s, 0, :, :], ALU.mult)
                    dve.tensor_tensor(den2[:, :, :], st[:, s, :, 1, C:C + H], d[:, s, 1, :, :], ALU.mult)
                    dve.drain()
                    if not (isinstance(q, int) and q >= groups - 2):
                        prefill(q + 2, s)
                    dve.tensor_tensor(ya[:, :, :], ya[:, :, :], yb[:, :, :], ALU.add)
                    dve.tensor_tensor(den[:, :, :], den[:, :, :], den2[:, :, :], ALU.add)
                    dve.drain()
                    if own is not None:
                        dve.tensor_tensor(by_head(yb[:, :, :]), by_head(own[0][:, at, :]), over_head(d[:, s, 2, :, :]), ALU.mult)
                        dve.tensor_tensor(den[:, :, :], den[:, :, :], d[:, s, 2, :, :], ALU.add)
                        dve.drain()
                        dve.tensor_tensor(ya[:, :, :], ya[:, :, :], yb[:, :, :], ALU.add)
                        dve.tensor_scalar(den[:, :, :], den[:, :, :], 1e-16, None, ALU.add)
                    else:
                        dve.tensor_scalar(den[:, :, :], den[:, :, :], 1e-16, None, ALU.max)
                    dve.drain()
                    dve.reciprocal(den[:, :, :], den[:, :, :])
                    dve.drain()
                    if own is None:
                        dve.tensor_tensor(by_head(ya[:, :, :]), by_head(ya[:, :, :]), over_head(den[:, :, :]), ALU.mult)
                        dve.drain()
                        dve.tensor_tensor(self.X[:, at, :], self.X[:, at, :], ya[:, :, :], ALU.add)
                    else:
                        dve.tensor_tensor(by_head(agg[:, at, :]), by_head(ya[:, :, :]), over_head(den[:, :, :]), ALU.mult)
                in_pairs(dve, groups, step)

    def project_ffn(self, own_h, own_m, xt_all):
        nc, io = self.nc, self.io
        C = FFN.cols
        ident = self.ident
        with ExitStack() as here:
            mean, rstd = self.norm_stats(here)
            att = self.sb(here, "att", [C, 2 * H])
            w = self.sb(here, "w_ffn", [P, 2, C + 2 * H])
            wt = self.sb(here, "w_turned_sb", [C, 2, P])
            (xn, xt, rows, own) = self.several(
                here, "row_parts",
                [P, 2, D],
                [P, 2, 2, P],
                [P, 2, C + 2 * H],
                [P, NT, H])
            tp, pz, pw = self.ps(here, "tp", [P, 2, 512]), self.ps(here, "pz", [P, 2, 512]), self.ps(here, "pw", [P, 512])
            names = ("att_clear", "w_loaded", "w_turned", "wt_ready", "w_made", "w_ready", "xn_ready", "turned", "xt_ready",
                     "projected", "evac")
            (att_clear, w_loaded, w_turned, wt_ready, w_made, w_ready, xn_ready, turned, xt_ready, projected, evac) = \
                (self.sem(here, n) for n in names)
            stored = [self.sem(here, f"stored{s}") for s in range(2)]
            block = here.enter_context(nc.Block())

            @block.sync
            def _(sp):
                sp.dma_start(w[:, :, 0:C], io["L0_ffn_W_gat"].rearrange("(k p) c -> p k c", p=P)).then_inc(w_loaded, 16)
                sp.wait_ge(att_clear, 1)
                for side, name in enumerate(("L0_ffn_att_src", "L0_ffn_att_dst")):
                    for h in range(H):
                        sp.dma_start(att[h * EXPERTS:(h + 1) * EXPERTS, side * H + h:side * H + h + 1],
                                     io[name][h, :].rearrange("(e a) -> e a", a=1)).then_inc(w_loaded, 16)
                sp.wait_ge(w_loaded, 144)

                def store(t, i, s):
                    sp.wait_ge(evac, t + 1)
                    sp.dma_start(self.row_dram["ffn"][bass.ds(t * P, P), :], rows[:, s, 0:FFN.row]).then_inc(stored[s], 16)
                in_pairs(sp, NT, store)
                for s in range(2):
                    sp.wait_ge(stored[s], 16 * ((NT + 1 - s) // 2))

            @block.tensor
            def _(pe):
                pe.wait_ge(w_loaded, 144)
                for k in range(2):
                    mm = pe.transpose(tp[0:C, k, 0:P], w[:, k, 0:C], ident[:, :])
                mm.then_inc(w_turned, 1)
                pe.wait_ge(wt_ready, 1)
                for k in range(2):
                    mm = pe.matmul(pw[:, k * 2 * H:(k + 1) * 2 * H], wt[:, k, :], att[:, :], start=True, stop=True)
                mm.then_inc(w_made, 1)
                pe.wait_ge(w_ready, 1)

                def turn(t, i, s):
                    pe.wait_ge(xn_ready, t + 1)
                    if not first(i):
                        pe.wait_ge(xt_ready, t - 1)
                    for k in range(2):
                        mm = pe.transpose(tp[:, s, k * P:(k + 1) * P], xn[:, s, k * P:(k + 1) * P], ident[:, :])
                    mm.then_inc(turned, 1)

                def products(t, i, s):
                    pe.wait_ge(xt_ready, t + 1)
                    if not first(i):
                        pe.wait_ge(evac, t - 1)
                    for k in range(2):
                        mm = pe.matmul(pz[:, s, 0:C + 2 * H], xt[:, s, k, :], w[:, k, :], start=(k == 0), stop=(k == 1))
                    mm.then_inc(projected, 1)
                in_two_stages(pe, NT, turn, products)

            @block.scalar
            def _(act):
                act.wait_ge(w_turned, 1)
                for k in range(2):
                    ins = act.activation(wt[:, k, :], tp[0:C, k, 0:P], ACT.Copy)
                ins.then_inc(wt_ready, 1)
                act.wait_ge(w_made, 1)
                for k in range(2):
                    ins = act.activation(w[:, k, C:C + 2 * H], pw[:, k * 2 * H:(k + 1) * 2 * H], ACT.Copy)
                ins.then_inc(w_ready, 1)

                def copy_turned(t, i, s):
                    act.wait_ge(turned, t + 1)
                    if not first(i):
                        act.wait_ge(projected, t - 1)
                    act.activation(xt_all[:, :, bass.ds(t * P, P)], tp[:, s, 0:D].rearrange("p (k n) -> p k n", k=2), ACT.Copy)
                    act.activation(xt[:, s, :, :].rearrange("p k n -> p (k n)"), tp[:, s, 0:D], ACT.Copy).then_inc(xt_ready, 1)

                def copy_products(t, i, s):
                    act.wait_ge(projected, t + 1)
                    if not first(i):
                        act.wait_ge(stored[s], i * 16)
                    act.activation(rows[:, s, :], pz[:, s, 0:C + 2 * H], ACT.Copy)
                    flat = "p a h -> p (a h)"
                    act.activation(own_h[:, bass.ds(t, 1), :].rearrange(flat), pz[:, s, 0:C], ACT.Copy)
                    act.activation(own[:, bass.ds(t, 1), :].rearrange(flat), pz[:, s, C:C + H], ACT.Copy)
                    act.activation(self.ed["ffn"][:, bass.ds(t, 1), :].rearrange(flat), pz[:, s, C + H:C + 2 * H], ACT.Copy) \
                       .then_inc(evac, 1)
                in_two_stages(act, NT, copy_turned, copy_products)

            @block.vector
            def _(dve):
                dve.memset(att[:, :], 0.0).then_inc(att_clear, 1)

                def step(t, i, s):
                    if not first(i):
                        dve.wait_ge(turned, t - 1)
                    dve.tensor_scalar(xn[:, s, :], self.X[:, bass.ds(t, 1), :].rearrange("p a d -> p (a d)"),
                                      mean[:, bass.ds(t, 1)], rstd[:, bass.ds(t, 1)], ALU.subtract, ALU.mult) \
                       .then_inc(xn_ready, 1)
                in_pairs(dve, NT, step)
                dve.wait_ge(evac, NT)
                dve.tensor_tensor(own[:, :, :], own[:, :, :], self.ed["ffn"][:, :, :], ALU.add)
                dve.drain()
                dve.scalar_tensor_tensor(own_m[:, :, :], own[:, :, :], FFN.slope, own[:, :, :], ALU.mult, ALU.max)

    def route(self, agg, gate):
        nc, io = self.nc, self.io
        C = FFN.cols
        with ExitStack() as here:
            (par, y, sq, mean, var, std, eps, sc, rank, cmp, tops, is_top, ex, ws) = self.several(
                here, "route_parts",
                [P, 3, C],
                [P, NT, C],
                [P, NT, C],
                [P, NT],
                [P, NT],
                [P, NT],
                [P, 1],
                [P, NT, EXPERTS],
                [P, NT, EXPERTS],
                [P, NT, EXPERTS],
                [P, 2, NT],
                [P, 2, NT, EXPERTS],
                [P, NT],
                [P, 2, NT])
            par_in, var_ready, std_ready, diff_ready, ex_ready = \
                (self.sem(here, n) for n in ("par_in", "var_ready", "std_ready", "diff_ready", "ex_ready"))
            block = here.enter_context(nc.Block())

            @block.sync
            def _(sp):
                for n, name in enumerate(("L0_ffn_b_gat", "L0_ffn_ln_gamma", "L0_ffn_ln_beta")):
                    sp.dma_start(par[:, n, :], io[name].partition_broadcast(P)).then_inc(par_in, 16)

            @block.scalar
            def _(act):
                act.wait_ge(var_ready, 1)
                act.activation(std[:, :], var[:, :], ACT.Sqrt, bias=eps[:, 0:1], scale=1.0 / C).then_inc(std_ready, 1)
                act.wait_ge(diff_ready, 1)
                act.activation(ex[:, :], ex[:, :], ACT.Exp).then_inc(ex_ready, 1)

            @block.vector
            def _(dve):
                def op(call, *args):
                    call(*args)
                    dve.drain()

                def over_nodes(ap):
                    return ap.unsqueeze(1).to_broadcast([P, NT, C])

                def over(ap, n):
                    return ap.unsqueeze(2).to_broadcast([P, NT, n])
                dve.memset(eps[:, :], EPS)
                dve.wait_ge(par_in, 48)
                op(dve.tensor_tensor, y[:, :, :], agg[:, 0:NT, :], over_nodes(par[:, 0, :]), ALU.add)
                op(dve.tensor_reduce, mean[:, :], y[:, :, :], AX, ALU.add)
                op(dve.tensor_scalar, mean[:, :], mean[:, :], 1.0 / C, None, ALU.mult)
                op(dve.tensor_tensor, y[:, :, :], y[:, :, :], over(mean[:, :], C), ALU.subtract)
                op(dve.tensor_tensor, sq[:, :, :], y[:, :, :], y[:, :, :], ALU.mult)
                dve.tensor_reduce(var[:, :], sq[:, :, :], AX, ALU.add).then_inc(var_ready, 1)
                dve.wait_ge(std_ready, 1)
                op(dve.reciprocal, std[:, :], std[:, :])
                op(dve.tensor_tensor, y[:, :, :], y[:, :, :], over(std[:, :], C), ALU.mult)
                op(dve.tensor_tensor, y[:, :, :], y[:, :, :], over_nodes(par[:, 1, :]), ALU.mult)
                op(dve.tensor_tensor, y[:, :, :], y[:, :, :], over_nodes(par[:, 2, :]), ALU.add)
                op(dve.tensor_tensor, sc[:, :, :], y[:, :, 0:EXPERTS], y[:, :, EXPERTS:2 * EXPERTS], ALU.add)
                for h in range(2, H):
                    op(dve.tensor_tensor, sc[:, :, :], sc[:, :, :], y[:, :, h * EXPERTS:(h + 1) * EXPERTS], ALU.add)
                op(dve.tensor_scalar, sc[:, :, :], sc[:, :, :], 1.0 / H, None, ALU.mult)
                op(dve.memset, rank[:, :, :], 0.0)
                for a in range(EXPERTS):
                    for lo, hi, rel in ((0, a, ALU.is_gt), (a + 1, EXPERTS, ALU.is_ge)):
                        if lo < hi:
                            op(dve.tensor_tensor, cmp[:, :, lo:hi], over(sc[:, :, a], hi - lo), sc[:, :, lo:hi], rel)
                            op(dve.tensor_tensor, rank[:, :, lo:hi], rank[:, :, lo:hi], cmp[:, :, lo:hi], ALU.add)
                for k in range(2):
                    op(dve.tensor_scalar, is_top[:, k, :, :], rank[:, :, :], float(k), None, ALU.is_equal)
                    op(dve.tensor_tensor, cmp[:, :, :], is_top[:, k, :, :], sc[:, :, :], ALU.mult)
                    op(dve.tensor_reduce, tops[:, k, :], cmp[:, :, :], AX, ALU.add)
                dve.tensor_tensor(ex[:, :], tops[:, 1, :], tops[:, 0, :], ALU.subtract).then_inc(diff_ready, 1)
                dve.wait_ge(ex_ready, 1)
                op(dve.tensor_scalar, ws[:, 0, :], ex[:, :], 1.0, None, ALU.add)
                op(dve.reciprocal, ws[:, 0, :], ws[:, 0, :])
                op(dve.tensor_tensor, ws[:, 1, :], ws[:, 0, :], ex[:, :], ALU.mult)
                op(dve.tensor_tensor, gate[:, :, :], is_top[:, 0, :, :], over(ws[:, 0, :], EXPERTS), ALU.mult)
                op(dve.tensor_tensor, cmp[:, :, :], is_top[:, 1, :, :], over(ws[:, 1, :], EXPERTS), ALU.mult)
                op(dve.tensor_tensor, gate[:, :, :], gate[:, :, :], cmp[:, :, :], ALU.add)

    def store_x(self):
        nc = self.nc
        with ExitStack() as here:
            stored = self.sem(here, "stored")
            block = here.enter_context(nc.Block())

            @block.sync
            def _(sp):
                sp.dma_start(self.x1_dram.rearrange("(t p) d -> p t d", p=P), self.X[:, :, :]).then_inc(stored, 16)
                sp.wait_ge(stored, 16)

    def run(self, out):
        def begin(part):
            self.part = part
        with self.keep:
            begin("setup")
            self.setup()
            self.x1_dram, self.y_dram = self.dram("x1", [NPAD, D]), self.dram("y", [NPAD, EXPERTS, D])
            with ExitStack() as with_x:
                self.load_x(with_x)
                begin("project")
                self.project()
            begin("segments_gnn")
            self.segments(GNN)
            begin("count_ffn")
            self.count_ffn()
            begin("segments_ffn")
            self.segments(FFN)
            with ExitStack() as mine:
                begin("sort")
                self.sort_columns(mine)
                begin("starts_gnn")
                self.starts(GNN, mine)
                fin, finm = self.several(mine, "last_states", [P, GNN.cols + H], [P, H])
                begin("iotas")
                self.gnn_and_sort(fin, finm)
                begin("carry_gnn")
                self.carry(GNN, fin, finm)
            with ExitStack() as later:
                own_h, own_m, agg, gate = self.several(
                    later, "by_node",
                    [P, NT, FFN.cols],
                    [P, NT, H],
                    [P, NT, FFN.cols],
                    [P, NT, EXPERTS])
                begin("ffn")
                xt_all = self.sb(later, "xt_all", [P, 2, NPAD])
                with ExitStack() as with_x:
                    begin("x_again")
                    self.load_x(with_x)
                    begin("mix")
                    self.mix(xt_all)
                    begin("nodes_gnn")
                    self.gather_nodes(GNN)
                    begin("project_ffn")
                    self.project_ffn(own_h, own_m, xt_all)
                    begin("x_stored")
                    self.store_x()
                with ExitStack() as mine:
                    begin("starts_ffn")
                    self.starts(FFN, mine)
                    fin, finm = self.several(mine, "last_states", [P, FFN.cols + H], [P, H])
                    begin("stage2")
                    self.ffn_and_experts(fin, finm, xt_all)
                    begin("carry_ffn")
                    self.carry(FFN, fin, finm)
                begin("nodes_ffn")
                self.gather_nodes(FFN, (own_h, own_m), agg)
                begin("route")
                self.route(agg, gate)
                begin("combine")
                self.combine(gate, out)


_INS = ['x', 'src', 'dst', 'L0_gnn_W', 'L0_gnn_att', 'L0_mix_Wqkv', 'L0_mix_Wout', 'L0_mix_gamma', 'L0_ffn_W_gat',
        'L0_ffn_att_src', 'L0_ffn_att_dst', 'L0_ffn_b_gat', 'L0_ffn_ln_gamma', 'L0_ffn_ln_beta', 'L0_ffn_W1',
        'L0_ffn_b1', 'L0_ffn_W2', 'L0_ffn_b2', 'L0_ffn_edge_index']


def kernel(**inputs):
    import numpy as _np
    import concourse.bacc as _bacc
    from concourse import mybir as _mybir
    from concourse.bass_utils import run_bass_kernel_spmd as _run

    nc = _bacc.Bacc("TRN2", target_bir_lowering=False, num_devices=1)
    arrays, io = {}, {}
    for name in _INS:
        a = _np.ascontiguousarray(inputs[name])
        arrays[f"in_{name}_dram"] = a
        io[name] = nc.dram_tensor(f"in_{name}_dram", a.shape, _mybir.dt.from_np(a.dtype), kind="ExternalInput").ap()
    out = nc.dram_tensor("out_0_dram", (N, D), _mybir.dt.float32, kind="ExternalOutput").ap()
    Kernel(nc, io).run(out)
    r = _run(nc, [arrays], core_ids=[0])
    return r.results[0]["out_0_dram"]
```
